# Optimizing a Trainium2 kernel written in Bass

```python
import numpy as np
import jax
import jax.numpy as jnp

def _softmax(x, axis=-1):
    return jax.nn.softmax(x, axis=axis)

def _gelu(x):
    return jax.nn.gelu(x, approximate=True)

def _silu(x):
    return jax.nn.silu(x)

def _sigmoid(x):
    return jax.nn.sigmoid(x)

def _layernorm(x, axis=-1, eps=1e-05):
    m = jnp.mean(x, axis=axis, keepdims=True)
    v = jnp.var(x, axis=axis, keepdims=True)
    return (x - m) / jnp.sqrt(v + eps)

def _scatter_add(tgt, idx, src, axis=0):
    return tgt.at[idx].add(src)

def _segment_sum(src, seg, n):
    return jax.ops.segment_sum(src, seg, n)
kernel_name = 'mk_gnn_preln_d4_gnn_r8_df303c'

def setup_inputs(seed: int=0):
    np.random.seed(seed)
    _w = jnp.asarray

    def _rec_inputs():
        import jax
        import jax.numpy as jnp
        _gk = jax.random.key(seed)
        x = -0.0001006 + 1 * jax.random.normal(jax.random.fold_in(_gk, 1), (12500, 48), jnp.float32)
        src = jax.random.randint(jax.random.fold_in(_gk, 2), (200000,), 0, 12500, jnp.int32)
        dst = jnp.minimum((12500 * jax.random.uniform(jax.random.fold_in(_gk, 3), (200000,)) ** 2.0).astype(jnp.int32), 99999)
        _o = jnp.argsort(dst, stable=True)
        src = src[_o]
        dst = dst[_o]
        edge_attr_40 = jax.random.uniform(jax.random.fold_in(_gk, 13), (200000, 40), jnp.float32, 0.0, 1)
        edge_attr_48 = -4.21973e-05 + 0.999841 * jax.random.normal(jax.random.fold_in(_gk, 14), (200000, 48), jnp.float32)
        edge_type_8 = jax.random.randint(jax.random.fold_in(_gk, 16), (200000,), 0, 8, jnp.int32)
        edge_weight = jax.random.uniform(jax.random.fold_in(_gk, 17), (200000,), jnp.float32, 0.0, 6.99999)
        edge_weight1 = jax.random.uniform(jax.random.fold_in(_gk, 18), (200000, 1), jnp.float32, 0.0, 1)
        node_type_119 = jax.random.randint(jax.random.fold_in(_gk, 19), (12500,), 0, 119, jnp.int32)
        node_vec = jax.random.uniform(jax.random.fold_in(_gk, 20), (12500,), jnp.float32, 0.0, 1.49999)
        return (x, src, dst, edge_attr_40, edge_attr_48, edge_type_8, edge_weight, edge_weight1, node_type_119, node_vec)
    x, src, dst, edge_attr_40, edge_attr_48, edge_type_8, edge_weight, edge_weight1, node_type_119, node_vec = _rec_inputs()

    def _L0_gnn_setup():
        import jax, jax.numpy as jnp
        import numpy as np
        N_NODES = 12500
        N_EDGES = 200000
        D_FEAT = 48
        key = jax.random.key(seed)
        k1, k2, k3, k4 = jax.random.split(key, 4)
        node_feat = jax.random.normal(k1, (N_NODES, D_FEAT), dtype=jnp.float32)
        edge_feat = jax.random.normal(k2, (N_EDGES, D_FEAT), dtype=jnp.float32)
        src = jax.random.randint(k3, (N_EDGES,), 0, N_NODES, dtype=jnp.int32)
        dst = jax.random.randint(k4, (N_EDGES,), 0, N_NODES, dtype=jnp.int32)
        eps = jnp.zeros((1,), dtype=jnp.float32)
        return {'node_feat': node_feat, 'edge_feat': edge_feat, 'src': src, 'dst': dst, 'eps': eps}
    _L0_gnn_all = _L0_gnn_setup()
    _L0_gnn_in = {k: v for k, v in _L0_gnn_all.items() if k in ('eps',)}
    del _L0_gnn_all

    def _L1_gnn_setup():
        import jax, jax.numpy as jnp
        import numpy as np
        N_NODES = 6250
        N_EDGES = 200000
        IN_FEAT = 48
        OUT_FEAT = 48
        NUM_RELS = 8
        key = jax.random.key(seed)
        ks = jax.random.split(key, 9)
        s1 = float(np.sqrt(2.0) * np.sqrt(6.0 / (IN_FEAT + IN_FEAT)))
        s2 = float(np.sqrt(2.0) * np.sqrt(6.0 / (IN_FEAT + OUT_FEAT)))
        return {'inputs': jax.random.normal(ks[0], (N_NODES, IN_FEAT), dtype=jnp.float32), 'norm': jax.random.uniform(ks[1], (N_EDGES, 1), dtype=jnp.float32), 'weight1': jax.random.uniform(ks[2], (NUM_RELS, IN_FEAT, IN_FEAT), jnp.float32, -s1, s1), 'weight2': jax.random.uniform(ks[3], (NUM_RELS, IN_FEAT, OUT_FEAT), jnp.float32, -s2, s2), 'bias1': jax.random.normal(ks[4], (IN_FEAT,), dtype=jnp.float32) * 0.1, 'bias2': jax.random.normal(ks[5], (OUT_FEAT,), dtype=jnp.float32) * 0.1, 'src': jax.random.randint(ks[6], (N_EDGES,), 0, N_NODES, dtype=jnp.int64) if jax.config.jax_enable_x64 else jax.random.randint(ks[6], (N_EDGES,), 0, N_NODES).astype(jnp.int32), 'dst': jax.random.randint(ks[7], (N_EDGES,), 0, N_NODES).astype(jnp.int32), 'rel_type': jax.random.randint(ks[8], (N_EDGES,), 0, NUM_RELS).astype(jnp.int32)}
    _L1_gnn_all = _L1_gnn_setup()
    _L1_gnn_in = {k: v for k, v in _L1_gnn_all.items() if k in ('weight1', 'weight2', 'bias1', 'bias2')}
    del _L1_gnn_all

    def _L2_gnn_setup():
        import jax, jax.numpy as jnp
        import numpy as np
        N_NODES = 6250
        N_EDGES = 200000
        D_IN = 48
        D_OUT = 48
        K = 4
        key = jax.random.key(seed)
        k1, k2, k3, k4, k5 = jax.random.split(key, 5)
        x = jax.random.normal(k1, (N_NODES, D_IN), dtype=jnp.float32)
        edge_index = jax.random.randint(k2, (2, N_EDGES), 0, N_NODES, dtype=jnp.int64)
        weight = jax.random.normal(k3, (K, D_IN, D_OUT), dtype=jnp.float32) * (1.0 / np.sqrt(D_IN))
        bias = jax.random.normal(k4, (D_OUT,), dtype=jnp.float32) * 0.01
        return {'x': x, 'edge_index': edge_index, 'weight': weight, 'bias': bias}
    _L2_gnn_all = _L2_gnn_setup()
    _L2_gnn_in = {k: v for k, v in _L2_gnn_all.items() if k in ('weight', 'bias')}
    del _L2_gnn_all

    def _L3_gnn_setup():
        import jax, jax.numpy as jnp
        import numpy as np
        CUTOFF = 6.0
        LN_EPS = 1e-05
        key = jax.random.key(seed)
        ks = jax.random.split(key, 16)
        N, E, H, R, NEL, G = (6250, 100000, 48, 40, 119, 32)
        inp = {'h': jax.random.normal(ks[0], (N, H), jnp.float32), 'edge_index': jax.random.randint(ks[1], (2, E), 0, N, jnp.int64), 'edge_attr': jax.random.uniform(ks[2], (E, R), jnp.float32), 'distances': jax.random.uniform(ks[3], (E,), jnp.float32) * 7.0, 'atom_z': jax.random.randint(ks[4], (N,), 0, NEL, jnp.int64), 'node_mult': jax.random.uniform(ks[5], (N,), jnp.float32) + 0.5, 'batch': jnp.zeros((N,), jnp.int64), 'W1': jax.random.normal(ks[6], (H, R), jnp.float32) / np.sqrt(R), 'b1': jax.random.normal(ks[7], (H,), jnp.float32) * 0.01, 'W2': jax.random.normal(ks[8], (H, H), jnp.float32) / np.sqrt(H), 'b2': jax.random.normal(ks[9], (H,), jnp.float32) * 0.01, 'emb': jax.random.normal(ks[10], (NEL, G), jnp.float32) * 0.01, 'adaptW': jax.random.normal(ks[11], (G, G), jnp.float32) * 0.01, 'gamma': jnp.ones((H,), jnp.float32), 'beta': jnp.zeros((H,), jnp.float32)}
        return inp
    _L3_gnn_all = _L3_gnn_setup()
    _L3_gnn_in = {k: v for k, v in _L3_gnn_all.items() if k in ('W1', 'b1', 'W2', 'b2', 'emb', 'adaptW', 'gamma', 'beta')}
    del _L3_gnn_all
    return {'x': x, 'src': src, 'dst': dst, 'edge_attr_40': edge_attr_40, 'edge_attr_48': edge_attr_48, 'edge_type_8': edge_type_8, 'edge_weight': edge_weight, 'edge_weight1': edge_weight1, 'node_type_119': node_type_119, 'node_vec': node_vec, 'L0_gnn_eps': _L0_gnn_in['eps'], 'L1_gnn_weight1': _L1_gnn_in['weight1'], 'L1_gnn_weight2': _L1_gnn_in['weight2'], 'L1_gnn_bias1': _L1_gnn_in['bias1'], 'L1_gnn_bias2': _L1_gnn_in['bias2'], 'L2_gnn_weight': _L2_gnn_in['weight'], 'L2_gnn_bias': _L2_gnn_in['bias'], 'L3_gnn_W1': _L3_gnn_in['W1'], 'L3_gnn_b1': _L3_gnn_in['b1'], 'L3_gnn_W2': _L3_gnn_in['W2'], 'L3_gnn_b2': _L3_gnn_in['b2'], 'L3_gnn_emb': _L3_gnn_in['emb'], 'L3_gnn_adaptW': _L3_gnn_in['adaptW'], 'L3_gnn_gamma': _L3_gnn_in['gamma'], 'L3_gnn_beta': _L3_gnn_in['beta']}

def reference(x, src, dst, edge_attr_40, edge_attr_48, edge_type_8, edge_weight, edge_weight1, node_type_119, node_vec, L0_gnn_eps, L1_gnn_weight1, L1_gnn_weight2, L1_gnn_bias1, L1_gnn_bias2, L2_gnn_weight, L2_gnn_bias, L3_gnn_W1, L3_gnn_b1, L3_gnn_W2, L3_gnn_b2, L3_gnn_emb, L3_gnn_adaptW, L3_gnn_gamma, L3_gnn_beta):
    import jax
    import jax.numpy as jnp

    def _L0_gnn_ref(node_feat, edge_feat, src, dst, eps):
        import jax, jax.numpy as jnp
        import numpy as np
        N_NODES = 12500
        N_EDGES = 200000
        D_FEAT = 48
        m = jax.nn.relu(node_feat[src] + edge_feat)
        neigh = jax.ops.segment_sum(m, dst, num_segments=N_NODES)
        return (1.0 + eps[0]) * node_feat + neigh

    def _L1_gnn_ref(inputs, norm, weight1, weight2, bias1, bias2, src, dst, rel_type):
        import jax, jax.numpy as jnp
        import numpy as np
        N_NODES = 6250
        N_EDGES = 200000
        IN_FEAT = 48
        OUT_FEAT = 48
        NUM_RELS = 8
        h1 = jax.nn.relu(jnp.einsum('ni,rij->nrj', inputs, weight1) + bias1)
        h2 = jnp.einsum('nrj,rjo->nro', h1, weight2)
        msg = h2[src, rel_type] * norm
        agg = jax.ops.segment_sum(msg, dst, num_segments=inputs.shape[0])
        return jax.nn.relu(agg + bias2)

    def _L2_gnn_ref(x, edge_index, weight, bias):
        import jax, jax.numpy as jnp
        import numpy as np
        N_NODES = 6250
        N_EDGES = 200000
        D_IN = 48
        D_OUT = 48
        K = 4
        'PyG ChebConv forward with sym normalization, lambda_max=2.0.\n\n            L_hat = 2L/lambda_max - I. With lambda_max=2 and sym Laplacian, the\n            diagonal becomes 0 and off-diagonal weights are -d_i^{-1/2} d_j^{-1/2}.\n            T0 = x, T1 = L_hat x, Tk = 2 L_hat T_{k-1} - T_{k-2};  out = sum_k Tk W_k + b.\n            '
        n = x.shape[0]
        row, col = (edge_index[0], edge_index[1])
        ew = (row != col).astype(x.dtype)
        deg = jax.ops.segment_sum(ew, row, num_segments=n)
        dis = jnp.where(deg > 0, jax.lax.rsqrt(deg), 0.0)
        w = -dis[row] * ew * dis[col]

        def prop(h):
            return jax.ops.segment_sum(w[:, None] * h[row], col, num_segments=n)
        tx0 = x
        out = tx0 @ weight[0]
        tx1 = prop(x)
        out = out + tx1 @ weight[1]
        for k in range(2, weight.shape[0]):
            tx2 = 2.0 * prop(tx1) - tx0
            out = out + tx2 @ weight[k]
            tx0, tx1 = (tx1, tx2)
        return out + bias

    def _L3_gnn_ref(h, edge_index, edge_attr, distances, atom_z, node_mult, batch, W1, b1, W2, b2, emb, adaptW, gamma, beta):
        import jax, jax.numpy as jnp
        import numpy as np
        CUTOFF = 6.0
        LN_EPS = 1e-05
        src, dst = (edge_index[0], edge_index[1])
        N = h.shape[0]
        gate = jax.nn.silu(edge_attr @ W1.T + b1) @ W2.T + b2
        ei = emb[atom_z[src]]
        ej = emb[atom_z[dst]]
        adapt_logit = jnp.sum(ei * (ej @ adaptW.T), axis=-1, keepdims=True)
        gate = gate + adapt_logit
        cw = jnp.where(distances < CUTOFF, 0.5 * (jnp.cos(jnp.pi * distances / CUTOFF) + 1.0), 0.0)
        mj = node_mult[dst]
        msg = gate * h[dst] * (cw * mj)[:, None]
        agg = jax.ops.segment_sum(msg, src, num_segments=N)
        tot = jax.ops.segment_sum(mj, src, num_segments=N)
        agg = agg / jnp.clip(tot, 1e-08, None)[:, None]
        x = h + agg
        mu = jnp.mean(x, axis=-1, keepdims=True)
        var = jnp.mean(jnp.square(x - mu), axis=-1, keepdims=True)
        return (x - mu) / jnp.sqrt(var + LN_EPS) * gamma + beta
    edge_index = jnp.stack([src, dst])
    batch0 = jnp.zeros((12500,), jnp.int32)
    h = jnp.maximum(_layernorm(x, axis=-1), 0.0)
    x = x + _L0_gnn_ref(h, edge_attr_48, src, dst, L0_gnn_eps)
    h = jnp.maximum(_layernorm(x, axis=-1), 0.0)
    x = x + _L1_gnn_ref(h, edge_weight1, L1_gnn_weight1, L1_gnn_weight2, L1_gnn_bias1, L1_gnn_bias2, src, dst, edge_type_8)
    h = jnp.maximum(_layernorm(x, axis=-1), 0.0)
    x = x + _L2_gnn_ref(h, edge_index, L2_gnn_weight, L2_gnn_bias)
    h = jnp.maximum(_layernorm(x, axis=-1), 0.0)
    x = x + _L3_gnn_ref(h, edge_index, edge_attr_40, edge_weight, node_type_119, node_vec, batch0, L3_gnn_W1, L3_gnn_b1, L3_gnn_W2, L3_gnn_b2, L3_gnn_emb, L3_gnn_adaptW, L3_gnn_gamma, L3_gnn_beta)
    return x

_drawn_inputs = setup_inputs


def setup_inputs(seed=0):
    import zlib

    import numpy as np

    out = dict(_drawn_inputs(seed))
    spreads = {'L3_gnn_gamma': (1.0, 0.6), 'L3_gnn_beta': (0.0, 2.0)}
    factors = {'edge_attr_40': 8.0,
     'edge_weight': 8.0,
     'node_vec': 110.29,
     'L1_gnn_bias1': 3.82,
     'L1_gnn_bias2': 8.0,
     'L2_gnn_bias': 64.0,
     'L3_gnn_W1': 8.0,
     'L3_gnn_b1': 200.0,
     'L3_gnn_W2': 8.0,
     'L3_gnn_b2': 200.0,
     'L3_gnn_emb': 200.0,
     'L3_gnn_adaptW': 200.0}
    for name, (base, spread) in spreads.items():
        noise = np.random.default_rng([zlib.crc32(name.encode()), seed]).standard_normal(out[name].shape)
        drawn = base * np.exp(spread * noise) if base else spread * noise
        out[name] = jnp.asarray(drawn.astype(out[name].dtype))
    for name, factor in factors.items():
        out[name] = (out[name] * factor).astype(out[name].dtype)
    return out
```

```python
import numpy as np
import concourse.bass as bass
from concourse import mybir
from contextlib import ExitStack


def gnn_program(nc, A, out):
    f32, i32, bf16 = mybir.dt.float32, mybir.dt.int32, mybir.dt.bfloat16
    ALU, ACT, AX = mybir.AluOpType, mybir.ActivationFunctionType, mybir.AxisListType

    P = 128
    F = A["x"].shape[2] if len(A["x"].shape) == 3 else 48
    NB = A["x"].shape[1]
    NP = P * NB
    T = A["src"].shape[1]
    NCH = T // 4
    CPS = 8
    HC = 4
    STEPS = NCH // CPS
    GB = 7
    NG = NB // GB
    WIN = 128
    NR = A["w1"].shape[1] // F
    RP = NR // 2
    NZ, ZD = A["emb"].shape
    R = A["ea_t"].shape[1]
    TW = 52
    ROW = F + 1 + NZ
    NT = 8
    MW = F + 1
    CUTOFF = 6.0
    EPS = 1e-5
    CG = A["dst_rows"].shape[0]

    def dram(name, shape, dt=f32):
        return nc.dram_tensor(name, shape, dt, kind="Internal").ap()

    table_l0 = dram("table_l0", [NP, TW])
    table_l1 = dram("table_l1", [NP * NR, F])
    table_l2 = dram("table_l2", [NP, F])
    table_l3 = dram("table_l3", [NP, ROW])
    logit_table = dram("logit_table", [NZ, NZ])
    src_rel = dram("src_rel", [P, T], i32)
    base_row = dram("base_row", [1, NCH])
    base_row_int = dram("base_row_int", [1, NCH], i32)
    span_row = dram("span_row", [1, NCH])
    sums = [dram(f"sum{k}", [NP + P, MW]) for k in range(NT)]

    top = ExitStack()
    with top:
        phase = [0]

        def sb(ctx, name, shape, dt=f32):
            return ctx.enter_context(nc.sbuf_tensor(f"{name}_p{phase[0]}", shape, dt))

        def ps(ctx, name, shape=None, dt=f32):
            return ctx.enter_context(nc.psum_tensor(f"{name}_p{phase[0]}", shape or [P, 512], dt))

        used = []

        def sem(ctx, name):
            s = ctx.enter_context(nc.semaphore(f"{name}_p{phase[0]}"))
            used.append(s)
            return s

        slot_gathered = [top.enter_context(nc.semaphore(f"slot_gathered{c}")) for c in range(8)]
        slot_scattered = [top.enter_context(nc.semaphore(f"slot_scattered{k}")) for k in range(2)]
        gathered_so_far = [0]

        def steps_from_first(eng, count, body):
            body(0, True)
            if count > 1:
                with eng.Fori(1, count) as s:
                    body(s, False)

        def clear_used():
            numbers = list(used)
            used.clear()
            phase[0] += 1

            with nc.Block() as block:
                @block.sync
                def _(sp):
                    for s in numbers:
                        sp.sem_clear(s)

        x_nodes = sb(top, "x_nodes", [P, NB, F])
        h_nodes = sb(top, "h_nodes", [P, NB, F])
        w_nodes = sb(top, "w_nodes", [P, NB, TW])
        src_type = sb(top, "src_type", [P, T])
        src_cols = sb(top, "src_cols", [P, T], i32)
        iota = sb(top, "iota", [P, P])
        part = sb(top, "part", [P, 1])
        ident = sb(top, "ident", [P, P])
        earlier = sb(top, "earlier", [P, P])
        eps_col = sb(top, "eps_col", [P, 1])
        stat = sb(top, "stat", [P, NB])
        stat2 = sb(top, "stat2", [P, NB])

        def layer_norm_relu(relu=True):
            with ExitStack() as ctx:
                step = sem(ctx, "ln_step")
                root = sem(ctx, "ln_root")
                with nc.Block() as block:
                    @block.vector
                    def _(dve):
                        dve.tensor_reduce(stat[:, :], x_nodes[:, :, :], AX.X, ALU.add).then_inc(step, 1)
                        dve.wait_ge(step, 1)
                        dve.tensor_scalar(stat[:, :], stat[:, :], -1.0 / F, None, ALU.mult).then_inc(step, 1)
                        dve.wait_ge(step, 2)
                        dve.tensor_tensor(h_nodes[:, :, :], x_nodes[:, :, :],
                                          stat[:, :].unsqueeze(2).broadcast_to([P, NB, F]), ALU.add).then_inc(step, 1)
                        dve.wait_ge(step, 3)
                        dve.tensor_tensor(w_nodes[:, :, 0:F], h_nodes[:, :, :], h_nodes[:, :, :],
                                          ALU.mult).then_inc(step, 1)
                        dve.wait_ge(step, 4)
                        dve.tensor_reduce(stat2[:, :], w_nodes[:, :, 0:F], AX.X, ALU.add).then_inc(step, 1)
                        dve.wait_ge(root, 1)
                        dve.reciprocal(stat2[:, :], stat2[:, :]).then_inc(step, 1)
                        dve.wait_ge(step, 6)
                        dve.tensor_tensor(h_nodes[:, :, :], h_nodes[:, :, :],
                                          stat2[:, :].unsqueeze(2).broadcast_to([P, NB, F]), ALU.mult).then_inc(step, 1)
                        dve.wait_ge(step, 7)
                        dve.tensor_scalar(h_nodes[:, :, :], h_nodes[:, :, :], 0.0, None, ALU.max).then_inc(step, 1)

                    @block.scalar
                    def _(act):
                        act.wait_ge(step, 5)
                        act.activation(stat2[:, :], stat2[:, :], ACT.Sqrt, bias=eps_col[:, 0:1],
                                       scale=1.0 / F).then_inc(root, 1)
            clear_used()

        agg = ExitStack()
        top.enter_context(agg)
        accT = sb(agg, "accT", [F, NP + WIN])
        dst_cols = sb(agg, "dst_cols", [P, T], i32)
        rel_col = sb(agg, "rel_col", [P, T])
        norm_col = sb(agg, "norm_col", [P, T])
        other_end = sb(agg, "other_end", [P, T])
        base_int = sb(agg, "base_int", [1, NCH], i32)
        span_max = sb(agg, "span_max", [1, 1], i32)
        degree = sb(agg, "degree", [P, NB])
        only_l0 = ExitStack()
        agg.enter_context(only_l0)
        src_hi = sb(only_l0, "src_hi", [P, T])
        src_lo = sb(only_l0, "src_lo", [P, T])

        with ExitStack() as ctx:
            type_int = sb(ctx, "type_int", [P, NB], i32)
            rel_type = sb(ctx, "rel_type", [P, T], i32)
            src_part = sb(ctx, "src_part", [P, T], i32)
            rows = sb(ctx, "rows", [CG, 4, 512], i32)
            base_b = sb(ctx, "base_b", [P, NCH])
            lowest = sb(ctx, "lowest", [CG, 4])
            lowest_int = sb(ctx, "lowest_int", [CG, 4], i32)
            highest = sb(ctx, "highest", [CG, 4])
            span = sb(ctx, "span", [1, NCH])
            loaded = {k: sem(ctx, "ld_" + k) for k in ("x", "src", "dst", "rows", "norm", "rel", "type", "base", "idx")}
            made = sem(ctx, "made")
            step = sem(ctx, "prep_step")
            stored = sem(ctx, "prep_stored")
            with nc.Block() as block:
                @block.gpsimd
                def _(pool):
                    pool.iota(iota[:, :], pattern=[[1, P]], base=0, channel_multiplier=0,
                              allow_small_or_imprecise_dtypes=True).then_inc(made, 1)
                    pool.iota(part[:, :], pattern=[[0, 1]], base=0, channel_multiplier=1,
                              allow_small_or_imprecise_dtypes=True).then_inc(made, 1)
                    pool.memset(eps_col[:, :], EPS).then_inc(made, 1)
                    pool.memset(w_nodes[:, :, :], 0.0).then_inc(made, 1)
                    pool.memset(accT[:, :], 0.0).then_inc(made, 1)

                @block.sync
                def _(sp):
                    sp.dma_start(rows[:, :, :], A["dst_rows"]).then_inc(loaded["rows"], 16)
                    sp.dma_start(x_nodes[:, :, :], A["x"]).then_inc(loaded["x"], 16)
                    sp.dma_start(dst_cols[:, :], A["dst"]).then_inc(loaded["dst"], 16)
                    sp.wait_ge(step, 3)
                    sp.dma_start(base_row.rearrange("a (p q) -> (a p) q", q=4), lowest[:, :]).then_inc(stored, 16)
                    sp.dma_start(base_row_int.rearrange("a (p q) -> (a p) q", q=4), lowest_int[:, :]).then_inc(stored, 16)
                    sp.dma_start(span_row.rearrange("a (p q) -> (a p) q", q=4), highest[:, :]).then_inc(stored, 16)
                    sp.wait_ge(stored, 48)
                    sp.dma_start(base_b[:, :], base_row.broadcast_to([P, NCH])).then_inc(loaded["base"], 16)
                    sp.dma_start(span[:, :], span_row).then_inc(loaded["base"], 16)
                    sp.dma_start(base_int[:, :], base_row_int).then_inc(loaded["base"], 16)
                    sp.wait_ge(step, 8)
                    sp.dma_start(src_rel, rel_type[:, :]).then_inc(loaded["idx"], 16)
                    sp.wait_ge(loaded["idx"], 16)

                @block.scalar
                def _(act):
                    act.dma_start(src_cols[:, :], A["src"]).then_inc(loaded["src"], 16)
                    act.dma_start(rel_type[:, :], A["edge_type"]).then_inc(loaded["rel"], 16)
                    act.dma_start(norm_col[:, :], A["norm"]).then_inc(loaded["norm"], 16)
                    act.dma_start(type_int[:, :], A["node_type"]).then_inc(loaded["type"], 16)
                    act.wait_ge(loaded["norm"], 16)

                @block.vector
                def _(dve):
                    dve.wait_ge(loaded["rows"], 16)
                    dve.tensor_reduce(lowest[:, :], rows[:, :, :], AX.X, ALU.min).then_inc(step, 1)
                    dve.tensor_reduce(highest[:, :], rows[:, :, :], AX.X, ALU.max)
                    dve.wait_ge(step, 1)
                    dve.tensor_copy(lowest_int[:, :], lowest[:, :]).then_inc(step, 1)
                    dve.drain()
                    dve.tensor_tensor(highest[:, :], highest[:, :], lowest[:, :], ALU.subtract).then_inc(step, 1)
                    dve.wait_ge(loaded["src"], 16)
                    dve.wait_ge(loaded["dst"], 16)
                    dve.tensor_tensor(other_end[:, :], src_cols[:, :], dst_cols[:, :], ALU.not_equal).then_inc(step, 1)
                    dve.tensor_single_scalar(src_part[:, :], src_cols[:, :], 7,
                                             op=ALU.logical_shift_right).then_inc(step, 1)
                    dve.wait_ge(step, 5)
                    dve.tensor_copy(src_hi[:, :], src_part[:, :]).then_inc(step, 1)
                    dve.wait_ge(step, 6)
                    dve.tensor_single_scalar(src_part[:, :], src_cols[:, :], P - 1, op=ALU.bitwise_and).then_inc(step, 1)
                    dve.wait_ge(loaded["rel"], 16)
                    dve.scalar_tensor_tensor(out=rel_type[:, :], in0=src_cols[:, :], scalar=float(NR),
                                             in1=rel_type[:, :], op0=ALU.mult, op1=ALU.add).then_inc(step, 1)
                    dve.wait_ge(step, 7)
                    dve.tensor_copy(src_lo[:, :], src_part[:, :]).then_inc(step, 1)
                    dve.wait_ge(loaded["base"], 48)
                    dve.tensor_tensor(rel_col[:, :].rearrange("p (g j) -> p g j", j=4),
                                      dst_cols[:, :].rearrange("p (g j) -> p g j", j=4),
                                      base_b[:, :].unsqueeze(2).broadcast_to([P, NCH, 4]), ALU.subtract).then_inc(step, 1)
                    dve.tensor_reduce(span_max[:, :], span[:, :], AX.X, ALU.max).then_inc(step, 1)
                    dve.wait_ge(made, 5)
                    dve.tensor_scalar(ident[:, :], iota[:, :], part[:, 0:1], None, ALU.is_equal).then_inc(step, 1)
                    dve.tensor_scalar(earlier[:, :], iota[:, :], part[:, 0:1], None, ALU.is_lt).then_inc(step, 1)
                    dve.wait_ge(loaded["type"], 16)
                    dve.tensor_copy(w_nodes[:, :, F], type_int[:, :]).then_inc(step, 1)
                    dve.wait_ge(loaded["x"], 16)
            clear_used()

        ET = mybir.EngineType
        residual = nc.values_load(span_max[0:1, 0:1], engines=[ET.Pool, ET.Activation, ET.PE, ET.DVE, ET.SP],
                                  min_val=0, max_val=NP)

        def store_table(table, width, fill):
            with ExitStack() as ctx:
                step = sem(ctx, "fill_step")
                stored = sem(ctx, "table_stored")
                with nc.Block() as block:
                    steps = []

                    @block.vector
                    def _(dve):
                        steps.append(fill(dve, step))

                    @block.sync
                    def _(sp):
                        sp.wait_ge(step, steps[0])
                        rows_of = table.rearrange("(p b) f -> p b f", b=NB)
                        sp.dma_start(rows_of, w_nodes[:, :, 0:width]).then_inc(stored, 16)
                        sp.wait_ge(stored, 16)
            clear_used()

        def edge_pass(layer, table, width, index_dram, scale_col):
            l0 = layer == 0
            OH, PB = 4, 4
            old = gathered_so_far[0]
            with ExitStack() as ctx:
                index = [sb(ctx, f"index{h}", [P, HC * 4], i32) for h in range(2)]
                gathered = [sb(ctx, f"gathered{c}", [P, 4, width]) for c in range(CPS)]
                onehot = [sb(ctx, f"onehot{k}", [P, 4, WIN]) for k in range(OH)]
                chunk_sum = [ps(ctx, f"chunk_sum{k}") for k in range(PB)]
                index_loaded = [sem(ctx, f"index_loaded{h}") for h in range(2)]
                rows_gathered = slot_gathered
                onehot_ready = sem(ctx, "onehot_ready")
                chunk_started = sem(ctx, "chunk_started")
                sum_ready = sem(ctx, "sum_ready")
                sum_added = sem(ctx, "sum_added")
                if l0:
                    attr = [sb(ctx, f"attr{h}", [P, HC, 4 * F]) for h in range(2)]
                    attr_loaded = [sem(ctx, f"attr_loaded{h}") for h in range(2)]
                    attr_added = sem(ctx, "attr_added")
                    type_kept = sem(ctx, "type_kept")
                    relu_done = sem(ctx, "relu_done")
                    cell_hi = [sb(ctx, f"cell_hi{k}", [P, 4, P], bf16) for k in range(2)]
                    cell_lo = [sb(ctx, f"cell_lo{k}", [P, 4, P], bf16) for k in range(2)]
                    cells_ready = sem(ctx, "cells_ready")
                    cells_counted = sem(ctx, "cells_counted")
                    histogram = ps(ctx, "histogram")
                    counts = sb(ctx, "counts", [P, P])
                    zero_cells = sb(ctx, "zero_cells", [P, P], bf16)
                    zeroed = sem(ctx, "zeroed")
                    count_copied = sem(ctx, "count_copied")
                    degree_dram = dram("degree_dram", [NP])
                    degree_moved = sem(ctx, "degree_moved")
                with nc.Block() as block:
                    @block.sync
                    def _(sp):
                        with sp.Fori(0, STEPS) as s:
                            for h in range(2):
                                sp.wait_ge(sum_ready, s * CPS + HC * (h + 1))
                                sp.dma_start(index[h][:, :], index_dram[:, bass.ds((s * 2 + h) * (HC * 4), HC * 4)]
                                             ).then_inc(index_loaded[h], 16)
                                if l0:
                                    sp.wait_ge(attr_added, s * CPS + HC * (h + 1))
                                    sp.dma_start(attr[h][:, :, :],
                                                 A["attr48"][bass.ds((s * 2 + h) * HC, HC), :, :]
                                                 .rearrange("c p f -> p c f")).then_inc(attr_loaded[h], 16)
                        if l0:
                            sp.wait_ge(count_copied, 1)
                            sp.dma_start(degree_dram.rearrange("(a b) -> a b", b=P), counts[0:NB, :]
                                         ).then_inc(degree_moved, 16)
                            sp.wait_ge(degree_moved, 16)
                            sp.dma_start(degree[:, :], degree_dram.rearrange("(p b) -> p b", b=NB)
                                         ).then_inc(degree_moved, 16)
                            sp.wait_ge(degree_moved, 32)

                    @block.gpsimd
                    def _(pool):
                        if l0:
                            pool.memset(zero_cells[:, :], 0.0).then_inc(zeroed, 1)
                        with pool.Fori(0, STEPS) as s:
                            for c in range(CPS):
                                if c % HC == 0:
                                    pool.wait_ge(index_loaded[c // HC], s * 16 + 16)
                                pool.wait_ge(sum_ready, s * CPS + c + 1)
                                if l0:
                                    pool.wait_ge(type_kept, s * CPS + c + 1)
                                pool.sem_inc(chunk_started, 1)
                                for j in range(4):
                                    t = (c % HC) * 4 + j
                                    pool.indirect_dma_start(
                                        gathered[c][:, j, :], None, table,
                                        bass.IndirectOffsetOnAxis(ap=index[c // HC][:, t:t + 1], axis=0),
                                    ).then_inc(rows_gathered[c], 16)

                    @block.tensor
                    def _(pe):
                        pe.sem_inc(sum_ready, CPS)
                        if l0:
                            pe.sem_inc(cells_counted, 2)
                            pe.wait_ge(zeroed, 1)
                            pe.matmul(histogram[:, 0:P], zero_cells[:, :], zero_cells[:, :], start=True, stop=False)
                        with pe.Fori(0, STEPS) as s:
                            for c in range(CPS):
                                q = s * CPS + c
                                if l0:
                                    pe.wait_ge(cells_ready, q + 1)
                                    for j in range(4):
                                        mm = pe.matmul(histogram[:, 0:P], cell_hi[c % 2][:, j, :],
                                                       cell_lo[c % 2][:, j, :], start=False, stop=False,
                                                       skip_group_check=True)
                                    mm.then_inc(cells_counted, 1)
                                pe.wait_ge(onehot_ready, q + 1)
                                if l0:
                                    pe.wait_ge(relu_done, q + 1)
                                else:
                                    pe.wait_ge(rows_gathered[c], s * 64 + 64 + old)
                                pe.wait_ge(sum_added, q + 1)
                                for j in range(4):
                                    mm = pe.matmul(chunk_sum[c % PB][0:F, 0:WIN], gathered[c][:, j, 0:F],
                                                   onehot[c % OH][:, j, :], start=(j == 0), stop=(j == 3))
                                mm.then_inc(sum_ready, 1)
                        if l0:
                            pe.matmul(histogram[:, 0:P], zero_cells[:, :], zero_cells[:, :], start=False,
                                      stop=True).then_inc(cells_counted, 1)

                    @block.vector
                    def _(dve):
                        dve.sem_inc(sum_added, PB)
                        if l0:
                            dve.sem_inc(attr_added, CPS)

                        def add_sum(s, c):
                            base = dve.value_load(base_int[0:1, bass.ds(s * CPS + c, 1)], min_val=0, max_val=NP)
                            dve.wait_ge(sum_ready, s * CPS + c + 1 + CPS)
                            dve.wait_ge(sum_added, s * CPS + c + PB)
                            dve.tensor_tensor(accT[:, bass.ds(base, WIN)], accT[:, bass.ds(base, WIN)],
                                              chunk_sum[c % PB][0:F, 0:WIN], ALU.add).then_inc(sum_added, 1)

                        def step_of(s):
                            for c in range(CPS):
                                q = s * CPS + c
                                dve.wait_ge(sum_ready, q + 1 + CPS - OH)
                                for j in range(4):
                                    t = q * 4 + j
                                    if scale_col is None:
                                        oh = dve.tensor_scalar(onehot[c % OH][:, j, :], iota[:, :],
                                                               rel_col[:, bass.ds(t, 1)], None, ALU.is_equal)
                                    else:
                                        oh = dve.tensor_scalar(onehot[c % OH][:, j, :], iota[:, :],
                                                               rel_col[:, bass.ds(t, 1)],
                                                               scale_col[:, bass.ds(t, 1)], ALU.is_equal, ALU.mult)
                                oh.then_inc(onehot_ready, 1)
                                if l0:
                                    dve.wait_ge(cells_counted, q + 1)
                                    for j in range(4):
                                        t = q * 4 + j
                                        dve.tensor_scalar(cell_hi[c % 2][:, j, :], iota[:, :],
                                                          src_hi[:, bass.ds(t, 1)], None, ALU.is_equal)
                                        oh = dve.tensor_scalar(cell_lo[c % 2][:, j, :], iota[:, :],
                                                               src_lo[:, bass.ds(t, 1)],
                                                               other_end[:, bass.ds(t, 1)], ALU.is_equal, ALU.mult)
                                    oh.then_inc(cells_ready, 1)
                                    dve.wait_ge(attr_loaded[c // HC], s * 16 + 16)
                                    dve.wait_ge(rows_gathered[c], s * 64 + 64 + old)
                                    dve.wait_ge(type_kept, q + 1)
                                    dve.tensor_tensor(gathered[c][:, :, 0:F], gathered[c][:, :, 0:F],
                                                      attr[c // HC][:, c % HC, :].rearrange("p (j f) -> p j f", f=F),
                                                      ALU.add).then_inc(attr_added, 1)
                                if c >= 1:
                                    add_sum(s, c - 1)
                            add_sum(s, CPS - 1)

                        with dve.Fori(0, STEPS) as s:
                            step_of(s)
                        if l0:
                            dve.wait_ge(cells_counted, NCH + 3)
                            dve.tensor_copy(counts[:, :], histogram[:, 0:P]).then_inc(count_copied, 1)

                    if l0:
                        @block.scalar
                        def _(act):
                            act.sem_inc(type_kept, CPS)
                            with act.Fori(0, STEPS) as s:
                                for c in range(CPS):
                                    q = s * CPS + c
                                    act.wait_ge(rows_gathered[c], s * 64 + 64 + old)
                                    act.activation(src_type[:, bass.ds(q * 4, 4)], gathered[c][:, :, F],
                                                   ACT.Copy).then_inc(type_kept, 1)
                                    act.wait_ge(attr_added, q + 1 + CPS)
                                    act.activation(gathered[c][:, :, 0:F], gathered[c][:, :, 0:F],
                                                   ACT.Relu).then_inc(relu_done, 1)
            clear_used()
            gathered_so_far[0] += STEPS * 64
            residual_pass(layer, table, width, index_dram, scale_col)

        def residual_pass(layer, table, width, index_dram, scale_col):
            with nc.If(residual > WIN - 1):
                with ExitStack() as ctx:
                    index = sb(ctx, "res_index", [P, 4], i32)
                    rows = sb(ctx, "res_rows", [P, 4, width])
                    attr = sb(ctx, "res_attr", [P, 4 * F])
                    place = sb(ctx, "res_place", [P, 4])
                    beyond = sb(ctx, "res_beyond", [P, 4])
                    onehot = sb(ctx, "res_onehot", [P, 4, WIN])
                    window_sum = ps(ctx, "res_window_sum")
                    loaded = sem(ctx, "res_loaded")
                    idle = sem(ctx, "res_idle")
                    gathered = top.enter_context(nc.semaphore(f"res_gathered_p{phase[0]}"))
                    chunk_started = sem(ctx, "res_chunk_started")
                    step = sem(ctx, "res_step")
                    placed = sem(ctx, "res_placed")
                    summed = sem(ctx, "res_summed")
                    added = sem(ctx, "res_added")
                    HEAD = 5
                    with nc.Block() as block:
                        @block.sync
                        def _(sp):
                            with sp.Fori(0, NCH) as g:
                                sp.wait_ge(added, g * NB + 1)
                                sp.dma_start(index[:, :], index_dram[:, bass.ds(g * 4, 4)]).then_inc(loaded, 16)
                                sp.dma_start(attr[:, :].unsqueeze(1), A["attr48"][bass.ds(g, 1), :, :]
                                             .rearrange("c p f -> p c f")).then_inc(loaded, 16)

                        @block.scalar
                        def _(act):
                            act.sem_inc(idle, 1)

                        @block.gpsimd
                        def _(pool):
                            with pool.Fori(0, NCH) as g:
                                pool.wait_ge(loaded, g * 32 + 32)
                                pool.sem_inc(chunk_started, 1)
                                for j in range(4):
                                    pool.indirect_dma_start(
                                        rows[:, j, :], None, table,
                                        bass.IndirectOffsetOnAxis(ap=index[:, j:j + 1], axis=0)).then_inc(gathered, 16)

                        @block.vector
                        def _(dve):
                            dve.sem_inc(added, 1)
                            with dve.Fori(0, NCH) as g:
                                cols = slice(None), bass.ds(g * 4, 4)
                                dve.tensor_scalar(beyond[:, :], rel_col[cols], float(WIN), None,
                                                  ALU.is_ge).then_inc(step, 1)
                                dve.wait_ge(step, g * HEAD + 1)
                                dve.scalar_tensor_tensor(out=place[:, :], in0=dst_cols[cols], scalar=1.0,
                                                         in1=beyond[:, :], op0=ALU.add, op1=ALU.mult).then_inc(step, 1)
                                dve.wait_ge(step, g * HEAD + 2)
                                dve.tensor_scalar(place[:, :], place[:, :], -1.0, None, ALU.add).then_inc(step, 1)
                                dve.wait_ge(gathered, g * 64 + 64)
                                if layer == 0:
                                    dve.tensor_tensor(rows[:, :, 0:F], rows[:, :, 0:F],
                                                      attr[:, :].rearrange("p (j f) -> p j f", f=F),
                                                      ALU.add).then_inc(step, 1)
                                    dve.wait_ge(step, g * HEAD + 4)
                                    dve.tensor_scalar(rows[:, :, 0:F], rows[:, :, 0:F], 0.0, None,
                                                      ALU.max).then_inc(step, 1)
                                else:
                                    dve.tensor_copy(beyond[:, :], beyond[:, :]).then_inc(step, 2)
                                with dve.Fori(0, NB) as k:
                                    dve.wait_ge(step, g * HEAD + HEAD)
                                    for j in range(4):
                                        scale = None if scale_col is None else scale_col[:, bass.ds(g * 4 + j, 1)]
                                        if scale is None:
                                            oh = dve.tensor_scalar(onehot[:, j, :], iota[:, :], place[:, j:j + 1],
                                                                   None, ALU.is_equal)
                                        else:
                                            oh = dve.tensor_scalar(onehot[:, j, :], iota[:, :], place[:, j:j + 1],
                                                                   scale, ALU.is_equal, ALU.mult)
                                    oh.then_inc(placed, 1)
                                    dve.wait_ge(placed, (g * NB + k) * 2 + 1)
                                    dve.tensor_scalar(place[:, :], place[:, :], -float(WIN), None,
                                                      ALU.add).then_inc(placed, 1)
                                    dve.wait_ge(placed, (g * NB + k) * 2 + 2)
                                    dve.wait_ge(summed, g * NB + k + 1)
                                    dve.tensor_tensor(accT[:, bass.ds(k * WIN, WIN)], accT[:, bass.ds(k * WIN, WIN)],
                                                      window_sum[0:F, 0:WIN], ALU.add).then_inc(added, 1)

                        @block.tensor
                        def _(pe):
                            with pe.Fori(0, NCH) as g:
                                with pe.Fori(0, NB) as k:
                                    pe.wait_ge(step, g * HEAD + HEAD)
                                    pe.wait_ge(placed, (g * NB + k) * 2 + 1)
                                    pe.wait_ge(added, g * NB + k + 1)
                                    for j in range(4):
                                        mm = pe.matmul(window_sum[0:F, 0:WIN], rows[:, j, 0:F], onehot[:, j, :],
                                                       start=(j == 0), stop=(j == 3))
                                    mm.then_inc(summed, 1)
                clear_used()

        def node_update(per_group, weight=None, n_dve=1):
            by_block = accT[:, 0:NP].rearrange("f (p b) -> f b p", b=NB)
            with ExitStack() as ctx:
                staged = [sb(ctx, f"staged{k}", [F, GB, P]) for k in range(2)]
                tmp = [sb(ctx, f"update_tmp{k}", [P, GB, F]) for k in range(2)]
                turned = [ps(ctx, f"turned{k}", [P, GB, F]) for k in range(2)]
                product = [ps(ctx, f"product{k}", [P, GB, F]) for k in range(2)]
                staged_ready = sem(ctx, "staged_ready")
                turned_ready = sem(ctx, "turned_ready")
                step = sem(ctx, "update_step")
                with nc.Block() as block:
                    @block.scalar
                    def _(act):
                        with act.Fori(0, NG // 2) as s:
                            for k in range(2):
                                act.wait_ge(turned_ready, s * 2 + k + 1)
                                act.activation(staged[k][:, :, :], by_block[:, bass.ds((s * 2 + k) * GB, GB), :],
                                               ACT.Copy).then_inc(staged_ready, 1)

                    @block.tensor
                    def _(pe):
                        pe.sem_inc(turned_ready, 2)
                        with pe.Fori(0, NG // 2) as s:
                            for k in range(2):
                                pe.wait_ge(staged_ready, s * 2 + k + 1)
                                pe.wait_ge(step, (s * 2 + k + 1) * n_dve)
                                for j in range(GB):
                                    mm = pe.matmul(turned[k][:, j, :], staged[k][:, j, :], ident[0:F, 0:F],
                                                   start=True, stop=True)
                                    if weight is not None:
                                        mm = pe.matmul(product[k][:, j, :], staged[k][:, j, :], weight,
                                                       start=True, stop=True)
                                mm.then_inc(turned_ready, 1)

                    @block.vector
                    def _(dve):
                        dve.sem_inc(step, 2 * n_dve)
                        with dve.Fori(0, NG // 2) as s:
                            for k in range(2):
                                dve.wait_ge(turned_ready, s * 2 + k + 1 + 2)
                                per_group(dve, (s * 2 + k) * GB, turned[k], product[k], tmp[k], step,
                                          (s * 2 + k + 2) * n_dve)
            clear_used()

        def clear_accT():
            with ExitStack() as ctx:
                cleared = sem(ctx, "acc_cleared")
                with nc.Block() as block:
                    @block.vector
                    def _(dve):
                        dve.memset(accT[:, :], 0.0).then_inc(cleared, 1)
                        dve.wait_ge(cleared, 1)
            clear_used()

        def group(tile, b0):
            return tile[:, bass.ds(b0, GB), 0:F]

        def per_node(col, b0):
            return col[:, bass.ds(b0, GB)].unsqueeze(2).broadcast_to([P, GB, F])

        layer_norm_relu()

        def fill_h(dve, step):
            dve.tensor_copy(w_nodes[:, :, 0:F], h_nodes[:, :, :]).then_inc(step, 1)
            return 1

        store_table(table_l0, TW, fill_h)
        edge_pass(0, table_l0, TW, A["src"], None)
        only_l0.close()

        def update_l0(dve, b0, turned, product, tmp, step, n):
            dve.tensor_tensor(group(x_nodes, b0), group(x_nodes, b0), turned[:, :, :], ALU.add).then_inc(step, 1)

        node_update(update_l0)

        with ExitStack() as ctx:
            one_eps = sb(ctx, "one_eps", [P, 1])
            got = sem(ctx, "eps_loaded")
            step = sem(ctx, "eps_step")
            with nc.Block() as block:
                @block.sync
                def _(sp):
                    sp.dma_start(one_eps[:, :], A["eps"].broadcast_to([P, 1])).then_inc(got, 16)

                @block.vector
                def _(dve):
                    dve.wait_ge(got, 16)
                    dve.tensor_scalar(one_eps[:, :], one_eps[:, :], 1.0, None, ALU.add).then_inc(step, 1)
                    dve.wait_ge(step, 1)
                    dve.scalar_tensor_tensor(out=x_nodes[:, :, :], in0=h_nodes[:, :, :], scalar=one_eps[:, 0:1],
                                             in1=x_nodes[:, :, :], op0=ALU.mult, op1=ALU.add).then_inc(step, 1)
        clear_used()

        layer_norm_relu()
        with ExitStack() as ctx:
            w1 = sb(ctx, "w1", [F, RP, 2 * F])
            w2 = sb(ctx, "w2", [2 * F, RP, 2 * F])
            bias1 = sb(ctx, "bias1", [2 * F, 1])
            h_stage = sb(ctx, "h_stage", [P, GB, F])
            hT = sb(ctx, "hT", [F, GB * P])
            h1T = sb(ctx, "h1T", [2 * F, RP, GB * P])
            rows = sb(ctx, "rel_rows", [P, GB, NR * F])
            hT_ps = ps(ctx, "hT_ps", [P, 1024])
            h1_ps = [ps(ctx, f"h1_ps{k}") for k in range(2)]
            h2_ps = [ps(ctx, f"h2_ps{k}") for k in range(2)]
            HALF = GB * P // 2
            weights = sem(ctx, "weights")
            zeroed = sem(ctx, "w2_zeroed")
            h_staged = sem(ctx, "h_staged")
            turned = sem(ctx, "h_turned")
            hT_ready = sem(ctx, "hT_ready")
            h1_ready = sem(ctx, "h1_ready")
            h1_taken = sem(ctx, "h1_taken")
            h2_ready = sem(ctx, "h2_ready")
            h2_taken = sem(ctx, "h2_taken")
            stored = sem(ctx, "rel_stored")
            N1 = RP * 2
            with nc.Block() as block:
                @block.gpsimd
                def _(pool):
                    pool.memset(w2[:, :, :], 0.0).then_inc(zeroed, 1)

                @block.sync
                def _(sp):
                    sp.dma_start(w1[:, :, :], A["w1"].rearrange("i (c n) -> i c n", c=RP)).then_inc(weights, 16)
                    sp.wait_ge(zeroed, 1)
                    for k in range(2):
                        sp.dma_start(w2[k * F:(k + 1) * F, :, k * F:(k + 1) * F],
                                     A["w2"].rearrange("i (c k o) -> i c k o", k=2, o=F)[:, :, k, :]
                                     ).then_inc(weights, 16)
                        sp.dma_start(bias1[k * F:(k + 1) * F, :], A["bias1"].rearrange("(f a) -> f a", a=1)
                                     ).then_inc(weights, 16)
                    table = table_l1.rearrange("(p b r) f -> p b (r f)", b=NB, r=NR)
                    with sp.Fori(0, NG) as g:
                        sp.wait_ge(h2_taken, g * GB + GB + 2)
                        sp.dma_start(table[:, bass.ds(g * GB, GB), :], rows[:, :, :]).then_inc(stored, 16)
                    sp.wait_ge(stored, NG * 16)

                @block.tensor
                def _(pe):
                    pe.wait_ge(weights, 80)

                    def group_of(g, first):
                        pe.wait_ge(h_staged, g + 1)
                        if not first:
                            pe.wait_ge(hT_ready, g)
                        for j in range(GB):
                            mm = pe.matmul(hT_ps[0:F, j * P:(j + 1) * P], h_stage[:, j, :], ident[:, :],
                                           start=True, stop=True)
                        mm.then_inc(turned, 1)
                        pe.wait_ge(hT_ready, g + 1)
                        for c in range(RP):
                            for k in range(2):
                                n = 2 * c + k
                                pe.wait_ge(h1_taken, g * N1 + n + 1)
                                pe.matmul(h1_ps[k][0:2 * F, 0:HALF], w1[:, c, :], hT[:, k * HALF:(k + 1) * HALF],
                                          start=True, stop=True).then_inc(h1_ready, 1)
                        pe.wait_ge(h1_taken, g * N1 + N1 + 2)
                        for j in range(GB):
                            k = j % 2
                            pe.wait_ge(h2_taken, g * GB + j + 1)
                            for c in range(RP):
                                mm = pe.matmul(h2_ps[k][:, c * 2 * F:(c + 1) * 2 * F], h1T[:, c, j * P:(j + 1) * P],
                                               w2[:, c, :], start=True, stop=True)
                            if j == GB - 1:
                                pe.wait_ge(h2_taken, g * GB + j + 2)
                            mm.then_inc(h2_ready, 1)

                    steps_from_first(pe, NG, group_of)

                @block.scalar
                def _(act):
                    act.sem_inc(h1_taken, 2)
                    act.wait_ge(weights, 80)

                    def group_of(g, first):
                        for c in range(RP):
                            for k in range(2):
                                n = 2 * c + k
                                act.wait_ge(h1_ready, g * N1 + n + 1)
                                if not first:
                                    act.wait_ge(h2_ready, g * GB)
                                act.activation(h1T[:, c, k * HALF:(k + 1) * HALF], h1_ps[k][0:2 * F, 0:HALF],
                                               ACT.Relu, bias=bias1[:, 0:1]).then_inc(h1_taken, 1)

                    steps_from_first(act, NG, group_of)

                @block.vector
                def _(dve):
                    dve.sem_inc(h2_taken, 2)

                    def group_of(g, first):
                        if not first:
                            dve.wait_ge(turned, g)
                        dve.tensor_copy(h_stage[:, :, :], group(h_nodes, g * GB)).then_inc(h_staged, 1)
                        dve.wait_ge(turned, g + 1)
                        if not first:
                            dve.wait_ge(h1_ready, g * N1)
                        dve.tensor_copy(hT[:, :], hT_ps[0:F, 0:GB * P]).then_inc(hT_ready, 1)
                        if not first:
                            dve.wait_ge(stored, g * 16)
                        for j in range(GB):
                            dve.wait_ge(h2_ready, g * GB + j + 1)
                            dve.tensor_copy(rows[:, j, :], h2_ps[j % 2][:, 0:NR * F]).then_inc(h2_taken, 1)

                    steps_from_first(dve, NG, group_of)
        clear_used()
        clear_accT()
        edge_pass(1, table_l1, F, src_rel, norm_col)

        def load_row(tile, row, tag):
            with ExitStack() as ctx:
                got = sem(ctx, "row_loaded_" + tag)
                with nc.Block() as block:
                    @block.sync
                    def _(sp):
                        sp.dma_start(tile, row).then_inc(got, 16)
                        sp.wait_ge(got, 16)
            clear_used()

        with ExitStack() as outer:
            bias2 = sb(outer, "bias2", [P, F])
            load_row(bias2[:, :], A["bias2"].broadcast_to([P, F]), "bias2")

            def update_l1(dve, b0, turned, product, tmp, step, n):
                dve.tensor_tensor(tmp[:, :, :], turned[:, :, :], bias2[:, :].unsqueeze(1).broadcast_to([P, GB, F]),
                                  ALU.add).then_inc(step, 1)
                dve.wait_ge(step, n + 1)
                dve.scalar_tensor_tensor(out=group(x_nodes, b0), in0=tmp[:, :, :], scalar=0.0,
                                         in1=group(x_nodes, b0), op0=ALU.max, op1=ALU.add).then_inc(step, 1)

            node_update(update_l1, n_dve=2)

        layer_norm_relu()
        with ExitStack() as outer:
            cheb = sb(outer, "cheb", [F, 4, F])
            bias = sb(outer, "cheb_bias", [P, F])
            inv_root = sb(outer, "inv_root", [P, NB])
            minus = sb(outer, "minus_inv_root", [P, NB])
            minus_sq = sb(outer, "minus_sq", [P, NB])
            with ExitStack() as ctx:
                got = sem(ctx, "cheb_loaded")
                step = sem(ctx, "cheb_step")
                root = sem(ctx, "cheb_root")
                has_edge = sb(ctx, "has_edge", [P, NB])
                with nc.Block() as block:
                    @block.sync
                    def _(sp):
                        sp.dma_start(cheb[:, :, :], A["cheb"].rearrange("i (k o) -> i k o", k=4)).then_inc(got, 16)
                        sp.dma_start(bias[:, :], A["cheb_bias"].broadcast_to([P, F])).then_inc(got, 16)

                    @block.scalar
                    def _(act):
                        act.wait_ge(step, 2)
                        act.activation(inv_root[:, :], inv_root[:, :], ACT.Sqrt).then_inc(root, 1)

                    @block.vector
                    def _(dve):
                        dve.tensor_scalar(has_edge[:, :], degree[:, :], 0.0, None, ALU.is_gt).then_inc(step, 1)
                        dve.tensor_scalar(inv_root[:, :], degree[:, :], 1.0, None, ALU.max).then_inc(step, 1)
                        dve.wait_ge(root, 1)
                        dve.reciprocal(inv_root[:, :], inv_root[:, :]).then_inc(step, 1)
                        dve.wait_ge(step, 3)
                        dve.tensor_tensor(inv_root[:, :], inv_root[:, :], has_edge[:, :], ALU.mult).then_inc(step, 1)
                        dve.wait_ge(step, 4)
                        dve.tensor_scalar(minus[:, :], inv_root[:, :], -1.0, None, ALU.mult).then_inc(step, 1)
                        dve.wait_ge(step, 5)
                        dve.tensor_tensor(minus_sq[:, :], minus[:, :], inv_root[:, :], ALU.mult).then_inc(step, 1)
                        dve.wait_ge(got, 32)
                        dve.tensor_tensor(cheb[:, 0:2, :], cheb[:, 0:2, :], cheb[:, 2:4, :], ALU.subtract).then_inc(step, 1)
                        dve.wait_ge(step, 7)
                        dve.tensor_scalar(cheb[:, 2:4, :], cheb[:, 2:4, :], 2.0, None, ALU.mult).then_inc(step, 1)
                        dve.wait_ge(step, 8)
            clear_used()

            with ExitStack() as ctx:
                h_stage = [sb(ctx, f"h_stage{k}", [P, GB, F]) for k in range(2)]
                hT = [sb(ctx, f"hT{k}", [F, GB * P]) for k in range(2)]
                tmp = [sb(ctx, f"tmp{k}", [P, GB, F]) for k in range(2)]
                hT_ps = [ps(ctx, f"hT_ps{k}", [P, 1024]) for k in range(2)]
                prod = [ps(ctx, f"prod{k}", [P, GB, F]) for k in range(2)]
                staged = sem(ctx, "staged")
                turned = sem(ctx, "turned")
                copied = sem(ctx, "copied")
                made = sem(ctx, "made")
                taken = sem(ctx, "taken")
                with nc.Block() as block:
                    @block.vector
                    def _(dve):
                        def two_groups(s, first):
                            for k in range(2):
                                if not first:
                                    dve.wait_ge(turned, s * 2 + k)
                                dve.tensor_copy(h_stage[k][:, :, :], group(h_nodes, (s * 2 + k) * GB)).then_inc(staged, 1)
                            for k in range(2):
                                q = s * 2 + k
                                dve.wait_ge(made, q + 1)
                                dve.tensor_tensor(tmp[k][:, :, :], prod[k][:, :, :],
                                                  bias[:, :].unsqueeze(1).broadcast_to([P, GB, F]),
                                                  ALU.add).then_inc(taken, 1)
                                dve.wait_ge(taken, q * 2 + 1)
                                dve.tensor_tensor(group(x_nodes, q * GB), group(x_nodes, q * GB), tmp[k][:, :, :],
                                                  ALU.add).then_inc(taken, 1)

                        steps_from_first(dve, NG // 2, two_groups)

                    @block.tensor
                    def _(pe):
                        def two_groups(s, first):
                            for k in range(2):
                                q = s * 2 + k
                                pe.wait_ge(staged, q + 1)
                                if not first:
                                    pe.wait_ge(copied, q)
                                for j in range(GB):
                                    mm = pe.matmul(hT_ps[k][0:F, j * P:(j + 1) * P], h_stage[k][:, j, :], ident[:, :],
                                                   start=True, stop=True)
                                mm.then_inc(turned, 1)
                            for k in range(2):
                                q = s * 2 + k
                                pe.wait_ge(copied, q + 1)
                                if not first:
                                    pe.wait_ge(taken, s * 4)
                                for j in range(GB):
                                    mm = pe.matmul(prod[k][:, j, :], hT[k][:, j * P:(j + 1) * P], cheb[:, 0, :],
                                                   start=True, stop=True)
                                mm.then_inc(made, 1)

                        steps_from_first(pe, NG // 2, two_groups)

                    @block.scalar
                    def _(act):
                        def two_groups(s, first):
                            for k in range(2):
                                q = s * 2 + k
                                act.wait_ge(turned, q + 1)
                                if not first:
                                    act.wait_ge(made, s * 2)
                                act.activation(hT[k][:, :], hT_ps[k][0:F, 0:GB * P], ACT.Copy).then_inc(copied, 1)

                        steps_from_first(act, NG // 2, two_groups)
            clear_used()

            def fill_scaled(dve, step):
                dve.tensor_tensor(h_nodes[:, :, :], h_nodes[:, :, :],
                                  inv_root[:, :].unsqueeze(2).broadcast_to([P, NB, F]), ALU.mult).then_inc(step, 1)
                dve.wait_ge(step, 1)
                dve.tensor_copy(w_nodes[:, :, 0:F], h_nodes[:, :, :]).then_inc(step, 1)
                return 2

            store_table(table_l2, F, fill_scaled)

            def fill_ready(dve, step):
                dve.nop().then_inc(step, 1)
                return 1

            for k in (1, 2, 3):
                clear_accT()
                edge_pass(2, table_l2, F, A["src"], other_end)

                def update_l2(dve, b0, turned, product, tmp, step, n):
                    dve.tensor_tensor(tmp[:, :, :], product[:, :, :], per_node(minus, b0), ALU.mult).then_inc(step, 1)
                    dve.wait_ge(step, n + 1)
                    dve.tensor_tensor(group(x_nodes, b0), group(x_nodes, b0), tmp[:, :, :], ALU.add).then_inc(step, 1)
                    dve.wait_ge(step, n + 2)
                    if k == 1:
                        dve.tensor_tensor(group(w_nodes, b0), turned[:, :, :], per_node(minus_sq, b0),
                                          ALU.mult).then_inc(step, 2)
                    elif k == 2:
                        dve.tensor_tensor(tmp[:, :, :], turned[:, :, :], per_node(minus_sq, b0), ALU.mult).then_inc(step, 1)
                        dve.wait_ge(step, n + 3)
                        dve.scalar_tensor_tensor(out=group(w_nodes, b0), in0=tmp[:, :, :], scalar=2.0,
                                                 in1=group(h_nodes, b0), op0=ALU.mult,
                                                 op1=ALU.subtract).then_inc(step, 1)

                node_update(update_l2, weight=cheb[:, k, :], n_dve=2 if k == 3 else 4)
                if k < 3:
                    store_table(table_l2, F, fill_ready)
        agg.close()

        layer_norm_relu()
        layer3 = ExitStack()
        top.enter_context(layer3)
        src_f = sb(layer3, "src_f", [P, T])
        cutoff = sb(layer3, "cutoff", [P, T])
        w1 = sb(layer3, "filter_w1", [R, F])
        b1 = sb(layer3, "filter_b1", [F, 1])
        w2 = sb(layer3, "filter_w2", [F + 16, F])
        gamma = sb(layer3, "gamma", [P, F])
        beta = sb(layer3, "beta", [P, F])
        spare = sb(layer3, "spare", [P, 1])
        ones = sb(layer3, "ones", [F + 16, 512])
        with ExitStack() as ctx:
            rows3 = sb(ctx, "rows3", [P, GB, ROW])
            emb_t = sb(ctx, "emb_t", [ZD, NZ])
            adapt_t = sb(ctx, "adapt_t", [ZD, ZD])
            ab = sb(ctx, "ab", [ZD, NZ])
            logits = sb(ctx, "logits", [NZ, NZ])
            type_cols = sb(ctx, "type_cols", [P, NB], i32)
            type_now = sb(ctx, "type_now", [P, GB], i32)
            mult = sb(ctx, "mult", [P, NB])
            dist = sb(ctx, "dist", [P, T])
            near = sb(ctx, "near", [P, T])
            half_pi = sb(ctx, "half_pi", [P, 1])
            zeros = sb(ctx, "zeros", [P, NB + 1, MW])
            pA = ps(ctx, "pA")
            pB = ps(ctx, "pB")
            small = sem(ctx, "small_loaded")
            dist_loaded = sem(ctx, "dist_loaded")
            consts = sem(ctx, "l3_consts")
            made = sem(ctx, "l3_made")
            prod = sem(ctx, "l3_prod")
            wave = sem(ctx, "l3_wave")
            logit_stored = sem(ctx, "logit_stored")
            zeroed = sem(ctx, "sums_zeroed")
            type_ready = sem(ctx, "type_ready")
            group_started = sem(ctx, "group_started")
            logit_rows = top.enter_context(nc.semaphore("logit_rows"))
            rows_ready = sem(ctx, "rows_ready")
            stored = sem(ctx, "l3_stored")
            with nc.Block() as block:
                @block.sync
                def _(sp):
                    for tile, what in ((emb_t[:, :], A["emb_t"]), (adapt_t[:, :], A["adapt_t"]),
                                       (type_cols[:, :], A["node_type"]), (mult[:, :], A["node_vec"]),
                                       (w1[:, :], A["fw1_t"]), (w2[0:F, :], A["fw2_t"]),
                                       (w2[F:F + 1, :], A["fb2"]), (b1[:, :], A["fb1"]),
                                       (gamma[:, :], A["gamma"].broadcast_to([P, F])),
                                       (beta[:, :], A["beta"].broadcast_to([P, F]))):
                        sp.dma_start(tile, what).then_inc(small, 16)
                    sp.wait_ge(made, 2)
                    sp.dma_start(logit_table, logits[:, :]).then_inc(logit_stored, 16)
                    table = table_l3.rearrange("(p b) f -> p b f", b=NB)
                    with sp.Fori(0, NG) as g:
                        sp.wait_ge(rows_ready, g + 1)
                        sp.wait_ge(logit_rows, g * (GB * 16) + GB * 16)
                        sp.dma_start(table[:, bass.ds(g * GB, GB), :], rows3[:, :, :]).then_inc(stored, 16)
                    sp.wait_ge(stored, NG * 16)
                    sp.wait_ge(small, 160)

                @block.scalar
                def _(act):
                    act.dma_start(dist[:, :], A["dist"]).then_inc(dist_loaded, 16)
                    act.wait_ge(consts, 4)
                    for k in range(NT):
                        act.dma_start(sums[k].rearrange("(p b) f -> p b f", b=NB + 1), zeros[:, :, :]).then_inc(zeroed, 16)
                    act.wait_ge(made, 4)
                    act.activation(dist[:, :], dist[:, :], ACT.Sin, bias=half_pi[:, 0:1],
                                   scale=-float(np.pi) / CUTOFF).then_inc(wave, 1)
                    act.wait_ge(zeroed, NT * 16)

                @block.gpsimd
                def _(pool):
                    pool.memset(zeros[:, :, :], 0.0).then_inc(consts, 1)
                    pool.memset(half_pi[:, :], float(np.pi) / 2).then_inc(consts, 1)
                    pool.memset(ones[:, :], 1.0).then_inc(consts, 1)
                    pool.iota(spare[:, :], pattern=[[0, 1]], base=NP, channel_multiplier=1,
                              allow_small_or_imprecise_dtypes=True).then_inc(consts, 1)
                    pool.wait_ge(logit_stored, 16)

                    def group_of(g, first):
                        pool.wait_ge(type_ready, g + 1)
                        if not first:
                            pool.wait_ge(stored, g * 16)
                        pool.sem_inc(group_started, 1)
                        for j in range(GB):
                            pool.indirect_dma_start(
                                rows3[:, j, F + 1:ROW], None, logit_table,
                                bass.IndirectOffsetOnAxis(ap=type_now[:, j:j + 1], axis=0)).then_inc(logit_rows, 16)

                    steps_from_first(pool, NG, group_of)

                @block.tensor
                def _(pe):
                    pe.wait_ge(small, 160)
                    pe.matmul(pA[0:ZD, 0:NZ], adapt_t[:, :], emb_t[:, :], start=True, stop=True).then_inc(prod, 1)
                    pe.wait_ge(made, 1)
                    pe.matmul(pB[0:NZ, 0:NZ], emb_t[:, :], ab[:, :], start=True, stop=True).then_inc(prod, 1)

                @block.vector
                def _(dve):
                    dve.wait_ge(prod, 1)
                    dve.tensor_copy(ab[:, :], pA[0:ZD, 0:NZ]).then_inc(made, 1)
                    dve.wait_ge(prod, 2)
                    dve.tensor_copy(logits[:, :], pB[0:NZ, 0:NZ]).then_inc(made, 1)
                    dve.wait_ge(dist_loaded, 16)
                    dve.tensor_scalar(near[:, :], dist[:, :], CUTOFF, None, ALU.is_lt).then_inc(made, 1)
                    dve.wait_ge(made, 3)
                    dve.tensor_scalar(dist[:, :], dist[:, :], -CUTOFF, CUTOFF, ALU.max, ALU.min).then_inc(made, 1)
                    dve.tensor_copy(src_f[:, :], src_cols[:, :]).then_inc(made, 1)
                    dve.wait_ge(wave, 1)
                    dve.tensor_scalar(dist[:, :], dist[:, :], 1.0, 0.5, ALU.add, ALU.mult).then_inc(made, 1)
                    dve.wait_ge(made, 6)
                    dve.tensor_tensor(cutoff[:, :], dist[:, :], near[:, :], ALU.mult).then_inc(made, 1)
                    dve.wait_ge(small, 160)

                    def group_of(g, first):
                        if not first:
                            dve.wait_ge(logit_rows, g * (GB * 16))
                            dve.wait_ge(stored, g * 16)
                        dve.tensor_copy(type_now[:, :], type_cols[:, bass.ds(g * GB, GB)]).then_inc(type_ready, 1)
                        dve.tensor_copy(rows3[:, :, 0:F], group(h_nodes, g * GB))
                        dve.tensor_copy(rows3[:, :, F], mult[:, bass.ds(g * GB, GB)]).then_inc(rows_ready, 1)

                    steps_from_first(dve, NG, group_of)
        clear_used()

        with ExitStack() as ctx:
            RS = 4
            old = gathered_so_far[0]
            index = [sb(ctx, f"dst_index{h}", [P, HC * 4], i32) for h in range(2)]
            attr_t = [sb(ctx, f"attr_t{h}", [R, HC * 512]) for h in range(2)]
            src_b = [sb(ctx, f"src_b{h}", [P, HC * 512], i32) for h in range(2)]
            rows = [sb(ctx, f"dst_rows{k}", [P, 4, ROW]) for k in range(RS)]
            hidden = [sb(ctx, f"hidden{k}", [F + 16, 512]) for k in range(2)]
            same = [sb(ctx, f"same{k}", [P, 4, P]) for k in range(2)]
            junk = sb(ctx, "junk", [P, 8, P])
            before = [sb(ctx, f"before{k}", [P, 4]) for k in range(2)]
            logit = [sb(ctx, f"logit{k}", [P, 4]) for k in range(2)]
            weight = [sb(ctx, f"weight{k}", [P, 4]) for k in range(2)]
            msg = [sb(ctx, f"msg{k}", [P, 4, MW]) for k in range(2)]
            to_row = [sb(ctx, f"to_row{k}", [P, 4], i32) for k in range(2)]
            summed = [sb(ctx, f"summed{k}", [P, 4, MW]) for k in range(2)]
            hid_ps = [ps(ctx, f"hid_ps{k}") for k in range(2)]
            gate_ps = [ps(ctx, f"gate_ps{k}") for k in range(2)]
            sum_ps = [ps(ctx, f"sum_ps{k}") for k in range(2)]
            index_loaded = [sem(ctx, f"index_loaded{h}") for h in range(2)]
            attr_loaded = [sem(ctx, f"attr_loaded{h}") for h in range(2)]
            src_loaded = [sem(ctx, f"src_loaded{h}") for h in range(2)]
            rows_gathered = slot_gathered[:RS]
            hid_made = sem(ctx, "hid_made")
            silu_done = sem(ctx, "silu_done")
            gate_made = sem(ctx, "gate_made")
            same_made = sem(ctx, "same_made")
            step = sem(ctx, "msg_step")
            msg_made = sem(ctx, "msg_made")
            sums_made = sem(ctx, "sums_made")
            summed_ready = sem(ctx, "summed_ready")
            scattered = slot_scattered
            dma_turn = sem(ctx, "dma_turn")
            filter_turn = sem(ctx, "filter_turn")
            D = 6
            with nc.Block() as block:
                @block.sync
                def _(sp):
                    with sp.Fori(0, STEPS) as s:
                        for h in range(2):
                            for k in range(RS):
                                sp.wait_ge(rows_gathered[k], s * 128 + old)
                            sp.dma_start(index[h][:, :], A["dst"][:, bass.ds((s * 2 + h) * (HC * 4), HC * 4)]
                                         ).then_inc(index_loaded[h], 16)
                            sp.wait_ge(hid_made, s * CPS + HC * (h + 1))
                            sp.dma_start(attr_t[h][:, :], A["ea_t"][bass.ds(s * 2 + h, 1), :, :]
                                         .rearrange("a r e -> (a r) e")).then_inc(attr_loaded[h], 16)
                            sp.wait_ge(same_made, s * CPS + HC * (h + 1))
                            sp.dma_start(src_b[h][:, :], A["src_lines"][bass.ds(s * 2 + h, 1), :]
                                         .broadcast_to([P, HC * 512])).then_inc(src_loaded[h], 16)

                @block.gpsimd
                def _(pool):
                    def gather(s, c):
                        if c % HC == 0:
                            pool.wait_ge(index_loaded[c // HC], s * 16 + 16)
                        pool.wait_ge(msg_made, s * CPS + c + 1)
                        pool.sem_inc(dma_turn, 1)
                        for j in range(4):
                            t = (c % HC) * 4 + j
                            pool.indirect_dma_start(
                                rows[c % RS][:, j, :], None, table_l3,
                                bass.IndirectOffsetOnAxis(ap=index[c // HC][:, t:t + 1], axis=0),
                            ).then_inc(rows_gathered[c % RS], 16)

                    def scatter(s, c, first):
                        pool.wait_ge(summed_ready, s * CPS + c + 1 + 2)
                        if not (first and c < 2):
                            pool.wait_ge(scattered[c % 2], s * 256 + (c // 2) * 64)
                        pool.sem_inc(dma_turn, 1)
                        for j in range(4):
                            pool.indirect_dma_start(
                                sums[(c % 2) * 4 + j],
                                bass.IndirectOffsetOnAxis(ap=to_row[c % 2][:, j:j + 1], axis=0),
                                summed[c % 2][:, j, :], None, compute_op=ALU.add,
                            ).then_inc(scattered[c % 2], 16)

                    AHEAD = 2
                    for c in range(AHEAD):
                        gather(0, c)

                    def step_of(s, first):
                        for c in range(CPS):
                            gather(s + (c + AHEAD) // CPS, (c + AHEAD) % CPS)
                            scatter(s, c, first)

                    steps_from_first(pool, STEPS - 1, step_of)
                    for c in range(CPS):
                        if c + AHEAD < CPS:
                            gather(STEPS - 1, c + AHEAD)
                        scatter(STEPS - 1, c, False)
                    for k in range(2):
                        pool.wait_ge(scattered[k], STEPS * 256)

                @block.tensor
                def _(pe):
                    pe.sem_inc(hid_made, CPS)
                    pe.sem_inc(gate_made, 2)
                    pe.sem_inc(sums_made, 2)

                    def filters(s, c):
                        q = s * CPS + c
                        pe.wait_ge(attr_loaded[c // HC], s * 16 + 16)
                        pe.wait_ge(silu_done, q + 1)
                        pe.sem_inc(filter_turn, 1)
                        pe.matmul(hid_ps[c % 2][0:F, :], w1[:, :],
                                  attr_t[c // HC][:, (c % HC) * 512:(c % HC + 1) * 512],
                                  start=True, stop=True).then_inc(hid_made, 1)
                        pe.wait_ge(silu_done, q + 1 + 2)
                        pe.wait_ge(msg_made, q + 1 + RS - 2)
                        for j in range(4):
                            mm = pe.matmul(gate_ps[c % 2][:, j * F:(j + 1) * F], hidden[c % 2][0:F + 1, j * P:(j + 1) * P],
                                           w2[0:F + 1, :], start=True, stop=True)
                        mm.then_inc(gate_made, 1)

                    def totals(s, c):
                        q = s * CPS + c
                        pe.wait_ge(same_made, q + 1 + CPS)
                        pe.wait_ge(msg_made, q + 1 + RS)
                        pe.wait_ge(summed_ready, q + 1)
                        for j in range(4):
                            mm = pe.matmul(sum_ps[c % 2][:, j * MW:(j + 1) * MW], same[c % 2][:, j, :],
                                           msg[c % 2][:, j, :], start=True, stop=True)
                        mm.then_inc(sums_made, 1)

                    with pe.Fori(0, STEPS) as s:
                        filters(s, 0)
                        for c in range(CPS):
                            if c + 1 < CPS:
                                filters(s, c + 1)
                            totals(s, c)

                @block.scalar
                def _(act):
                    act.sem_inc(silu_done, 2)
                    act.sem_inc(summed_ready, 2)
                    for k in range(2):
                        act.activation(hidden[k][:, :], ones[:, :], ACT.Copy)
                    act.drain()

                    def silu(s, c):
                        q = s * CPS + c
                        act.wait_ge(hid_made, q + 1 + CPS)
                        act.wait_ge(gate_made, q + 1)
                        act.activation(hidden[c % 2][0:F, :], hid_ps[c % 2][0:F, :], ACT.Silu,
                                       bias=b1[:, 0:1]).then_inc(silu_done, 1)

                    def step_of(s, first):
                        silu(s, 0)
                        for c in range(CPS):
                            if c + 1 < CPS:
                                silu(s, c + 1)
                            act.wait_ge(sums_made, s * CPS + c + 1 + 2)
                            if not (first and c < 2):
                                act.wait_ge(scattered[c % 2], s * 256 + (c // 2) * 64)
                            act.activation(summed[c % 2][:, :, :].rearrange("p j f -> p (j f)"),
                                           sum_ps[c % 2][:, 0:4 * MW], ACT.Copy).then_inc(summed_ready, 1)

                    steps_from_first(act, STEPS, step_of)

                @block.vector
                def _(dve):
                    dve.sem_inc(same_made, CPS)
                    dve.sem_inc(msg_made, RS)

                    def step_of(s, first):
                        for c in range(CPS):
                            q = s * CPS + c
                            k = c % 2
                            n = q * D
                            dve.wait_ge(src_loaded[c // HC], s * 16 + 16)
                            dve.wait_ge(sums_made, q + 1)
                            if not (first and c < 2):
                                dve.wait_ge(scattered[k], s * 256 + (c // 2) * 64)
                            for j in range(4):
                                line = src_b[c // HC][:, (c % HC) * 512 + j * P:(c % HC) * 512 + (j + 1) * P]
                                col = src_f[:, bass.ds(q * 4 + j, 1)]
                                dve.tensor_scalar(same[k][:, j, :], line, col, None, ALU.is_equal)
                                got = dve.scalar_tensor_tensor(out=junk[:, j, :], in0=line, scalar=col, in1=earlier[:, :],
                                                               op0=ALU.is_equal, op1=ALU.mult,
                                                               accum_out=before[k][:, j:j + 1])
                            got.then_inc(step, 1)
                            dve.wait_ge(step, n + 1)
                            dve.tensor_scalar(before[k][:, :], before[k][:, :], float(2 * NP), spare[:, 0:1],
                                              ALU.mult, ALU.min).then_inc(step, 1)
                            dve.wait_ge(rows_gathered[c % RS], s * 128 + (c // RS) * 64 + 64 + old)
                            r = rows[c % RS]
                            for j in range(4):
                                got = dve.scalar_tensor_tensor(out=junk[:, 4 + j, 0:NZ], in0=iota[:, 0:NZ],
                                                               scalar=src_type[:, bass.ds(q * 4 + j, 1)],
                                                               in1=r[:, j, F + 1:ROW], op0=ALU.is_equal,
                                                               op1=ALU.mult, accum_out=logit[k][:, j:j + 1])
                            got.then_inc(step, 1)
                            dve.wait_ge(step, n + 2)
                            dve.tensor_tensor(to_row[k][:, :], before[k][:, :], src_f[:, bass.ds(q * 4, 4)],
                                              ALU.max).then_inc(same_made, 1)
                            dve.tensor_tensor(weight[k][:, :], cutoff[:, bass.ds(q * 4, 4)], r[:, :, F],
                                              ALU.mult).then_inc(step, 1)
                            dve.wait_ge(gate_made, q + 1 + 2)
                            dve.wait_ge(step, n + 4)
                            for j in range(4):
                                got = dve.scalar_tensor_tensor(out=msg[k][:, j, 0:F], in0=gate_ps[k][:, j * F:(j + 1) * F],
                                                               scalar=logit[k][:, j:j + 1], in1=r[:, j, 0:F],
                                                               op0=ALU.add, op1=ALU.mult)
                            got.then_inc(step, 1)
                            dve.tensor_copy(msg[k][:, :, F], r[:, :, F]).then_inc(step, 1)
                            dve.wait_ge(step, n + 6)
                            dve.tensor_tensor(msg[k][:, :, 0:F], msg[k][:, :, 0:F],
                                              weight[k][:, :].unsqueeze(2).broadcast_to([P, 4, F]),
                                              ALU.mult).then_inc(msg_made, 1)

                    steps_from_first(dve, STEPS, step_of)
        clear_used()

        with ExitStack() as ctx:
            total = sb(ctx, "total", [P, NB, MW])
            part_sum = [sb(ctx, f"part_sum{k}", [P, NB, MW]) for k in range(2)]
            mean = sb(ctx, "mean", [P, NB])
            loaded = [sem(ctx, f"part_loaded{k}") for k in range(2)]
            first = sem(ctx, "first_loaded")
            step = sem(ctx, "fin_step")
            root = sem(ctx, "fin_root")
            stored = sem(ctx, "out_stored")

            def nodes_of(k):
                return sums[k][0:NP, :].rearrange("(p b) f -> p b f", b=NB)

            per = lambda col: col[:, :].unsqueeze(2).broadcast_to([P, NB, F])
            row = lambda t: t[:, :].unsqueeze(1).broadcast_to([P, NB, F])
            with nc.Block() as block:
                @block.sync
                def _(sp):
                    sp.dma_start(total[:, :, :], nodes_of(0)).then_inc(first, 16)
                    for k in range(1, NT):
                        if k > 2:
                            sp.wait_ge(step, k - 2)
                        sp.dma_start(part_sum[k % 2][:, :, :], nodes_of(k)).then_inc(loaded[k % 2], 16)
                    sp.wait_ge(step, NT - 1 + 15)
                    sp.dma_start(out, x_nodes[:, :, :]).then_inc(stored, 16)
                    sp.wait_ge(stored, 16)

                @block.scalar
                def _(act):
                    act.wait_ge(step, NT - 1 + 9)
                    act.activation(stat2[:, :], stat2[:, :], ACT.Sqrt, bias=eps_col[:, 0:1],
                                   scale=1.0 / F).then_inc(root, 1)

                @block.vector
                def _(dve):
                    n = 0

                    def done(ins):
                        ins.then_inc(step, 1)
                        return n + 1

                    dve.wait_ge(first, 16)
                    for k in range(1, NT):
                        dve.wait_ge(loaded[k % 2], 16 * ((k + 1) // 2))
                        n = done(dve.tensor_tensor(total[:, :, :], total[:, :, :], part_sum[k % 2][:, :, :], ALU.add))
                        dve.wait_ge(step, n)
                    n = done(dve.tensor_scalar(stat[:, :], total[:, :, F], 1e-8, None, ALU.max))
                    dve.wait_ge(step, n)
                    n = done(dve.reciprocal(stat[:, :], stat[:, :]))
                    dve.wait_ge(step, n)
                    n = done(dve.tensor_tensor(total[:, :, 0:F], total[:, :, 0:F], per(stat), ALU.mult))
                    dve.wait_ge(step, n)
                    n = done(dve.tensor_tensor(h_nodes[:, :, :], h_nodes[:, :, :], total[:, :, 0:F], ALU.add))
                    dve.wait_ge(step, n)
                    n = done(dve.tensor_reduce(mean[:, :], h_nodes[:, :, :], AX.X, ALU.add))
                    dve.wait_ge(step, n)
                    n = done(dve.tensor_scalar(mean[:, :], mean[:, :], -1.0 / F, None, ALU.mult))
                    dve.wait_ge(step, n)
                    n = done(dve.tensor_tensor(h_nodes[:, :, :], h_nodes[:, :, :], per(mean), ALU.add))
                    dve.wait_ge(step, n)
                    n = done(dve.tensor_tensor(w_nodes[:, :, 0:F], h_nodes[:, :, :], h_nodes[:, :, :], ALU.mult))
                    dve.wait_ge(step, n)
                    n = done(dve.tensor_reduce(stat2[:, :], w_nodes[:, :, 0:F], AX.X, ALU.add))
                    dve.wait_ge(root, 1)
                    n = done(dve.reciprocal(stat2[:, :], stat2[:, :]))
                    dve.wait_ge(step, n)
                    n = done(dve.tensor_tensor(h_nodes[:, :, :], h_nodes[:, :, :], per(stat2), ALU.mult))
                    dve.wait_ge(step, n)
                    n = done(dve.tensor_tensor(h_nodes[:, :, :], h_nodes[:, :, :], row(gamma), ALU.mult))
                    dve.wait_ge(step, n)
                    n = done(dve.tensor_tensor(h_nodes[:, :, :], h_nodes[:, :, :], row(beta), ALU.add))
                    dve.wait_ge(step, n)
                    n = done(dve.tensor_tensor(x_nodes[:, :, :], x_nodes[:, :, :], h_nodes[:, :, :], ALU.add))
                    dve.wait_ge(step, n)
                    done(dve.nop())


def kernel(x, src, dst, edge_attr_40, edge_attr_48, edge_type_8, edge_weight, edge_weight1, node_type_119, node_vec,
           L0_gnn_eps, L1_gnn_weight1, L1_gnn_weight2, L1_gnn_bias1, L1_gnn_bias2, L2_gnn_weight, L2_gnn_bias,
           L3_gnn_W1, L3_gnn_b1, L3_gnn_W2, L3_gnn_b2, L3_gnn_emb, L3_gnn_adaptW, L3_gnn_gamma, L3_gnn_beta):
    import numpy as _np
    import concourse.bacc as _bacc
    from concourse import mybir as _mybir
    from concourse.bass_utils import run_bass_kernel_spmd as _run

    P = 128
    N, F = x.shape
    E = src.shape[0]
    NB = -(-N // (14 * P)) * 14
    NCH = -(-E // (8 * 512)) * 8
    more_n, more_e = NB * P - N, NCH * 512 - E

    def nodes(a, fill=0):
        a = _np.asarray(a)
        return _np.pad(a, [(0, more_n)] + [(0, 0)] * (a.ndim - 1), constant_values=fill)

    def edges(a, fill=0):
        a = _np.asarray(a)
        return _np.pad(a, [(0, more_e)] + [(0, 0)] * (a.ndim - 1), constant_values=fill)

    def cols(a, fill=0):
        return edges(a, fill).reshape(NCH, P, 4).transpose(1, 0, 2).reshape(P, NCH * 4)

    src_e, dst_e = edges(src, N), edges(dst, N)
    R = edge_attr_40.shape[1]
    arrays = {
        "x": nodes(x).reshape(P, NB, F),
        "src": cols(src, N),
        "dst": cols(dst, N),
        "dst_rows": dst_e.reshape(NCH // 4, 4, 512),
        "src_lines": src_e.reshape(NCH // 4, 4, P, 4).transpose(0, 1, 3, 2).reshape(NCH // 4, 4 * 512),
        "attr48": edges(edge_attr_48).reshape(NCH, P, 4 * F),
        "ea_t": edges(edge_attr_40).reshape(NCH // 4, 4, P, 4, R).transpose(0, 4, 1, 3, 2).reshape(NCH // 4, R, 4 * 512),
        "edge_type": cols(edge_type_8),
        "dist": cols(edge_weight),
        "norm": cols(_np.asarray(edge_weight1).reshape(E)),
        "node_type": nodes(node_type_119).reshape(P, NB),
        "node_vec": nodes(node_vec).reshape(P, NB),
        "eps": _np.asarray(L0_gnn_eps).reshape(1, 1),
        "w1": _np.asarray(L1_gnn_weight1).transpose(1, 0, 2).reshape(F, -1),
        "w2": _np.asarray(L1_gnn_weight2).transpose(1, 0, 2).reshape(F, -1),
        "bias1": _np.asarray(L1_gnn_bias1),
        "bias2": _np.asarray(L1_gnn_bias2).reshape(1, F),
        "cheb": _np.asarray(L2_gnn_weight).transpose(1, 0, 2).reshape(F, -1),
        "cheb_bias": _np.asarray(L2_gnn_bias).reshape(1, F),
        "fw1_t": _np.asarray(L3_gnn_W1).T,
        "fb1": _np.asarray(L3_gnn_b1).reshape(F, 1),
        "fw2_t": _np.asarray(L3_gnn_W2).T,
        "fb2": _np.asarray(L3_gnn_b2).reshape(1, F),
        "emb": _np.asarray(L3_gnn_emb),
        "emb_t": _np.asarray(L3_gnn_emb).T,
        "adapt_t": _np.asarray(L3_gnn_adaptW),
        "gamma": _np.asarray(L3_gnn_gamma).reshape(1, F),
        "beta": _np.asarray(L3_gnn_beta).reshape(1, F),
    }
    nc = _bacc.Bacc("TRN2", target_bir_lowering=False, num_devices=1)
    ins, given = {}, {}
    for name, a in arrays.items():
        a = _np.ascontiguousarray(a)
        if name != "emb":
            given[f"in_{name}"] = a
        ins[name] = nc.dram_tensor(f"in_{name}", a.shape, _mybir.dt.from_np(a.dtype), kind="ExternalInput").ap() \
            if name != "emb" else a
    out = nc.dram_tensor("out_0", [P, NB, F], _mybir.dt.float32, kind="ExternalOutput").ap()
    gnn_program(nc, ins, out)
    r = _run(nc, [given], core_ids=[0])
    return r.results[0]["out_0"].reshape(NB * P, F)[:N]
```

```python
import numpy as np
import concourse.bass as bass
from concourse import mybir
from contextlib import ExitStack


def gnn_program(nc, A, out):
    f32, i32, bf16 = mybir.dt.float32, mybir.dt.int32, mybir.dt.bfloat16
    ALU, ACT, AX = mybir.AluOpType, mybir.ActivationFunctionType, mybir.AxisListType

    P = 128
    F = A["x"].shape[2] if len(A["x"].shape) == 3 else 48
    NB = A["x"].shape[1]
    NP = P * NB
    T = A["src"].shape[1]
    NCH = T // 4
    CPS = 8
    HC = 4
    STEPS = NCH // CPS
    GB = 7
    NG = NB // GB
    WIN = 128
    NR = A["w1"].shape[1] // F
    RP = NR // 2
    ZD, NZ = A["emb_t"].shape
    R = A["fw1_t"].shape[0]
    TW = 52
    NT = 8
    MW = F + 1
    CUTOFF = 6.0
    EPS = 1e-5
    CG = A["dst_rows"].shape[0]

    def dram(name, shape, dt=f32):
        return nc.dram_tensor(name, shape, dt, kind="Internal").ap()

    table_l0 = dram("table_l0", [NP, TW])
    table_l1 = dram("table_l1", [NP * NR, F])
    table_l2 = dram("table_l2", [NP, F])
    table_l3 = dram("table_l3", [NP + WIN, 3 * MW], bf16)
    pair_rows = dram("pair_rows", [NP + WIN, NZ])
    sum_rows = dram("sum_rows", [P, T], i32)
    src_rel = dram("src_rel", [P, T], i32)
    base_row = dram("base_row", [1, NCH])
    base_row_int = dram("base_row_int", [1, NCH], i32)
    span_row = dram("span_row", [1, NCH])
    sums = [dram(f"sum{k}", [NP + P, MW]) for k in range(NT)]

    top = ExitStack()
    with top:
        phase = [0]

        def sb(ctx, name, shape, dt=f32):
            return ctx.enter_context(nc.sbuf_tensor(f"{name}_p{phase[0]}", shape, dt))

        def ps(ctx, name, shape=None, dt=f32):
            return ctx.enter_context(nc.psum_tensor(f"{name}_p{phase[0]}", shape or [P, 512], dt))

        used = []

        def sem(ctx, name):
            s = ctx.enter_context(nc.semaphore(f"{name}_p{phase[0]}"))
            used.append(s)
            return s

        slot_gathered = [top.enter_context(nc.semaphore(f"slot_gathered{c}")) for c in range(8)]
        slot_scattered = [top.enter_context(nc.semaphore(f"slot_scattered{k}")) for k in range(2)]
        gathered_so_far = [0]

        def steps_from_first(eng, count, body):
            body(0, True)
            if count > 1:
                with eng.Fori(1, count) as s:
                    body(s, False)

        def clear_used():
            numbers = list(used)
            used.clear()
            phase[0] += 1

            with nc.Block() as block:
                @block.sync
                def _(sp):
                    for s in numbers:
                        sp.sem_clear(s)

        x_nodes = sb(top, "x_nodes", [P, NB, F])
        h_nodes = sb(top, "h_nodes", [P, NB, F])
        w_nodes = sb(top, "w_nodes", [P, NB, TW])
        src_type = sb(top, "src_type", [P, T])
        src_cols = sb(top, "src_cols", [P, T], i32)
        window_part = sb(top, "window_part", [P, NCH])
        logit_all = sb(top, "logit_all", [P, T])
        base_int = sb(top, "base_int", [1, NCH], i32)
        spare = sb(top, "spare", [P, 1])
        iota = sb(top, "iota", [P, P])
        part = sb(top, "part", [P, 1])
        ident = sb(top, "ident", [P, P])
        earlier = sb(top, "earlier", [P, P])
        eps_col = sb(top, "eps_col", [P, 1])
        stat = sb(top, "stat", [P, NB])
        stat2 = sb(top, "stat2", [P, NB])

        def layer_norm_relu(relu=True):
            with ExitStack() as ctx:
                step = sem(ctx, "ln_step")
                root = sem(ctx, "ln_root")
                with nc.Block() as block:
                    @block.vector
                    def _(dve):
                        dve.tensor_reduce(stat[:, :], x_nodes[:, :, :], AX.X, ALU.add).then_inc(step, 1)
                        dve.wait_ge(step, 1)
                        dve.tensor_scalar(stat[:, :], stat[:, :], -1.0 / F, None, ALU.mult).then_inc(step, 1)
                        dve.wait_ge(step, 2)
                        dve.tensor_tensor(h_nodes[:, :, :], x_nodes[:, :, :],
                                          stat[:, :].unsqueeze(2).broadcast_to([P, NB, F]), ALU.add).then_inc(step, 1)
                        dve.wait_ge(step, 3)
                        dve.tensor_tensor(w_nodes[:, :, 0:F], h_nodes[:, :, :], h_nodes[:, :, :],
                                          ALU.mult).then_inc(step, 1)
                        dve.wait_ge(step, 4)
                        dve.tensor_reduce(stat2[:, :], w_nodes[:, :, 0:F], AX.X, ALU.add).then_inc(step, 1)
                        dve.wait_ge(root, 1)
                        dve.reciprocal(stat2[:, :], stat2[:, :]).then_inc(step, 1)
                        dve.wait_ge(step, 6)
                        dve.tensor_tensor(h_nodes[:, :, :], h_nodes[:, :, :],
                                          stat2[:, :].unsqueeze(2).broadcast_to([P, NB, F]), ALU.mult).then_inc(step, 1)
                        dve.wait_ge(step, 7)
                        dve.tensor_scalar(h_nodes[:, :, :], h_nodes[:, :, :], 0.0, None, ALU.max).then_inc(step, 1)

                    @block.scalar
                    def _(act):
                        act.wait_ge(step, 5)
                        act.activation(stat2[:, :], stat2[:, :], ACT.Sqrt, bias=eps_col[:, 0:1],
                                       scale=1.0 / F).then_inc(root, 1)
            clear_used()

        agg = ExitStack()
        top.enter_context(agg)
        accT = sb(agg, "accT", [F, NP + WIN])
        rel_col = sb(agg, "rel_col", [P, T])
        norm_col = sb(agg, "norm_col", [P, T])
        other_end = sb(agg, "other_end", [P, T])
        span_max = sb(agg, "span_max", [1, 1], i32)
        degree = sb(agg, "degree", [P, NB])
        only_l0 = ExitStack()
        agg.enter_context(only_l0)
        src_hi = sb(only_l0, "src_hi", [P, T])
        src_lo = sb(only_l0, "src_lo", [P, T])

        with ExitStack() as ctx:
            dst_cols = sb(ctx, "dst_cols", [P, T], i32)
            type_int = sb(ctx, "type_int", [P, NB], i32)
            rel_type = sb(ctx, "rel_type", [P, T], i32)
            src_part = sb(ctx, "src_part", [P, T], i32)
            rows = sb(ctx, "rows", [CG, 4, 512], i32)
            base_b = sb(ctx, "base_b", [P, NCH])
            lowest = sb(ctx, "lowest", [CG, 4])
            lowest_int = sb(ctx, "lowest_int", [CG, 4], i32)
            highest = sb(ctx, "highest", [CG, 4])
            span = sb(ctx, "span", [1, NCH])
            loaded = {k: sem(ctx, "ld_" + k) for k in ("x", "src", "dst", "rows", "norm", "rel", "type", "base", "idx")}
            made = sem(ctx, "made")
            step = sem(ctx, "prep_step")
            stored = sem(ctx, "prep_stored")
            with nc.Block() as block:
                @block.gpsimd
                def _(pool):
                    pool.iota(iota[:, :], pattern=[[1, P]], base=0, channel_multiplier=0,
                              allow_small_or_imprecise_dtypes=True).then_inc(made, 1)
                    pool.iota(part[:, :], pattern=[[0, 1]], base=0, channel_multiplier=1,
                              allow_small_or_imprecise_dtypes=True).then_inc(made, 1)
                    pool.memset(eps_col[:, :], EPS).then_inc(made, 1)
                    pool.memset(w_nodes[:, :, :], 0.0).then_inc(made, 1)
                    pool.memset(accT[:, :], 0.0).then_inc(made, 1)
                    pool.iota(spare[:, :], pattern=[[0, 1]], base=NP, channel_multiplier=1,
                              allow_small_or_imprecise_dtypes=True)

                @block.sync
                def _(sp):
                    sp.dma_start(rows[:, :, :], A["dst_rows"]).then_inc(loaded["rows"], 16)
                    sp.dma_start(x_nodes[:, :, :], A["x"]).then_inc(loaded["x"], 16)
                    sp.dma_start(dst_cols[:, :], A["dst"]).then_inc(loaded["dst"], 16)
                    sp.wait_ge(step, 3)
                    sp.dma_start(base_row.rearrange("a (p q) -> (a p) q", q=4), lowest[:, :]).then_inc(stored, 16)
                    sp.dma_start(base_row_int.rearrange("a (p q) -> (a p) q", q=4), lowest_int[:, :]).then_inc(stored, 16)
                    sp.dma_start(span_row.rearrange("a (p q) -> (a p) q", q=4), highest[:, :]).then_inc(stored, 16)
                    sp.wait_ge(stored, 48)
                    sp.dma_start(base_b[:, :], base_row.broadcast_to([P, NCH])).then_inc(loaded["base"], 16)
                    sp.dma_start(span[:, :], span_row).then_inc(loaded["base"], 16)
                    sp.dma_start(base_int[:, :], base_row_int).then_inc(loaded["base"], 16)
                    sp.wait_ge(step, 8)
                    sp.dma_start(src_rel, rel_type[:, :]).then_inc(loaded["idx"], 16)
                    sp.wait_ge(loaded["idx"], 16)

                @block.scalar
                def _(act):
                    act.dma_start(src_cols[:, :], A["src"]).then_inc(loaded["src"], 16)
                    act.dma_start(rel_type[:, :], A["edge_type"]).then_inc(loaded["rel"], 16)
                    act.dma_start(norm_col[:, :], A["norm"]).then_inc(loaded["norm"], 16)
                    act.dma_start(type_int[:, :], A["node_type"]).then_inc(loaded["type"], 16)
                    act.wait_ge(loaded["norm"], 16)

                @block.vector
                def _(dve):
                    dve.wait_ge(loaded["rows"], 16)
                    dve.tensor_reduce(lowest[:, :], rows[:, :, :], AX.X, ALU.min).then_inc(step, 1)
                    dve.tensor_reduce(highest[:, :], rows[:, :, :], AX.X, ALU.max)
                    dve.wait_ge(step, 1)
                    dve.tensor_copy(lowest_int[:, :], lowest[:, :]).then_inc(step, 1)
                    dve.drain()
                    dve.tensor_tensor(highest[:, :], highest[:, :], lowest[:, :], ALU.subtract).then_inc(step, 1)
                    dve.wait_ge(loaded["src"], 16)
                    dve.wait_ge(loaded["dst"], 16)
                    dve.tensor_tensor(other_end[:, :], src_cols[:, :], dst_cols[:, :], ALU.not_equal).then_inc(step, 1)
                    dve.tensor_single_scalar(src_part[:, :], src_cols[:, :], 7,
                                             op=ALU.logical_shift_right).then_inc(step, 1)
                    dve.wait_ge(step, 5)
                    dve.tensor_copy(src_hi[:, :], src_part[:, :]).then_inc(step, 1)
                    dve.wait_ge(step, 6)
                    dve.tensor_single_scalar(src_part[:, :], src_cols[:, :], P - 1, op=ALU.bitwise_and).then_inc(step, 1)
                    dve.wait_ge(loaded["rel"], 16)
                    dve.scalar_tensor_tensor(out=rel_type[:, :], in0=src_cols[:, :], scalar=float(NR),
                                             in1=rel_type[:, :], op0=ALU.mult, op1=ALU.add).then_inc(step, 1)
                    dve.wait_ge(step, 7)
                    dve.tensor_copy(src_lo[:, :], src_part[:, :]).then_inc(step, 1)
                    dve.wait_ge(loaded["base"], 48)
                    dve.tensor_tensor(rel_col[:, :].rearrange("p (g j) -> p g j", j=4),
                                      dst_cols[:, :].rearrange("p (g j) -> p g j", j=4),
                                      base_b[:, :].unsqueeze(2).broadcast_to([P, NCH, 4]), ALU.subtract).then_inc(step, 1)
                    dve.tensor_reduce(span_max[:, :], span[:, :], AX.X, ALU.max).then_inc(step, 1)
                    dve.wait_ge(made, 5)
                    dve.tensor_scalar(ident[:, :], iota[:, :], part[:, 0:1], None, ALU.is_equal).then_inc(step, 1)
                    dve.tensor_scalar(earlier[:, :], iota[:, :], part[:, 0:1], None, ALU.is_lt).then_inc(step, 1)
                    dve.tensor_scalar(window_part[:, :], base_b[:, :], part[:, 0:1], None, ALU.add).then_inc(step, 1)
                    dve.wait_ge(loaded["type"], 16)
                    dve.tensor_copy(w_nodes[:, :, F], type_int[:, :]).then_inc(step, 1)
                    dve.wait_ge(loaded["x"], 16)
            clear_used()

        ET = mybir.EngineType
        residual = nc.values_load(span_max[0:1, 0:1], engines=[ET.Pool, ET.Activation, ET.PE, ET.DVE, ET.SP],
                                  min_val=0, max_val=NP)

        def store_table(table, width, fill):
            with ExitStack() as ctx:
                step = sem(ctx, "fill_step")
                stored = sem(ctx, "table_stored")
                with nc.Block() as block:
                    steps = []

                    @block.vector
                    def _(dve):
                        steps.append(fill(dve, step))

                    @block.sync
                    def _(sp):
                        sp.wait_ge(step, steps[0])
                        rows_of = table.rearrange("(p b) f -> p b f", b=NB)
                        sp.dma_start(rows_of, w_nodes[:, :, 0:width]).then_inc(stored, 16)
                        sp.wait_ge(stored, 16)
            clear_used()

        def edge_pass(layer, table, width, index_dram, scale_col, rows_too=False, logits_too=False):
            LS = 4
            l0 = layer == 0
            OH, PB = 4, 4
            old = gathered_so_far[0]
            with ExitStack() as ctx:
                index = [sb(ctx, f"index{h}", [P, HC * 4], i32) for h in range(2)]
                gathered = [sb(ctx, f"gathered{c}", [P, 4, width]) for c in range(CPS)]
                onehot = [sb(ctx, f"onehot{k}", [P, 4, WIN]) for k in range(OH)]
                chunk_sum = [ps(ctx, f"chunk_sum{k}") for k in range(PB)]
                index_loaded = [sem(ctx, f"index_loaded{h}") for h in range(2)]
                rows_gathered = slot_gathered
                onehot_ready = sem(ctx, "onehot_ready")
                chunk_started = sem(ctx, "chunk_started")
                sum_ready = sem(ctx, "sum_ready")
                sum_added = sem(ctx, "sum_added")
                if rows_too or logits_too:
                    line = [sb(ctx, f"line{k}", [P, 512], i32) for k in range(LS)]
                    line_loaded = [sem(ctx, f"line_loaded{k}") for k in range(LS)]
                    line_used = sem(ctx, "line_used")
                    beside_step = sem(ctx, "beside_step")
                    junk = sb(ctx, "junk", [P, 4, P])
                if rows_too:
                    before = sb(ctx, "before", [P, 4])
                    to_row = sb(ctx, "to_row", [P, T], i32)
                    rows_stored = sem(ctx, "rows_stored")
                if logits_too:
                    window = [sb(ctx, f"window{k}", [WIN, NZ]) for k in range(LS)]
                    window_loaded = [sem(ctx, f"window_loaded{k}") for k in range(LS)]
                    turned_hot = [sb(ctx, f"turned_hot{k}", [WIN, 512]) for k in range(2)]
                    turned_ready = sem(ctx, "turned_ready")
                    pairs = [ps(ctx, f"pairs{k}") for k in range(2)]
                    pairs_ready = sem(ctx, "pairs_ready")
                if l0:
                    attr = [sb(ctx, f"attr{h}", [P, HC, 4 * F]) for h in range(2)]
                    attr_loaded = [sem(ctx, f"attr_loaded{h}") for h in range(2)]
                    attr_added = sem(ctx, "attr_added")
                    type_kept = sem(ctx, "type_kept")
                    relu_done = sem(ctx, "relu_done")
                    cell_hi = [sb(ctx, f"cell_hi{k}", [P, 4, P], bf16) for k in range(2)]
                    cell_lo = [sb(ctx, f"cell_lo{k}", [P, 4, P], bf16) for k in range(2)]
                    cells_ready = sem(ctx, "cells_ready")
                    cells_counted = sem(ctx, "cells_counted")
                    histogram = ps(ctx, "histogram")
                    counts = sb(ctx, "counts", [P, P])
                    zero_cells = sb(ctx, "zero_cells", [P, P], bf16)
                    zeroed = sem(ctx, "zeroed")
                    count_copied = sem(ctx, "count_copied")
                    degree_dram = dram("degree_dram", [NP])
                    degree_moved = sem(ctx, "degree_moved")
                with nc.Block() as block:
                    @block.sync
                    def _(sp):
                        with sp.Fori(0, STEPS) as s:
                            for h in range(2):
                                sp.wait_ge(sum_ready, s * CPS + HC * (h + 1))
                                sp.dma_start(index[h][:, :], index_dram[:, bass.ds((s * 2 + h) * (HC * 4), HC * 4)]
                                             ).then_inc(index_loaded[h], 16)
                                if l0:
                                    sp.wait_ge(attr_added, s * CPS + HC * (h + 1))
                                    sp.dma_start(attr[h][:, :, :],
                                                 A["attr48"][bass.ds((s * 2 + h) * HC, HC), :, :]
                                                 .rearrange("c p f -> p c f")).then_inc(attr_loaded[h], 16)
                                for c in range(HC * h, HC * (h + 1)):
                                    q = s * CPS + c
                                    if rows_too or logits_too:
                                        sp.wait_ge(line_used, q + 1)
                                        sp.dma_start(line[c % LS][:, :],
                                                     A["src_lines" if rows_too else "dst_lines"][bass.ds(q, 1), :]
                                                     .broadcast_to([P, 512])).then_inc(line_loaded[c % LS], 16)
                                    if logits_too:
                                        base = sp.value_load(base_int[0:1, bass.ds(q, 1)], min_val=0, max_val=NP)
                                        sp.wait_ge(pairs_ready, q + 1)
                                        sp.dma_start(window[c % LS][:, :], pair_rows[bass.ds(base, WIN), :]
                                                     ).then_inc(window_loaded[c % LS], 16)
                        if rows_too:
                            sp.wait_ge(beside_step, NCH * 3)
                            sp.dma_start(sum_rows, to_row[:, :]).then_inc(rows_stored, 16)
                            sp.wait_ge(rows_stored, 16)
                        if l0:
                            sp.wait_ge(count_copied, 1)
                            sp.dma_start(degree_dram.rearrange("(a b) -> a b", b=P), counts[0:NB, :]
                                         ).then_inc(degree_moved, 16)
                            sp.wait_ge(degree_moved, 16)
                            sp.dma_start(degree[:, :], degree_dram.rearrange("(p b) -> p b", b=NB)
                                         ).then_inc(degree_moved, 16)
                            sp.wait_ge(degree_moved, 32)

                    @block.gpsimd
                    def _(pool):
                        if l0:
                            pool.memset(zero_cells[:, :], 0.0).then_inc(zeroed, 1)
                        with pool.Fori(0, STEPS) as s:
                            for c in range(CPS):
                                if c % HC == 0:
                                    pool.wait_ge(index_loaded[c // HC], s * 16 + 16)
                                pool.wait_ge(sum_ready, s * CPS + c + 1)
                                if l0:
                                    pool.wait_ge(type_kept, s * CPS + c + 1)
                                pool.sem_inc(chunk_started, 1)
                                for j in range(4):
                                    t = (c % HC) * 4 + j
                                    pool.indirect_dma_start(
                                        gathered[c][:, j, :], None, table,
                                        bass.IndirectOffsetOnAxis(ap=index[c // HC][:, t:t + 1], axis=0),
                                    ).then_inc(rows_gathered[c], 16)

                    @block.tensor
                    def _(pe):
                        pe.sem_inc(sum_ready, CPS)
                        if logits_too:
                            pe.sem_inc(pairs_ready, LS)
                        if l0:
                            pe.sem_inc(cells_counted, 2)
                            pe.wait_ge(zeroed, 1)
                            pe.matmul(histogram[:, 0:P], zero_cells[:, :], zero_cells[:, :], start=True, stop=False)
                        with pe.Fori(0, STEPS) as s:
                            for c in range(CPS):
                                q = s * CPS + c
                                if l0:
                                    pe.wait_ge(cells_ready, q + 1)
                                    for j in range(4):
                                        mm = pe.matmul(histogram[:, 0:P], cell_hi[c % 2][:, j, :],
                                                       cell_lo[c % 2][:, j, :], start=False, stop=False,
                                                       skip_group_check=True)
                                    mm.then_inc(cells_counted, 1)
                                pe.wait_ge(onehot_ready, q + 1)
                                if l0:
                                    pe.wait_ge(relu_done, q + 1)
                                else:
                                    pe.wait_ge(rows_gathered[c], s * 64 + 64 + old)
                                pe.wait_ge(sum_added, q + 1)
                                for j in range(4):
                                    mm = pe.matmul(chunk_sum[c % PB][0:F, 0:WIN], gathered[c][:, j, 0:F],
                                                   onehot[c % OH][:, j, :], start=(j == 0), stop=(j == 3))
                                mm.then_inc(sum_ready, 1)
                                if logits_too:
                                    pe.wait_ge(turned_ready, q + 1)
                                    pe.wait_ge(window_loaded[c % LS], s * 32 + (c // LS) * 16 + 16)
                                    pe.wait_ge(beside_step, q + 1)
                                    for j in range(4):
                                        mm = pe.matmul(pairs[c % 2][:, j * NZ:(j + 1) * NZ],
                                                       turned_hot[c % 2][:, j * P:(j + 1) * P], window[c % LS][:, :],
                                                       start=True, stop=True)
                                    mm.then_inc(pairs_ready, 1)
                        if l0:
                            pe.matmul(histogram[:, 0:P], zero_cells[:, :], zero_cells[:, :], start=False,
                                      stop=True).then_inc(cells_counted, 1)

                    @block.vector
                    def _(dve):
                        dve.sem_inc(sum_added, PB)
                        if l0:
                            dve.sem_inc(attr_added, CPS)

                        def add_sum(s, c):
                            base = dve.value_load(base_int[0:1, bass.ds(s * CPS + c, 1)], min_val=0, max_val=NP)
                            dve.wait_ge(sum_ready, s * CPS + c + 1 + CPS)
                            dve.wait_ge(sum_added, s * CPS + c + PB)
                            dve.tensor_tensor(accT[:, bass.ds(base, WIN)], accT[:, bass.ds(base, WIN)],
                                              chunk_sum[c % PB][0:F, 0:WIN], ALU.add).then_inc(sum_added, 1)

                        def rows_of(s, c):
                            q = s * CPS + c
                            dve.wait_ge(line_loaded[c % LS], s * 32 + (c // LS) * 16 + 16)
                            for j in range(4):
                                got = dve.scalar_tensor_tensor(out=junk[:, j, :], in0=line[c % LS][:, j * P:(j + 1) * P],
                                                               scalar=src_cols[:, bass.ds(q * 4 + j, 1)],
                                                               in1=earlier[:, :], op0=ALU.is_equal, op1=ALU.mult,
                                                               accum_out=before[:, j:j + 1])
                            got.then_inc(beside_step, 1)
                            dve.wait_ge(beside_step, q * 3 + 1)
                            dve.sem_inc(line_used, 1)
                            dve.tensor_scalar(before[:, :], before[:, :], float(2 * NP), spare[:, 0:1],
                                              ALU.mult, ALU.min).then_inc(beside_step, 1)
                            dve.wait_ge(beside_step, q * 3 + 2)
                            dve.tensor_tensor(to_row[:, bass.ds(q * 4, 4)], before[:, :], src_cols[:, bass.ds(q * 4, 4)],
                                              ALU.max).then_inc(beside_step, 1)
                            dve.wait_ge(beside_step, q * 3 + 3)

                        def turned_onehot(s, c):
                            q = s * CPS + c
                            dve.wait_ge(line_loaded[c % LS], s * 32 + (c // LS) * 16 + 16)
                            dve.wait_ge(pairs_ready, q + 1 + LS - 2)
                            dve.tensor_scalar(turned_hot[c % 2][:, :], line[c % LS][:, :],
                                              window_part[:, bass.ds(q, 1)], None, ALU.is_equal).then_inc(turned_ready, 1)

                        def logits_of(s, c):
                            q = s * CPS + c
                            dve.wait_ge(pairs_ready, q + 1 + LS)
                            dve.wait_ge(beside_step, q + 2)
                            dve.sem_inc(line_used, 1)
                            for j in range(4):
                                got = dve.scalar_tensor_tensor(out=junk[:, j, 0:NZ], in0=iota[:, 0:NZ],
                                                               scalar=src_type[:, bass.ds(q * 4 + j, 1)],
                                                               in1=pairs[c % 2][:, j * NZ:(j + 1) * NZ],
                                                               op0=ALU.is_equal, op1=ALU.mult,
                                                               accum_out=logit_all[:, bass.ds(q * 4 + j, 1)])
                            got.then_inc(beside_step, 1)

                        if rows_too or logits_too:
                            dve.sem_inc(line_used, LS)
                        if logits_too:
                            dve.sem_inc(beside_step, 2)

                        def step_of(s):
                            for c in range(CPS):
                                q = s * CPS + c
                                dve.wait_ge(sum_ready, q + 1 + CPS - OH)
                                for j in range(4):
                                    t = q * 4 + j
                                    if scale_col is None:
                                        oh = dve.tensor_scalar(onehot[c % OH][:, j, :], iota[:, :],
                                                               rel_col[:, bass.ds(t, 1)], None, ALU.is_equal)
                                    else:
                                        oh = dve.tensor_scalar(onehot[c % OH][:, j, :], iota[:, :],
                                                               rel_col[:, bass.ds(t, 1)],
                                                               scale_col[:, bass.ds(t, 1)], ALU.is_equal, ALU.mult)
                                oh.then_inc(onehot_ready, 1)
                                if l0:
                                    dve.wait_ge(cells_counted, q + 1)
                                    for j in range(4):
                                        t = q * 4 + j
                                        dve.tensor_scalar(cell_hi[c % 2][:, j, :], iota[:, :],
                                                          src_hi[:, bass.ds(t, 1)], None, ALU.is_equal)
                                        oh = dve.tensor_scalar(cell_lo[c % 2][:, j, :], iota[:, :],
                                                               src_lo[:, bass.ds(t, 1)],
                                                               other_end[:, bass.ds(t, 1)], ALU.is_equal, ALU.mult)
                                    oh.then_inc(cells_ready, 1)
                                    dve.wait_ge(attr_loaded[c // HC], s * 16 + 16)
                                    dve.wait_ge(rows_gathered[c], s * 64 + 64 + old)
                                    dve.wait_ge(type_kept, q + 1)
                                    dve.tensor_tensor(gathered[c][:, :, 0:F], gathered[c][:, :, 0:F],
                                                      attr[c // HC][:, c % HC, :].rearrange("p (j f) -> p j f", f=F),
                                                      ALU.add).then_inc(attr_added, 1)
                                if rows_too:
                                    rows_of(s, c)
                                if logits_too:
                                    turned_onehot(s, c)
                                if c >= 1:
                                    add_sum(s, c - 1)
                                    if logits_too:
                                        logits_of(s, c - 1)
                            add_sum(s, CPS - 1)
                            if logits_too:
                                logits_of(s, CPS - 1)

                        with dve.Fori(0, STEPS) as s:
                            step_of(s)
                        if l0:
                            dve.wait_ge(cells_counted, NCH + 3)
                            dve.tensor_copy(counts[:, :], histogram[:, 0:P]).then_inc(count_copied, 1)

                    if l0:
                        @block.scalar
                        def _(act):
                            act.sem_inc(type_kept, CPS)
                            with act.Fori(0, STEPS) as s:
                                for c in range(CPS):
                                    q = s * CPS + c
                                    act.wait_ge(rows_gathered[c], s * 64 + 64 + old)
                                    act.activation(src_type[:, bass.ds(q * 4, 4)], gathered[c][:, :, F],
                                                   ACT.Copy).then_inc(type_kept, 1)
                                    act.wait_ge(attr_added, q + 1 + CPS)
                                    act.activation(gathered[c][:, :, 0:F], gathered[c][:, :, 0:F],
                                                   ACT.Relu).then_inc(relu_done, 1)
            clear_used()
            gathered_so_far[0] += STEPS * 64
            residual_pass(layer, table, width, index_dram, scale_col)

        def residual_pass(layer, table, width, index_dram, scale_col):
            with nc.If(residual > WIN - 1):
                with ExitStack() as ctx:
                    index = sb(ctx, "res_index", [P, 4], i32)
                    rows = sb(ctx, "res_rows", [P, 4, width])
                    attr = sb(ctx, "res_attr", [P, 4 * F])
                    dst_now = sb(ctx, "res_dst", [P, 4], i32)
                    place = sb(ctx, "res_place", [P, 4])
                    beyond = sb(ctx, "res_beyond", [P, 4])
                    onehot = sb(ctx, "res_onehot", [P, 4, WIN])
                    window_sum = ps(ctx, "res_window_sum")
                    loaded = sem(ctx, "res_loaded")
                    idle = sem(ctx, "res_idle")
                    gathered = top.enter_context(nc.semaphore(f"res_gathered_p{phase[0]}"))
                    chunk_started = sem(ctx, "res_chunk_started")
                    step = sem(ctx, "res_step")
                    placed = sem(ctx, "res_placed")
                    summed = sem(ctx, "res_summed")
                    added = sem(ctx, "res_added")
                    HEAD = 5
                    with nc.Block() as block:
                        @block.sync
                        def _(sp):
                            with sp.Fori(0, NCH) as g:
                                sp.wait_ge(added, g * NB + 1)
                                sp.dma_start(index[:, :], index_dram[:, bass.ds(g * 4, 4)]).then_inc(loaded, 16)
                                sp.dma_start(attr[:, :].unsqueeze(1), A["attr48"][bass.ds(g, 1), :, :]
                                             .rearrange("c p f -> p c f")).then_inc(loaded, 16)
                                sp.dma_start(dst_now[:, :], A["dst"][:, bass.ds(g * 4, 4)]).then_inc(loaded, 16)

                        @block.scalar
                        def _(act):
                            act.sem_inc(idle, 1)

                        @block.gpsimd
                        def _(pool):
                            with pool.Fori(0, NCH) as g:
                                pool.wait_ge(loaded, g * 48 + 48)
                                pool.sem_inc(chunk_started, 1)
                                for j in range(4):
                                    pool.indirect_dma_start(
                                        rows[:, j, :], None, table,
                                        bass.IndirectOffsetOnAxis(ap=index[:, j:j + 1], axis=0)).then_inc(gathered, 16)

                        @block.vector
                        def _(dve):
                            dve.sem_inc(added, 1)
                            with dve.Fori(0, NCH) as g:
                                cols = slice(None), bass.ds(g * 4, 4)
                                dve.tensor_scalar(beyond[:, :], rel_col[cols], float(WIN), None,
                                                  ALU.is_ge).then_inc(step, 1)
                                dve.wait_ge(step, g * HEAD + 1)
                                dve.wait_ge(loaded, g * 48 + 48)
                                dve.scalar_tensor_tensor(out=place[:, :], in0=dst_now[:, :], scalar=1.0,
                                                         in1=beyond[:, :], op0=ALU.add, op1=ALU.mult).then_inc(step, 1)
                                dve.wait_ge(step, g * HEAD + 2)
                                dve.tensor_scalar(place[:, :], place[:, :], -1.0, None, ALU.add).then_inc(step, 1)
                                dve.wait_ge(gathered, g * 64 + 64)
                                if layer == 0:
                                    dve.tensor_tensor(rows[:, :, 0:F], rows[:, :, 0:F],
                                                      attr[:, :].rearrange("p (j f) -> p j f", f=F),
                                                      ALU.add).then_inc(step, 1)
                                    dve.wait_ge(step, g * HEAD + 4)
                                    dve.tensor_scalar(rows[:, :, 0:F], rows[:, :, 0:F], 0.0, None,
                                                      ALU.max).then_inc(step, 1)
                                else:
                                    dve.tensor_copy(beyond[:, :], beyond[:, :]).then_inc(step, 2)
                                with dve.Fori(0, NB) as k:
                                    dve.wait_ge(step, g * HEAD + HEAD)
                                    for j in range(4):
                                        scale = None if scale_col is None else scale_col[:, bass.ds(g * 4 + j, 1)]
                                        if scale is None:
                                            oh = dve.tensor_scalar(onehot[:, j, :], iota[:, :], place[:, j:j + 1],
                                                                   None, ALU.is_equal)
                                        else:
                                            oh = dve.tensor_scalar(onehot[:, j, :], iota[:, :], place[:, j:j + 1],
                                                                   scale, ALU.is_equal, ALU.mult)
                                    oh.then_inc(placed, 1)
                                    dve.wait_ge(placed, (g * NB + k) * 2 + 1)
                                    dve.tensor_scalar(place[:, :], place[:, :], -float(WIN), None,
                                                      ALU.add).then_inc(placed, 1)
                                    dve.wait_ge(placed, (g * NB + k) * 2 + 2)
                                    dve.wait_ge(summed, g * NB + k + 1)
                                    dve.tensor_tensor(accT[:, bass.ds(k * WIN, WIN)], accT[:, bass.ds(k * WIN, WIN)],
                                                      window_sum[0:F, 0:WIN], ALU.add).then_inc(added, 1)

                        @block.tensor
                        def _(pe):
                            with pe.Fori(0, NCH) as g:
                                with pe.Fori(0, NB) as k:
                                    pe.wait_ge(step, g * HEAD + HEAD)
                                    pe.wait_ge(placed, (g * NB + k) * 2 + 1)
                                    pe.wait_ge(added, g * NB + k + 1)
                                    for j in range(4):
                                        mm = pe.matmul(window_sum[0:F, 0:WIN], rows[:, j, 0:F], onehot[:, j, :],
                                                       start=(j == 0), stop=(j == 3))
                                    mm.then_inc(summed, 1)
                clear_used()

        def node_update(per_group, weight=None, n_dve=1):
            by_block = accT[:, 0:NP].rearrange("f (p b) -> f b p", b=NB)
            with ExitStack() as ctx:
                staged = [sb(ctx, f"staged{k}", [F, GB, P]) for k in range(2)]
                tmp = [sb(ctx, f"update_tmp{k}", [P, GB, F]) for k in range(2)]
                turned = [ps(ctx, f"turned{k}", [P, GB, F]) for k in range(2)]
                product = [ps(ctx, f"product{k}", [P, GB, F]) for k in range(2)]
                staged_ready = sem(ctx, "staged_ready")
                turned_ready = sem(ctx, "turned_ready")
                step = sem(ctx, "update_step")
                with nc.Block() as block:
                    @block.scalar
                    def _(act):
                        with act.Fori(0, NG // 2) as s:
                            for k in range(2):
                                act.wait_ge(turned_ready, s * 2 + k + 1)
                                act.activation(staged[k][:, :, :], by_block[:, bass.ds((s * 2 + k) * GB, GB), :],
                                               ACT.Copy).then_inc(staged_ready, 1)

                    @block.tensor
                    def _(pe):
                        pe.sem_inc(turned_ready, 2)
                        with pe.Fori(0, NG // 2) as s:
                            for k in range(2):
                                pe.wait_ge(staged_ready, s * 2 + k + 1)
                                pe.wait_ge(step, (s * 2 + k + 1) * n_dve)
                                for j in range(GB):
                                    mm = pe.matmul(turned[k][:, j, :], staged[k][:, j, :], ident[0:F, 0:F],
                                                   start=True, stop=True)
                                    if weight is not None:
                                        mm = pe.matmul(product[k][:, j, :], staged[k][:, j, :], weight,
                                                       start=True, stop=True)
                                mm.then_inc(turned_ready, 1)

                    @block.vector
                    def _(dve):
                        dve.sem_inc(step, 2 * n_dve)
                        with dve.Fori(0, NG // 2) as s:
                            for k in range(2):
                                dve.wait_ge(turned_ready, s * 2 + k + 1 + 2)
                                per_group(dve, (s * 2 + k) * GB, turned[k], product[k], tmp[k], step,
                                          (s * 2 + k + 2) * n_dve)
            clear_used()

        def clear_accT():
            with ExitStack() as ctx:
                cleared = sem(ctx, "acc_cleared")
                with nc.Block() as block:
                    @block.vector
                    def _(dve):
                        dve.memset(accT[:, :], 0.0).then_inc(cleared, 1)
                        dve.wait_ge(cleared, 1)
            clear_used()

        def group(tile, b0):
            return tile[:, bass.ds(b0, GB), 0:F]

        def per_node(col, b0):
            return col[:, bass.ds(b0, GB)].unsqueeze(2).broadcast_to([P, GB, F])

        layer_norm_relu()

        def fill_h(dve, step):
            dve.tensor_copy(w_nodes[:, :, 0:F], h_nodes[:, :, :]).then_inc(step, 1)
            return 1

        store_table(table_l0, TW, fill_h)
        edge_pass(0, table_l0, TW, A["src"], None)
        only_l0.close()

        def update_l0(dve, b0, turned, product, tmp, step, n):
            dve.tensor_tensor(group(x_nodes, b0), group(x_nodes, b0), turned[:, :, :], ALU.add).then_inc(step, 1)

        node_update(update_l0)

        with ExitStack() as ctx:
            one_eps = sb(ctx, "one_eps", [P, 1])
            got = sem(ctx, "eps_loaded")
            step = sem(ctx, "eps_step")
            with nc.Block() as block:
                @block.sync
                def _(sp):
                    sp.dma_start(one_eps[:, :], A["eps"].broadcast_to([P, 1])).then_inc(got, 16)

                @block.vector
                def _(dve):
                    dve.wait_ge(got, 16)
                    dve.tensor_scalar(one_eps[:, :], one_eps[:, :], 1.0, None, ALU.add).then_inc(step, 1)
                    dve.wait_ge(step, 1)
                    dve.scalar_tensor_tensor(out=x_nodes[:, :, :], in0=h_nodes[:, :, :], scalar=one_eps[:, 0:1],
                                             in1=x_nodes[:, :, :], op0=ALU.mult, op1=ALU.add).then_inc(step, 1)
        clear_used()

        layer_norm_relu()
        with ExitStack() as ctx:
            w1 = sb(ctx, "w1", [F, RP, 2 * F])
            w2 = sb(ctx, "w2", [2 * F, RP, 2 * F])
            bias1 = sb(ctx, "bias1", [2 * F, 1])
            h_stage = sb(ctx, "h_stage", [P, GB, F])
            hT = sb(ctx, "hT", [F, GB * P])
            h1T = sb(ctx, "h1T", [2 * F, RP, GB * P])
            rows = sb(ctx, "rel_rows", [P, GB, NR * F])
            hT_ps = ps(ctx, "hT_ps", [P, 1024])
            h1_ps = [ps(ctx, f"h1_ps{k}") for k in range(2)]
            h2_ps = [ps(ctx, f"h2_ps{k}") for k in range(2)]
            HALF = GB * P // 2
            weights = sem(ctx, "weights")
            zeroed = sem(ctx, "w2_zeroed")
            h_staged = sem(ctx, "h_staged")
            turned = sem(ctx, "h_turned")
            hT_ready = sem(ctx, "hT_ready")
            h1_ready = sem(ctx, "h1_ready")
            h1_taken = sem(ctx, "h1_taken")
            h2_ready = sem(ctx, "h2_ready")
            h2_taken = sem(ctx, "h2_taken")
            stored = sem(ctx, "rel_stored")
            N1 = RP * 2
            with nc.Block() as block:
                @block.gpsimd
                def _(pool):
                    pool.memset(w2[:, :, :], 0.0).then_inc(zeroed, 1)

                @block.sync
                def _(sp):
                    sp.dma_start(w1[:, :, :], A["w1"].rearrange("i (c n) -> i c n", c=RP)).then_inc(weights, 16)
                    sp.wait_ge(zeroed, 1)
                    for k in range(2):
                        sp.dma_start(w2[k * F:(k + 1) * F, :, k * F:(k + 1) * F],
                                     A["w2"].rearrange("i (c k o) -> i c k o", k=2, o=F)[:, :, k, :]
                                     ).then_inc(weights, 16)
                        sp.dma_start(bias1[k * F:(k + 1) * F, :], A["bias1"].rearrange("(f a) -> f a", a=1)
                                     ).then_inc(weights, 16)
                    table = table_l1.rearrange("(p b r) f -> p b (r f)", b=NB, r=NR)
                    with sp.Fori(0, NG) as g:
                        sp.wait_ge(h2_taken, g * GB + GB + 2)
                        sp.dma_start(table[:, bass.ds(g * GB, GB), :], rows[:, :, :]).then_inc(stored, 16)
                    sp.wait_ge(stored, NG * 16)

                @block.tensor
                def _(pe):
                    pe.wait_ge(weights, 80)

                    def group_of(g, first):
                        pe.wait_ge(h_staged, g + 1)
                        if not first:
                            pe.wait_ge(hT_ready, g)
                        for j in range(GB):
                            mm = pe.matmul(hT_ps[0:F, j * P:(j + 1) * P], h_stage[:, j, :], ident[:, :],
                                           start=True, stop=True)
                        mm.then_inc(turned, 1)
                        pe.wait_ge(hT_ready, g + 1)
                        for c in range(RP):
                            for k in range(2):
                                n = 2 * c + k
                                pe.wait_ge(h1_taken, g * N1 + n + 1)
                                pe.matmul(h1_ps[k][0:2 * F, 0:HALF], w1[:, c, :], hT[:, k * HALF:(k + 1) * HALF],
                                          start=True, stop=True).then_inc(h1_ready, 1)
                        pe.wait_ge(h1_taken, g * N1 + N1 + 2)
                        for j in range(GB):
                            k = j % 2
                            pe.wait_ge(h2_taken, g * GB + j + 1)
                            for c in range(RP):
                                mm = pe.matmul(h2_ps[k][:, c * 2 * F:(c + 1) * 2 * F], h1T[:, c, j * P:(j + 1) * P],
                                               w2[:, c, :], start=True, stop=True)
                            if j == GB - 1:
                                pe.wait_ge(h2_taken, g * GB + j + 2)
                            mm.then_inc(h2_ready, 1)

                    steps_from_first(pe, NG, group_of)

                @block.scalar
                def _(act):
                    act.sem_inc(h1_taken, 2)
                    act.wait_ge(weights, 80)

                    def group_of(g, first):
                        for c in range(RP):
                            for k in range(2):
                                n = 2 * c + k
                                act.wait_ge(h1_ready, g * N1 + n + 1)
                                if not first:
                                    act.wait_ge(h2_ready, g * GB)
                                act.activation(h1T[:, c, k * HALF:(k + 1) * HALF], h1_ps[k][0:2 * F, 0:HALF],
                                               ACT.Relu, bias=bias1[:, 0:1]).then_inc(h1_taken, 1)

                    steps_from_first(act, NG, group_of)

                @block.vector
                def _(dve):
                    dve.sem_inc(h2_taken, 2)

                    def group_of(g, first):
                        if not first:
                            dve.wait_ge(turned, g)
                        dve.tensor_copy(h_stage[:, :, :], group(h_nodes, g * GB)).then_inc(h_staged, 1)
                        dve.wait_ge(turned, g + 1)
                        if not first:
                            dve.wait_ge(h1_ready, g * N1)
                        dve.tensor_copy(hT[:, :], hT_ps[0:F, 0:GB * P]).then_inc(hT_ready, 1)
                        if not first:
                            dve.wait_ge(stored, g * 16)
                        for j in range(GB):
                            dve.wait_ge(h2_ready, g * GB + j + 1)
                            dve.tensor_copy(rows[:, j, :], h2_ps[j % 2][:, 0:NR * F]).then_inc(h2_taken, 1)

                    steps_from_first(dve, NG, group_of)
        clear_used()
        clear_accT()
        edge_pass(1, table_l1, F, src_rel, norm_col, rows_too=True)

        def load_row(tile, row, tag):
            with ExitStack() as ctx:
                got = sem(ctx, "row_loaded_" + tag)
                with nc.Block() as block:
                    @block.sync
                    def _(sp):
                        sp.dma_start(tile, row).then_inc(got, 16)
                        sp.wait_ge(got, 16)
            clear_used()

        with ExitStack() as outer:
            bias2 = sb(outer, "bias2", [P, F])
            load_row(bias2[:, :], A["bias2"].broadcast_to([P, F]), "bias2")

            def update_l1(dve, b0, turned, product, tmp, step, n):
                dve.tensor_tensor(tmp[:, :, :], turned[:, :, :], bias2[:, :].unsqueeze(1).broadcast_to([P, GB, F]),
                                  ALU.add).then_inc(step, 1)
                dve.wait_ge(step, n + 1)
                dve.scalar_tensor_tensor(out=group(x_nodes, b0), in0=tmp[:, :, :], scalar=0.0,
                                         in1=group(x_nodes, b0), op0=ALU.max, op1=ALU.add).then_inc(step, 1)

            node_update(update_l1, n_dve=2)

        with ExitStack() as ctx:
            emb_t = sb(ctx, "emb_t", [ZD, NZ])
            adapt = sb(ctx, "adapt", [ZD, ZD])
            ab = sb(ctx, "ab", [ZD, NZ])
            logits = sb(ctx, "logits", [NZ, NZ])
            GN = GB * P
            types = [sb(ctx, f"types{k}", [NZ, GN], i32) for k in range(2)]
            type_hot = sb(ctx, "type_hot", [NZ, GN])
            made_rows = sb(ctx, "made_rows", [P, GB, NZ])
            pA = ps(ctx, "pA")
            pR = [ps(ctx, f"pR{k}") for k in range(2)]
            small = sem(ctx, "small_loaded")
            types_loaded = [sem(ctx, f"types_loaded{k}") for k in range(2)]
            prod = sem(ctx, "pair_prod")
            made = sem(ctx, "pair_made")
            hot = sem(ctx, "type_hot_ready")
            found = sem(ctx, "pair_found")
            copied = sem(ctx, "pair_copied")
            stored = sem(ctx, "pair_stored")
            with nc.Block() as block:
                @block.sync
                def _(sp):
                    sp.dma_start(emb_t[:, :], A["emb_t"]).then_inc(small, 16)
                    sp.dma_start(adapt[:, :], A["adapt"]).then_inc(small, 16)

                    def load(g, k):
                        sp.dma_start(types[k][:, :], A["type_line"][:, bass.ds(g * GN, GN)].broadcast_to([NZ, GN])
                                     ).then_inc(types_loaded[k], 16)

                    load(0, 0)
                    load(1, 1)
                    with sp.Fori(0, NG // 2) as s:
                        for k in range(2):
                            g = s * 2 + k
                            sp.wait_ge(hot, g + 1 + 2)
                            load(g + 2, k)
                            sp.wait_ge(copied, g * 2 + 2 + 2)
                            sp.dma_start(pair_rows[bass.ds(g * GN, GN), :].rearrange("(b p) z -> p b z", p=P),
                                         made_rows[:, :, :]).then_inc(stored, 16)
                    sp.wait_ge(copied, NG * 2 + 3)
                    sp.dma_start(pair_rows[NP:NP + WIN, :], made_rows[:, 0, :]).then_inc(stored, 16)
                    sp.wait_ge(stored, NG * 16 + 16)
                    for k in range(2):
                        sp.wait_ge(types_loaded[k], NG * 8 + 16)

                @block.tensor
                def _(pe):
                    pe.wait_ge(small, 32)
                    pe.matmul(pA[0:ZD, 0:NZ], adapt[:, :], emb_t[:, :], start=True, stop=True).then_inc(prod, 1)
                    pe.wait_ge(made, 1)
                    pe.matmul(pR[0][0:NZ, 0:NZ], emb_t[:, :], ab[:, :], start=True, stop=True).then_inc(prod, 1)
                    pe.wait_ge(made, 2)
                    with pe.Fori(0, NG) as g:
                        pe.wait_ge(hot, g + 1 + 2)
                        for k, blocks in enumerate((range(0, 4), range(4, GB))):
                            pe.wait_ge(copied, g * 2 + k + 1)
                            for j in blocks:
                                mm = pe.matmul(pR[k][:, (j % 4) * NZ:(j % 4 + 1) * NZ], type_hot[:, j * P:(j + 1) * P],
                                               logits[:, :], start=True, stop=True)
                            mm.then_inc(found, 1)

                @block.vector
                def _(dve):
                    dve.wait_ge(prod, 1)
                    dve.tensor_copy(ab[:, :], pA[0:ZD, 0:NZ]).then_inc(made, 1)
                    dve.wait_ge(prod, 2)
                    dve.tensor_copy(logits[:, :], pR[0][0:NZ, 0:NZ]).then_inc(made, 1)
                    dve.sem_inc(hot, 2)

                    def two_groups(s, first):
                        for k in range(2):
                            g = s * 2 + k
                            dve.wait_ge(types_loaded[k], s * 16 + 16)
                            if not (first and k == 0):
                                dve.wait_ge(found, g * 2)
                            dve.tensor_scalar(type_hot[:, :], types[k][:, :], part[0:NZ, 0:1], None,
                                              ALU.is_equal).then_inc(hot, 1)

                    steps_from_first(dve, NG // 2, two_groups)

                @block.scalar
                def _(act):
                    act.sem_inc(copied, 2)

                    def group_of(g, first):
                        if not first:
                            act.wait_ge(stored, g * 16)
                        for k, (a, b) in enumerate(((0, 4), (4, GB))):
                            act.wait_ge(found, g * 2 + k + 1)
                            act.activation(made_rows[:, a:b, :].rearrange("p b z -> p (b z)"),
                                           pR[k][:, 0:(b - a) * NZ], ACT.Copy).then_inc(copied, 1)

                    steps_from_first(act, NG, group_of)
                    act.wait_ge(stored, NG * 16)
                    act.activation(made_rows[:, 0, :], made_rows[:, 0, :], ACT.Copy, scale=0.0).then_inc(copied, 1)
        clear_used()

        layer_norm_relu()
        with ExitStack() as outer:
            cheb = sb(outer, "cheb", [F, 4, F])
            bias = sb(outer, "cheb_bias", [P, F])
            inv_root = sb(outer, "inv_root", [P, NB])
            minus = sb(outer, "minus_inv_root", [P, NB])
            minus_sq = sb(outer, "minus_sq", [P, NB])
            with ExitStack() as ctx:
                got = sem(ctx, "cheb_loaded")
                step = sem(ctx, "cheb_step")
                root = sem(ctx, "cheb_root")
                has_edge = sb(ctx, "has_edge", [P, NB])
                with nc.Block() as block:
                    @block.sync
                    def _(sp):
                        sp.dma_start(cheb[:, :, :], A["cheb"].rearrange("i (k o) -> i k o", k=4)).then_inc(got, 16)
                        sp.dma_start(bias[:, :], A["cheb_bias"].broadcast_to([P, F])).then_inc(got, 16)

                    @block.scalar
                    def _(act):
                        act.wait_ge(step, 2)
                        act.activation(inv_root[:, :], inv_root[:, :], ACT.Sqrt).then_inc(root, 1)

                    @block.vector
                    def _(dve):
                        dve.tensor_scalar(has_edge[:, :], degree[:, :], 0.0, None, ALU.is_gt).then_inc(step, 1)
                        dve.tensor_scalar(inv_root[:, :], degree[:, :], 1.0, None, ALU.max).then_inc(step, 1)
                        dve.wait_ge(root, 1)
                        dve.reciprocal(inv_root[:, :], inv_root[:, :]).then_inc(step, 1)
                        dve.wait_ge(step, 3)
                        dve.tensor_tensor(inv_root[:, :], inv_root[:, :], has_edge[:, :], ALU.mult).then_inc(step, 1)
                        dve.wait_ge(step, 4)
                        dve.tensor_scalar(minus[:, :], inv_root[:, :], -1.0, None, ALU.mult).then_inc(step, 1)
                        dve.wait_ge(step, 5)
                        dve.tensor_tensor(minus_sq[:, :], minus[:, :], inv_root[:, :], ALU.mult).then_inc(step, 1)
                        dve.wait_ge(got, 32)
                        dve.tensor_tensor(cheb[:, 0:2, :], cheb[:, 0:2, :], cheb[:, 2:4, :], ALU.subtract).then_inc(step, 1)
                        dve.wait_ge(step, 7)
                        dve.tensor_scalar(cheb[:, 2:4, :], cheb[:, 2:4, :], 2.0, None, ALU.mult).then_inc(step, 1)
                        dve.wait_ge(step, 8)
            clear_used()

            with ExitStack() as ctx:
                h_stage = [sb(ctx, f"h_stage{k}", [P, GB, F]) for k in range(2)]
                hT = [sb(ctx, f"hT{k}", [F, GB * P]) for k in range(2)]
                tmp = [sb(ctx, f"tmp{k}", [P, GB, F]) for k in range(2)]
                hT_ps = [ps(ctx, f"hT_ps{k}", [P, 1024]) for k in range(2)]
                prod = [ps(ctx, f"prod{k}", [P, GB, F]) for k in range(2)]
                staged = sem(ctx, "staged")
                turned = sem(ctx, "turned")
                copied = sem(ctx, "copied")
                made = sem(ctx, "made")
                taken = sem(ctx, "taken")
                with nc.Block() as block:
                    @block.vector
                    def _(dve):
                        def two_groups(s, first):
                            for k in range(2):
                                if not first:
                                    dve.wait_ge(turned, s * 2 + k)
                                dve.tensor_copy(h_stage[k][:, :, :], group(h_nodes, (s * 2 + k) * GB)).then_inc(staged, 1)
                            for k in range(2):
                                q = s * 2 + k
                                dve.wait_ge(made, q + 1)
                                dve.tensor_tensor(tmp[k][:, :, :], prod[k][:, :, :],
                                                  bias[:, :].unsqueeze(1).broadcast_to([P, GB, F]),
                                                  ALU.add).then_inc(taken, 1)
                                dve.wait_ge(taken, q * 2 + 1)
                                dve.tensor_tensor(group(x_nodes, q * GB), group(x_nodes, q * GB), tmp[k][:, :, :],
                                                  ALU.add).then_inc(taken, 1)

                        steps_from_first(dve, NG // 2, two_groups)

                    @block.tensor
                    def _(pe):
                        def two_groups(s, first):
                            for k in range(2):
                                q = s * 2 + k
                                pe.wait_ge(staged, q + 1)
                                if not first:
                                    pe.wait_ge(copied, q)
                                for j in range(GB):
                                    mm = pe.matmul(hT_ps[k][0:F, j * P:(j + 1) * P], h_stage[k][:, j, :], ident[:, :],
                                                   start=True, stop=True)
                                mm.then_inc(turned, 1)
                            for k in range(2):
                                q = s * 2 + k
                                pe.wait_ge(copied, q + 1)
                                if not first:
                                    pe.wait_ge(taken, s * 4)
                                for j in range(GB):
                                    mm = pe.matmul(prod[k][:, j, :], hT[k][:, j * P:(j + 1) * P], cheb[:, 0, :],
                                                   start=True, stop=True)
                                mm.then_inc(made, 1)

                        steps_from_first(pe, NG // 2, two_groups)

                    @block.scalar
                    def _(act):
                        def two_groups(s, first):
                            for k in range(2):
                                q = s * 2 + k
                                act.wait_ge(turned, q + 1)
                                if not first:
                                    act.wait_ge(made, s * 2)
                                act.activation(hT[k][:, :], hT_ps[k][0:F, 0:GB * P], ACT.Copy).then_inc(copied, 1)

                        steps_from_first(act, NG // 2, two_groups)
            clear_used()

            def fill_scaled(dve, step):
                dve.tensor_tensor(h_nodes[:, :, :], h_nodes[:, :, :],
                                  inv_root[:, :].unsqueeze(2).broadcast_to([P, NB, F]), ALU.mult).then_inc(step, 1)
                dve.wait_ge(step, 1)
                dve.tensor_copy(w_nodes[:, :, 0:F], h_nodes[:, :, :]).then_inc(step, 1)
                return 2

            store_table(table_l2, F, fill_scaled)

            def fill_ready(dve, step):
                dve.nop().then_inc(step, 1)
                return 1

            for k in (1, 2, 3):
                clear_accT()
                edge_pass(2, table_l2, F, A["src"], other_end, logits_too=(k == 1))

                def update_l2(dve, b0, turned, product, tmp, step, n):
                    dve.tensor_tensor(tmp[:, :, :], product[:, :, :], per_node(minus, b0), ALU.mult).then_inc(step, 1)
                    dve.wait_ge(step, n + 1)
                    dve.tensor_tensor(group(x_nodes, b0), group(x_nodes, b0), tmp[:, :, :], ALU.add).then_inc(step, 1)
                    dve.wait_ge(step, n + 2)
                    if k == 1:
                        dve.tensor_tensor(group(w_nodes, b0), turned[:, :, :], per_node(minus_sq, b0),
                                          ALU.mult).then_inc(step, 2)
                    elif k == 2:
                        dve.tensor_tensor(tmp[:, :, :], turned[:, :, :], per_node(minus_sq, b0), ALU.mult).then_inc(step, 1)
                        dve.wait_ge(step, n + 3)
                        dve.scalar_tensor_tensor(out=group(w_nodes, b0), in0=tmp[:, :, :], scalar=2.0,
                                                 in1=group(h_nodes, b0), op0=ALU.mult,
                                                 op1=ALU.subtract).then_inc(step, 1)

                node_update(update_l2, weight=cheb[:, k, :], n_dve=2 if k == 3 else 4)
                if k < 3:
                    store_table(table_l2, F, fill_ready)
        agg.close()

        layer_norm_relu()
        layer3 = ExitStack()
        top.enter_context(layer3)
        cutoff = sb(layer3, "cutoff", [P, T])
        w1 = sb(layer3, "filter_w1", [2 * R, 2 * F])
        b1 = sb(layer3, "filter_b1", [2 * F, 1])
        w2 = sb(layer3, "filter_w2", [2 * F + 1, 2 * F])
        gamma = sb(layer3, "gamma", [P, F])
        beta = sb(layer3, "beta", [P, F])
        hidden = [sb(layer3, f"hidden{k}", [2 * F + 1, 256]) for k in range(2)]
        with ExitStack() as ctx:
            mult = sb(ctx, "mult", [P, NB])
            dist = sb(ctx, "dist", [P, T])
            near = sb(ctx, "near", [P, T])
            half_pi = sb(ctx, "half_pi", [P, 1])
            zeros = sb(ctx, "zeros", [P, NB + 1, MW])
            parts = sb(ctx, "parts", [P, NB, 3, MW], bf16)
            small = sem(ctx, "small_loaded")
            mult_loaded = sem(ctx, "mult_loaded")
            dist_loaded = sem(ctx, "dist_loaded")
            consts = sem(ctx, "l3_consts")
            made = sem(ctx, "l3_made")
            rows_made = sem(ctx, "l3_rows_made")
            wave = sem(ctx, "l3_wave")
            zeroed = sem(ctx, "sums_zeroed")
            stored = sem(ctx, "l3_stored")
            with nc.Block() as block:
                @block.sync
                def _(sp):
                    sp.dma_start(mult[:, :], A["node_vec"]).then_inc(mult_loaded, 16)
                    for tile, what in ((gamma[:, :], A["gamma"].broadcast_to([P, F])),
                                       (beta[:, :], A["beta"].broadcast_to([P, F]))):
                        sp.dma_start(tile, what).then_inc(small, 16)
                    sp.wait_ge(consts, 6)
                    for k in range(2):
                        out_cols = slice(k * F, (k + 1) * F)
                        for tile, what in ((w1[k * R:(k + 1) * R, out_cols], A["fw1_t"]),
                                           (w2[k * F:(k + 1) * F, out_cols], A["fw2_t"]),
                                           (w2[2 * F:2 * F + 1, out_cols], A["fb2"]),
                                           (b1[k * F:(k + 1) * F, :], A["fb1"])):
                            sp.dma_start(tile, what).then_inc(small, 16)
                    sp.wait_ge(rows_made, 7)
                    sp.dma_start(table_l3[0:NP, :].rearrange("(p b) f -> p (b f)", b=NB),
                                 parts[:, :, :, :].rearrange("p b k f -> p (b k f)")).then_inc(stored, 16)
                    sp.wait_ge(stored, 16)
                    sp.wait_ge(small, 160)

                @block.scalar
                def _(act):
                    act.dma_start(dist[:, :], A["dist"]).then_inc(dist_loaded, 16)
                    act.wait_ge(consts, 6)
                    for k in range(NT):
                        act.dma_start(sums[k].rearrange("(p b) f -> p b f", b=NB + 1), zeros[:, :, :]).then_inc(zeroed, 16)
                    act.dma_start(table_l3[NP:NP + WIN, :],
                                  zeros[:, 0:3, :].rearrange("p k f -> p (k f)").bitcast(bf16)[:, 0:3 * MW]
                                  ).then_inc(zeroed, 16)
                    act.wait_ge(made, 2)
                    act.activation(dist[:, :], dist[:, :], ACT.Sin, bias=half_pi[:, 0:1],
                                   scale=-float(np.pi) / CUTOFF).then_inc(wave, 1)
                    act.wait_ge(zeroed, (NT + 1) * 16)

                @block.gpsimd
                def _(pool):
                    pool.memset(zeros[:, :, :], 0.0).then_inc(consts, 1)
                    pool.memset(half_pi[:, :], float(np.pi) / 2).then_inc(consts, 1)
                    for k in range(2):
                        pool.memset(hidden[k][:, :], 1.0).then_inc(consts, 1)
                    pool.memset(w1[:, :], 0.0).then_inc(consts, 1)
                    pool.memset(w2[:, :], 0.0).then_inc(consts, 1)

                @block.vector
                def _(dve):
                    dve.tensor_copy(w_nodes[:, :, 0:F], h_nodes[:, :, :]).then_inc(rows_made, 1)
                    dve.wait_ge(mult_loaded, 16)
                    dve.tensor_copy(w_nodes[:, :, F], mult[:, :]).then_inc(rows_made, 1)
                    dve.wait_ge(rows_made, 2)
                    rest = w_nodes[:, :, 0:MW]
                    for k in range(2):
                        dve.tensor_copy(parts[:, :, k, :], rest).then_inc(rows_made, 1)
                        dve.wait_ge(rows_made, 3 + 2 * k)
                        dve.tensor_tensor(rest, rest, parts[:, :, k, :], ALU.subtract).then_inc(rows_made, 1)
                        dve.wait_ge(rows_made, 4 + 2 * k)
                    dve.tensor_copy(parts[:, :, 2, :], rest).then_inc(rows_made, 1)
                    dve.wait_ge(dist_loaded, 16)
                    dve.tensor_scalar(near[:, :], dist[:, :], CUTOFF, None, ALU.is_lt).then_inc(made, 1)
                    dve.wait_ge(made, 1)
                    dve.tensor_scalar(dist[:, :], dist[:, :], -CUTOFF, CUTOFF, ALU.max, ALU.min).then_inc(made, 1)
                    dve.wait_ge(wave, 1)
                    dve.tensor_scalar(dist[:, :], dist[:, :], 1.0, 0.5, ALU.add, ALU.mult).then_inc(made, 1)
                    dve.wait_ge(made, 3)
                    dve.tensor_tensor(cutoff[:, :], dist[:, :], near[:, :], ALU.mult).then_inc(made, 1)
        clear_used()

        def by_tile(col):
            return col.unsqueeze(2).broadcast_to([P, 4, P])

        with ExitStack() as ctx:
            index = [sb(ctx, f"row_index{h}", [P, HC * 4], i32) for h in range(2)]
            attr_t = [sb(ctx, f"attr_t{h}", [2 * R, HC, 256]) for h in range(2)]
            src_b = [sb(ctx, f"src_b{h}", [P, HC, 512], i32) for h in range(2)]
            dst_b = [sb(ctx, f"dst_b{h}", [P, HC, 512], i32) for h in range(2)]
            window = [sb(ctx, f"window{k}", [WIN, 3 * MW], bf16) for k in range(4)]
            turned_hot = [sb(ctx, f"turned_hot{k}", [WIN, 512], bf16) for k in range(2)]
            same = [sb(ctx, f"same{k}", [P, 4, P], bf16) for k in range(2)]
            rows = [sb(ctx, f"dst_rows{k}", [P, 4, MW]) for k in range(2)]
            weight = [sb(ctx, f"weight{k}", [P, 4]) for k in range(2)]
            msg = [sb(ctx, f"msg{k}", [P, 4, MW]) for k in range(2)]
            part = [[sb(ctx, f"msg{k}_part{i}", [P, 4, MW], bf16) for i in range(3)] for k in range(2)]
            summed = [sb(ctx, f"summed{k}", [P, 4, MW]) for k in range(4)]
            hid_ps = [ps(ctx, f"hid_ps{k}") for k in range(2)]
            gate_ps = [ps(ctx, f"gate_ps{k}") for k in range(2)]
            rows_ps = [ps(ctx, f"rows_ps{k}") for k in range(2)]
            sum_ps = [ps(ctx, f"sum_ps{k}") for k in range(2)]
            index_loaded = [sem(ctx, f"index_loaded{h}") for h in range(2)]
            attr_loaded = [sem(ctx, f"attr_loaded{h}") for h in range(2)]
            src_loaded = [sem(ctx, f"src_loaded{h}") for h in range(2)]
            dst_loaded = [sem(ctx, f"dst_loaded{h}") for h in range(2)]
            window_loaded = [sem(ctx, f"window_loaded{k}") for k in range(4)]
            hid_made = sem(ctx, "hid_made")
            silu_done = sem(ctx, "silu_done")
            gate_made = sem(ctx, "gate_made")
            turned_ready = sem(ctx, "turned_ready")
            rows_found = sem(ctx, "rows_found")
            rows_ready = sem(ctx, "rows_ready")
            same_made = sem(ctx, "same_made")
            step = sem(ctx, "msg_step")
            msg_made = sem(ctx, "msg_made")
            high_made = sem(ctx, "high_made")
            rest_made = sem(ctx, "rest_made")
            mid_made = sem(ctx, "mid_made")
            low_made = sem(ctx, "low_made")
            sums_made = sem(ctx, "sums_made")
            summed_ready = sem(ctx, "summed_ready")
            scattered = slot_scattered
            dma_turn = sem(ctx, "dma_turn")
            D = 3

            def pipelined_steps(eng, body):
                body(0, True, False)
                with eng.Fori(1, STEPS - 1) as s:
                    body(s, False, False)
                body(STEPS - 1, False, True)

            def ahead(stage, s, c, n, last):
                if not (last and c + n >= CPS):
                    stage(s + (c + n) // CPS, (c + n) % CPS)

            with nc.Block() as block:
                @block.sync
                def _(sp):
                    def step_of(s, first):
                        for h in range(2):
                            sp.wait_ge(hid_made, s * CPS + HC * (h + 1))
                            sp.dma_start(attr_t[h][:, :, :],
                                         A["ea_t"][bass.ds((s * 2 + h) * HC, HC), :, :]
                                         .rearrange("c r e -> r c e")).then_inc(attr_loaded[h], 16)
                            sp.wait_ge(turned_ready, s * CPS + HC * (h + 1))
                            sp.dma_start(dst_b[h][:, :, :], A["dst_lines"][bass.ds((s * 2 + h) * HC, HC), :]
                                         .unsqueeze(0).broadcast_to([P, HC, 512])).then_inc(dst_loaded[h], 16)
                            sp.wait_ge(same_made, s * CPS + HC * (h + 1))
                            sp.dma_start(src_b[h][:, :, :], A["src_lines"][bass.ds((s * 2 + h) * HC, HC), :]
                                         .unsqueeze(0).broadcast_to([P, HC, 512])).then_inc(src_loaded[h], 16)
                            for c in range(HC * h, HC * (h + 1)):
                                q = s * CPS + c
                                base = sp.value_load(base_int[0:1, bass.ds(q, 1)], min_val=0, max_val=NP)
                                sp.wait_ge(rows_found, q + 1)
                                sp.dma_start(window[c % 4][:, :], table_l3[bass.ds(base, WIN), :]
                                             ).then_inc(window_loaded[c % 4], 16)
                            if not first:
                                for k in range(2):
                                    sp.wait_ge(scattered[k], s * 256 - 128 + h * 128)
                            sp.dma_start(index[h][:, :], sum_rows[:, bass.ds((s * 2 + h) * (HC * 4), HC * 4)]
                                         ).then_inc(index_loaded[h], 16)

                    steps_from_first(sp, STEPS, step_of)

                @block.gpsimd
                def _(pool):
                    def step_of(s, first):
                        for c in range(CPS):
                            if c % HC == 0:
                                pool.wait_ge(index_loaded[c // HC], s * 16 + 16)
                            pool.wait_ge(summed_ready, s * CPS + c + 1 + 2)
                            if not (first and c < 2):
                                pool.wait_ge(scattered[c % 2], s * 256 + (c // 2) * 64)
                            pool.sem_inc(dma_turn, 1)
                            for j in range(4):
                                t = (c % HC) * 4 + j
                                pool.indirect_dma_start(
                                    sums[(c % 2) * 4 + j],
                                    bass.IndirectOffsetOnAxis(ap=index[c // HC][:, t:t + 1], axis=0),
                                    summed[c % 4][:, j, :], None, compute_op=ALU.add,
                                ).then_inc(scattered[c % 2], 16)

                    steps_from_first(pool, STEPS, step_of)
                    for k in range(2):
                        pool.wait_ge(scattered[k], STEPS * 256)

                @block.tensor
                def _(pe):
                    pe.sem_inc(hid_made, CPS)
                    pe.sem_inc(gate_made, 2)
                    pe.sem_inc(sums_made, 2)
                    pe.sem_inc(rows_found, 4)

                    def hid(s, c):
                        q = s * CPS + c
                        pe.wait_ge(attr_loaded[c // HC], s * 16 + 16)
                        pe.wait_ge(silu_done, q + 1)
                        pe.matmul(hid_ps[c % 2][0:2 * F, 0:256], w1[:, :], attr_t[c // HC][:, c % HC, :],
                                  start=True, stop=True).then_inc(hid_made, 1)

                    def rows_of(s, c):
                        q = s * CPS + c
                        pe.wait_ge(turned_ready, q + 1 + CPS)
                        pe.wait_ge(window_loaded[c % 4], s * 32 + (c // 4) * 16 + 16)
                        pe.wait_ge(rows_ready, q + 1)
                        for j in range(4):
                            for i in range(3):
                                mm = pe.matmul(rows_ps[c % 2][:, j * MW:(j + 1) * MW],
                                               turned_hot[c % 2][:, j * P:(j + 1) * P],
                                               window[c % 4][:, i * MW:(i + 1) * MW], start=(i == 0), stop=(i == 2))
                        mm.then_inc(rows_found, 1)

                    def gate(s, c):
                        q = s * CPS + c
                        pe.wait_ge(silu_done, q + 1 + 2)
                        pe.wait_ge(msg_made, q + 1)
                        for e in range(2):
                            mm = pe.matmul(gate_ps[c % 2][:, e * 2 * F:(e + 1) * 2 * F], hidden[c % 2][:, e * P:(e + 1) * P],
                                           w2[:, :], start=True, stop=True)
                        mm.then_inc(gate_made, 1)

                    def totals(s, c):
                        q = s * CPS + c
                        pe.wait_ge(same_made, q + 1 + CPS)
                        pe.wait_ge(low_made, q + 1)
                        pe.wait_ge(summed_ready, q + 1)
                        for j in range(4):
                            for i in range(3):
                                mm = pe.matmul(sum_ps[c % 2][:, j * MW:(j + 1) * MW], same[c % 2][:, j, :],
                                               part[c % 2][i][:, j, :], start=(i == 0), stop=(i == 2))
                        mm.then_inc(sums_made, 1)

                    hid(0, 0)
                    hid(0, 1)
                    rows_of(0, 0)
                    gate(0, 0)

                    def step_of(s, first, last):
                        for c in range(CPS):
                            ahead(hid, s, c, 2, last)
                            ahead(rows_of, s, c, 1, last)
                            ahead(gate, s, c, 1, last)
                            totals(s, c)

                    pipelined_steps(pe, step_of)

                @block.scalar
                def _(act):
                    act.sem_inc(silu_done, 2)
                    act.sem_inc(summed_ready, 2)
                    act.sem_inc(rows_ready, 2)

                    def silu(s, c):
                        q = s * CPS + c
                        act.wait_ge(hid_made, q + 1 + CPS)
                        act.wait_ge(gate_made, q + 1)
                        act.activation(hidden[c % 2][0:2 * F, :], hid_ps[c % 2][0:2 * F, 0:256], ACT.Silu,
                                       bias=b1[:, 0:1]).then_inc(silu_done, 1)

                    def rows_of(s, c):
                        q = s * CPS + c
                        act.wait_ge(rows_found, q + 1 + 4)
                        act.wait_ge(msg_made, q + 1)
                        act.activation(rows[c % 2][:, :, :].rearrange("p j f -> p (j f)"),
                                       rows_ps[c % 2][:, 0:4 * MW], ACT.Copy).then_inc(rows_ready, 1)

                    silu(0, 0)
                    silu(0, 1)
                    rows_of(0, 0)

                    def step_of(s, first, last):
                        for c in range(CPS):
                            q = s * CPS + c
                            k = c % 2
                            ahead(rows_of, s, c, 1, last)
                            act.wait_ge(msg_made, q + 1 + 2)
                            act.wait_ge(sums_made, q + 1)
                            act.activation(part[k][0][:, :, :], msg[k][:, :, :], ACT.Copy).then_inc(high_made, 1)
                            ahead(silu, s, c, 2, last)
                            act.wait_ge(rest_made, q + 1)
                            act.activation(part[k][1][:, :, :], msg[k][:, :, :], ACT.Copy).then_inc(mid_made, 1)
                            act.wait_ge(sums_made, q + 1 + 2)
                            if not (first and c < 4):
                                act.wait_ge(scattered[k], s * 256 + (c // 2) * 64 - 64)
                            act.activation(summed[c % 4][:, :, :].rearrange("p j f -> p (j f)"),
                                           sum_ps[k][:, 0:4 * MW], ACT.Copy).then_inc(summed_ready, 1)

                    pipelined_steps(act, step_of)

                @block.vector
                def _(dve):
                    dve.sem_inc(same_made, CPS)
                    dve.sem_inc(turned_ready, CPS)
                    dve.sem_inc(msg_made, 2)

                    def turned_onehot(s, c):
                        q = s * CPS + c
                        dve.wait_ge(dst_loaded[c // HC], s * 16 + 16)
                        dve.wait_ge(rows_found, q + 1 + 4 - 2)
                        dve.tensor_scalar(turned_hot[c % 2][:, :], dst_b[c // HC][:, c % HC, :],
                                          window_part[:, bass.ds(q, 1)], None, ALU.is_equal).then_inc(turned_ready, 1)

                    def same_source(s, c):
                        q = s * CPS + c
                        dve.wait_ge(src_loaded[c // HC], s * 16 + 16)
                        dve.wait_ge(sums_made, q + 1)
                        dve.tensor_tensor(same[c % 2][:, :, :],
                                          src_b[c // HC][:, c % HC, :].rearrange("p (j e) -> p j e", e=P),
                                          by_tile(src_cols[:, bass.ds(q * 4, 4)]), ALU.is_equal).then_inc(same_made, 1)

                    turned_onehot(0, 0)
                    turned_onehot(0, 1)
                    same_source(0, 0)

                    def step_of(s, first, last):
                        for c in range(CPS):
                            q = s * CPS + c
                            k = c % 2
                            n = q * D
                            dve.wait_ge(rows_ready, q + 1 + 2)
                            dve.wait_ge(sums_made, q + 1)
                            dve.tensor_tensor(weight[k][:, :], cutoff[:, bass.ds(q * 4, 4)], rows[k][:, :, F],
                                              ALU.mult).then_inc(step, 1)
                            dve.tensor_copy(msg[k][:, :, F], rows[k][:, :, F]).then_inc(step, 1)
                            dve.wait_ge(gate_made, q + 1 + 2)
                            for j in range(4):
                                at = ((j % 2) * 2 + j // 2) * F
                                got = dve.scalar_tensor_tensor(out=msg[k][:, j, 0:F], in0=gate_ps[k][:, at:at + F],
                                                               scalar=logit_all[:, bass.ds(q * 4 + j, 1)],
                                                               in1=rows[k][:, j, 0:F], op0=ALU.add, op1=ALU.mult)
                            got.then_inc(step, 1)
                            dve.wait_ge(step, n + D)
                            dve.tensor_tensor(msg[k][:, :, 0:F], msg[k][:, :, 0:F],
                                              weight[k][:, :].unsqueeze(2).broadcast_to([P, 4, F]),
                                              ALU.mult).then_inc(msg_made, 1)
                            ahead(turned_onehot, s, c, 2, last)
                            dve.wait_ge(high_made, q + 1)
                            dve.tensor_tensor(msg[k][:, :, :], msg[k][:, :, :], part[k][0][:, :, :],
                                              ALU.subtract).then_inc(rest_made, 1)
                            ahead(same_source, s, c, 1, last)
                            dve.wait_ge(mid_made, q + 1)
                            dve.tensor_tensor(part[k][2][:, :, :], msg[k][:, :, :], part[k][1][:, :, :],
                                              ALU.subtract).then_inc(low_made, 1)

                    pipelined_steps(dve, step_of)
        clear_used()

        with nc.If(residual > WIN - 1):
            with ExitStack() as ctx:
                row_index = sb(ctx, "res_row_index", [P, 4], i32)
                dst_now = sb(ctx, "res_dst", [P, 4], i32)
                attr_t = sb(ctx, "res_attr_t", [2 * R, 256])
                src_b = sb(ctx, "res_src_b", [P, 4, P], i32)
                base_b = sb(ctx, "res_base_b", [P, NCH])
                row_parts = sb(ctx, "res_row_parts", [P, 4, 3 * MW], bf16)
                rows = sb(ctx, "res_rows", [P, 4, MW])
                pair = sb(ctx, "res_pair", [P, 4, NZ])
                beyond = sb(ctx, "res_beyond", [P, 4])
                far = sb(ctx, "res_far", [P, 4])
                logit = sb(ctx, "res_logit", [P, 4])
                junk = sb(ctx, "res_junk", [P, 4, P])
                same = sb(ctx, "res_same", [P, 4, P])
                msg = sb(ctx, "res_msg", [P, 4, MW])
                summed = sb(ctx, "res_summed", [P, 4, MW])
                hid_ps = ps(ctx, "res_hid_ps")
                gate_ps = ps(ctx, "res_gate_ps")
                sum_ps = ps(ctx, "res_sum_ps")
                loaded = sem(ctx, "res_loaded")
                base_loaded = sem(ctx, "res_base_loaded")
                gathered = top.enter_context(nc.semaphore("res_l3_gathered"))
                scattered = top.enter_context(nc.semaphore("res_l3_scattered"))
                chunk_started = sem(ctx, "res_chunk_started")
                silu_done = sem(ctx, "res_silu_done")
                products = sem(ctx, "res_products")
                step = sem(ctx, "res_step")
                summed_ready = sem(ctx, "res_summed_ready")
                chunk_over = sem(ctx, "res_chunk_over")
                D = 10
                with nc.Block() as block:
                    @block.sync
                    def _(sp):
                        sp.dma_start(base_b[:, :], base_row.broadcast_to([P, NCH])).then_inc(base_loaded, 16)
                        with sp.Fori(0, NCH) as g:
                            sp.wait_ge(chunk_over, g + 1)
                            sp.dma_start(row_index[:, :], sum_rows[:, bass.ds(g * 4, 4)]).then_inc(loaded, 16)
                            sp.dma_start(dst_now[:, :], A["dst"][:, bass.ds(g * 4, 4)]).then_inc(loaded, 16)
                            sp.dma_start(attr_t[:, :], A["ea_t"][bass.ds(g, 1), :, :]
                                         .rearrange("a r e -> (a r) e")).then_inc(loaded, 16)
                            sp.dma_start(src_b[:, :, :].rearrange("p j e -> p (j e)"),
                                         A["src_lines"][bass.ds(g, 1), :].broadcast_to([P, 512])).then_inc(loaded, 16)

                    @block.gpsimd
                    def _(pool):
                        pool.sem_inc(chunk_over, 1)
                        with pool.Fori(0, NCH) as g:
                            pool.wait_ge(loaded, g * 64 + 64)
                            pool.sem_inc(chunk_started, 1)
                            for j in range(4):
                                pool.indirect_dma_start(
                                    row_parts[:, j, :], None, table_l3,
                                    bass.IndirectOffsetOnAxis(ap=dst_now[:, j:j + 1], axis=0)).then_inc(gathered, 16)
                                pool.indirect_dma_start(
                                    pair[:, j, :], None, pair_rows,
                                    bass.IndirectOffsetOnAxis(ap=dst_now[:, j:j + 1], axis=0)).then_inc(gathered, 16)
                            pool.wait_ge(summed_ready, g + 1)
                            pool.sem_inc(chunk_started, 1)
                            for j in range(4):
                                pool.indirect_dma_start(
                                    sums[j], bass.IndirectOffsetOnAxis(ap=row_index[:, j:j + 1], axis=0),
                                    summed[:, j, :], None, compute_op=ALU.add).then_inc(scattered, 16)
                            pool.wait_ge(scattered, g * 64 + 64)
                            pool.sem_inc(chunk_over, 1)

                    @block.tensor
                    def _(pe):
                        with pe.Fori(0, NCH) as g:
                            pe.wait_ge(loaded, g * 64 + 64)
                            pe.sem_inc(chunk_started, 1)
                            pe.matmul(hid_ps[0:2 * F, 0:256], w1[:, :], attr_t[:, :], start=True, stop=True
                                      ).then_inc(products, 1)
                            pe.wait_ge(silu_done, g + 1)
                            for e in range(2):
                                mm = pe.matmul(gate_ps[:, e * 2 * F:(e + 1) * 2 * F], hidden[0][:, e * P:(e + 1) * P],
                                               w2[:, :], start=True, stop=True)
                            mm.then_inc(products, 1)
                            pe.wait_ge(step, g * D + D)
                            for j in range(4):
                                mm = pe.matmul(sum_ps[:, j * MW:(j + 1) * MW], same[:, j, :], msg[:, j, :],
                                               start=True, stop=True)
                            mm.then_inc(products, 1)

                    @block.scalar
                    def _(act):
                        with act.Fori(0, NCH) as g:
                            act.wait_ge(products, g * 3 + 1)
                            act.activation(hidden[0][0:2 * F, :], hid_ps[0:2 * F, 0:256], ACT.Silu,
                                           bias=b1[:, 0:1]).then_inc(silu_done, 1)
                            act.wait_ge(products, g * 3 + 3)
                            act.activation(summed[:, :, :].rearrange("p j f -> p (j f)"), sum_ps[:, 0:4 * MW],
                                           ACT.Copy).then_inc(summed_ready, 1)

                    @block.vector
                    def _(dve):
                        dve.wait_ge(base_loaded, 16)
                        with dve.Fori(0, NCH) as g:
                            n = g * D
                            cols = slice(None), bass.ds(g * 4, 4)
                            dve.wait_ge(loaded, g * 64 + 64)
                            dve.tensor_scalar(far[:, :], dst_now[:, :], base_b[:, bass.ds(g, 1)], float(WIN),
                                              ALU.subtract, ALU.is_ge).then_inc(step, 1)
                            dve.tensor_tensor(same[:, :, :], src_b[:, :, :], by_tile(src_cols[cols]),
                                              ALU.is_equal).then_inc(step, 1)
                            dve.wait_ge(gathered, g * 128 + 128)
                            for j in range(4):
                                got = dve.scalar_tensor_tensor(out=junk[:, j, 0:NZ], in0=iota[:, 0:NZ],
                                                               scalar=src_type[:, bass.ds(g * 4 + j, 1)],
                                                               in1=pair[:, j, :], op0=ALU.is_equal, op1=ALU.mult,
                                                               accum_out=logit[:, j:j + 1])
                            got.then_inc(step, 1)
                            dve.tensor_tensor(rows[:, :, :], row_parts[:, :, 0:MW], row_parts[:, :, MW:2 * MW],
                                              ALU.add).then_inc(step, 1)
                            dve.wait_ge(step, n + 4)
                            dve.tensor_tensor(rows[:, :, :], rows[:, :, :], row_parts[:, :, 2 * MW:3 * MW],
                                              ALU.add).then_inc(step, 1)
                            dve.wait_ge(step, n + 5)
                            dve.tensor_tensor(msg[:, :, F], rows[:, :, F], far[:, :], ALU.mult).then_inc(step, 1)
                            dve.wait_ge(step, n + 6)
                            dve.tensor_tensor(beyond[:, :], cutoff[cols], msg[:, :, F], ALU.mult).then_inc(step, 1)
                            dve.wait_ge(products, g * 3 + 2)
                            for j in range(4):
                                at = ((j % 2) * 2 + j // 2) * F
                                got = dve.scalar_tensor_tensor(out=msg[:, j, 0:F], in0=gate_ps[:, at:at + F],
                                                               scalar=logit[:, j:j + 1], in1=rows[:, j, 0:F],
                                                               op0=ALU.add, op1=ALU.mult)
                            got.then_inc(step, 1)
                            dve.wait_ge(step, n + 8)
                            dve.tensor_tensor(msg[:, :, 0:F], msg[:, :, 0:F],
                                              beyond[:, :].unsqueeze(2).broadcast_to([P, 4, F]),
                                              ALU.mult).then_inc(step, 2)
            clear_used()

        with ExitStack() as ctx:
            total = sb(ctx, "total", [P, NB, MW])
            part_sum = [sb(ctx, f"part_sum{k}", [P, NB, MW]) for k in range(2)]
            mean = sb(ctx, "mean", [P, NB])
            loaded = [sem(ctx, f"part_loaded{k}") for k in range(2)]
            first = sem(ctx, "first_loaded")
            step = sem(ctx, "fin_step")
            root = sem(ctx, "fin_root")
            stored = sem(ctx, "out_stored")

            def nodes_of(k):
                return sums[k][0:NP, :].rearrange("(p b) f -> p b f", b=NB)

            per = lambda col: col[:, :].unsqueeze(2).broadcast_to([P, NB, F])
            row = lambda t: t[:, :].unsqueeze(1).broadcast_to([P, NB, F])
            with nc.Block() as block:
                @block.sync
                def _(sp):
                    sp.dma_start(total[:, :, :], nodes_of(0)).then_inc(first, 16)
                    for k in range(1, NT):
                        if k > 2:
                            sp.wait_ge(step, k - 2)
                        sp.dma_start(part_sum[k % 2][:, :, :], nodes_of(k)).then_inc(loaded[k % 2], 16)
                    sp.wait_ge(step, NT - 1 + 15)
                    sp.dma_start(out, x_nodes[:, :, :]).then_inc(stored, 16)
                    sp.wait_ge(stored, 16)

                @block.scalar
                def _(act):
                    act.wait_ge(step, NT - 1 + 9)
                    act.activation(stat2[:, :], stat2[:, :], ACT.Sqrt, bias=eps_col[:, 0:1],
                                   scale=1.0 / F).then_inc(root, 1)

                @block.vector
                def _(dve):
                    n = 0

                    def done(ins):
                        ins.then_inc(step, 1)
                        return n + 1

                    dve.wait_ge(first, 16)
                    for k in range(1, NT):
                        dve.wait_ge(loaded[k % 2], 16 * ((k + 1) // 2))
                        n = done(dve.tensor_tensor(total[:, :, :], total[:, :, :], part_sum[k % 2][:, :, :], ALU.add))
                        dve.wait_ge(step, n)
                    n = done(dve.tensor_scalar(stat[:, :], total[:, :, F], 1e-8, None, ALU.max))
                    dve.wait_ge(step, n)
                    n = done(dve.reciprocal(stat[:, :], stat[:, :]))
                    dve.wait_ge(step, n)
                    n = done(dve.tensor_tensor(total[:, :, 0:F], total[:, :, 0:F], per(stat), ALU.mult))
                    dve.wait_ge(step, n)
                    n = done(dve.tensor_tensor(h_nodes[:, :, :], h_nodes[:, :, :], total[:, :, 0:F], ALU.add))
                    dve.wait_ge(step, n)
                    n = done(dve.tensor_reduce(mean[:, :], h_nodes[:, :, :], AX.X, ALU.add))
                    dve.wait_ge(step, n)
                    n = done(dve.tensor_scalar(mean[:, :], mean[:, :], -1.0 / F, None, ALU.mult))
                    dve.wait_ge(step, n)
                    n = done(dve.tensor_tensor(h_nodes[:, :, :], h_nodes[:, :, :], per(mean), ALU.add))
                    dve.wait_ge(step, n)
                    n = done(dve.tensor_tensor(w_nodes[:, :, 0:F], h_nodes[:, :, :], h_nodes[:, :, :], ALU.mult))
                    dve.wait_ge(step, n)
                    n = done(dve.tensor_reduce(stat2[:, :], w_nodes[:, :, 0:F], AX.X, ALU.add))
                    dve.wait_ge(root, 1)
                    n = done(dve.reciprocal(stat2[:, :], stat2[:, :]))
                    dve.wait_ge(step, n)
                    n = done(dve.tensor_tensor(h_nodes[:, :, :], h_nodes[:, :, :], per(stat2), ALU.mult))
                    dve.wait_ge(step, n)
                    n = done(dve.tensor_tensor(h_nodes[:, :, :], h_nodes[:, :, :], row(gamma), ALU.mult))
                    dve.wait_ge(step, n)
                    n = done(dve.tensor_tensor(h_nodes[:, :, :], h_nodes[:, :, :], row(beta), ALU.add))
                    dve.wait_ge(step, n)
                    n = done(dve.tensor_tensor(x_nodes[:, :, :], x_nodes[:, :, :], h_nodes[:, :, :], ALU.add))
                    dve.wait_ge(step, n)
                    done(dve.nop())


def kernel(x, src, dst, edge_attr_40, edge_attr_48, edge_type_8, edge_weight, edge_weight1, node_type_119, node_vec,
           L0_gnn_eps, L1_gnn_weight1, L1_gnn_weight2, L1_gnn_bias1, L1_gnn_bias2, L2_gnn_weight, L2_gnn_bias,
           L3_gnn_W1, L3_gnn_b1, L3_gnn_W2, L3_gnn_b2, L3_gnn_emb, L3_gnn_adaptW, L3_gnn_gamma, L3_gnn_beta):
    import numpy as _np
    import concourse.bacc as _bacc
    from concourse import mybir as _mybir
    from concourse.bass_utils import run_bass_kernel_spmd as _run

    P = 128
    N, F = x.shape
    E = src.shape[0]
    NB = -(-N // (14 * P)) * 14
    NCH = -(-E // (8 * 512)) * 8
    more_n, more_e = NB * P - N, NCH * 512 - E

    def nodes(a, fill=0):
        a = _np.asarray(a)
        return _np.pad(a, [(0, more_n)] + [(0, 0)] * (a.ndim - 1), constant_values=fill)

    def edges(a, fill=0):
        a = _np.asarray(a)
        return _np.pad(a, [(0, more_e)] + [(0, 0)] * (a.ndim - 1), constant_values=fill)

    def cols(a, fill=0):
        return edges(a, fill).reshape(NCH, P, 4).transpose(1, 0, 2).reshape(P, NCH * 4)

    src_e, dst_e = edges(src, N), edges(dst, N)
    R = edge_attr_40.shape[1]
    arrays = {
        "x": nodes(x).reshape(P, NB, F),
        "src": cols(src, N),
        "dst": cols(dst, N),
        "dst_rows": dst_e.reshape(NCH // 4, 4, 512),
        "src_lines": src_e.reshape(NCH, P, 4).transpose(0, 2, 1).reshape(NCH, 512),
        "dst_lines": dst_e.reshape(NCH, P, 4).transpose(0, 2, 1).reshape(NCH, 512),
        "attr48": edges(edge_attr_48).reshape(NCH, P, 4 * F),
        "ea_t": edges(edge_attr_40).reshape(NCH, P, 2, 2, R).transpose(0, 2, 4, 3, 1).reshape(NCH, 2 * R, 256),
        "edge_type": cols(edge_type_8),
        "dist": cols(edge_weight),
        "norm": cols(_np.asarray(edge_weight1).reshape(E)),
        "node_type": nodes(node_type_119).reshape(P, NB),
        "node_vec": nodes(node_vec).reshape(P, NB),
        "eps": _np.asarray(L0_gnn_eps).reshape(1, 1),
        "w1": _np.asarray(L1_gnn_weight1).transpose(1, 0, 2).reshape(F, -1),
        "w2": _np.asarray(L1_gnn_weight2).transpose(1, 0, 2).reshape(F, -1),
        "bias1": _np.asarray(L1_gnn_bias1),
        "bias2": _np.asarray(L1_gnn_bias2).reshape(1, F),
        "cheb": _np.asarray(L2_gnn_weight).transpose(1, 0, 2).reshape(F, -1),
        "cheb_bias": _np.asarray(L2_gnn_bias).reshape(1, F),
        "fw1_t": _np.asarray(L3_gnn_W1).T,
        "fb1": _np.asarray(L3_gnn_b1).reshape(F, 1),
        "fw2_t": _np.asarray(L3_gnn_W2).T,
        "fb2": _np.asarray(L3_gnn_b2).reshape(1, F),
        "emb_t": _np.asarray(L3_gnn_emb).T,
        "adapt": _np.asarray(L3_gnn_adaptW),
        "type_line": _np.pad(nodes(node_type_119), (0, 14 * P)).reshape(1, -1),
        "gamma": _np.asarray(L3_gnn_gamma).reshape(1, F),
        "beta": _np.asarray(L3_gnn_beta).reshape(1, F),
    }
    nc = _bacc.Bacc("TRN2", target_bir_lowering=False, num_devices=1)
    ins, given = {}, {}
    for name, a in arrays.items():
        a = _np.ascontiguousarray(a)
        given[f"in_{name}"] = a
        ins[name] = nc.dram_tensor(f"in_{name}", a.shape, _mybir.dt.from_np(a.dtype), kind="ExternalInput").ap()
    out = nc.dram_tensor("out_0", [P, NB, F], _mybir.dt.float32, kind="ExternalOutput").ap()
    gnn_program(nc, ins, out)
    r = _run(nc, [given], core_ids=[0])
    return r.results[0]["out_0"].reshape(NB * P, F)[:N]
```

```python
import numpy as np
import concourse.bass as bass
from concourse import mybir
from contextlib import ExitStack


def gnn_program(nc, A, out):
    f32, i32, bf16 = mybir.dt.float32, mybir.dt.int32, mybir.dt.bfloat16
    ALU, ACT, AX = mybir.AluOpType, mybir.ActivationFunctionType, mybir.AxisListType

    P = 128
    F = A["x"].shape[2] if len(A["x"].shape) == 3 else 48
    NB = A["x"].shape[1]
    NP = P * NB
    T = A["src"].shape[1]
    NCH = T // 4
    CPS = 8
    HC = 4
    STEPS = NCH // CPS
    BPS = NB // STEPS
    assert BPS * STEPS == NB and BPS % 2 == 0
    GB = 7
    NG = NB // GB
    WIN = 128
    NR = A["w1"].shape[1] // F
    RP = NR // 2
    ZD, NZ = A["emb_t"].shape
    R = A["fw1_t"].shape[0]
    TW = 52
    NT = 8
    MW = F + 1
    CUTOFF = 6.0
    EPS = 1e-5
    CG = A["dst_rows"].shape[0]

    def dram(name, shape, dt=f32):
        return nc.dram_tensor(name, shape, dt, kind="Internal").ap()

    table_l0 = dram("table_l0", [NP, TW])
    table_l1 = dram("table_l1", [NP * NR, F])
    table_l2 = dram("table_l2", [NP, F])
    table_l3 = dram("table_l3", [NP + WIN, 3 * MW], bf16)
    pair_rows = dram("pair_rows", [NP + WIN, NZ])
    sum_rows = dram("sum_rows", [P, T], i32)
    src_rel = dram("src_rel", [P, T], i32)
    base_row = dram("base_row", [1, NCH])
    base_row_int = dram("base_row_int", [1, NCH], i32)
    span_row = dram("span_row", [1, NCH])
    sums = [dram(f"sum{k}", [NP + P, MW]) for k in range(NT)]

    top = ExitStack()
    with top:
        phase = [0]

        def sb(ctx, name, shape, dt=f32):
            return ctx.enter_context(nc.sbuf_tensor(f"{name}_p{phase[0]}", shape, dt))

        def ps(ctx, name, shape=None, dt=f32):
            return ctx.enter_context(nc.psum_tensor(f"{name}_p{phase[0]}", shape or [P, 512], dt))

        used = []

        def sem(ctx, name):
            s = ctx.enter_context(nc.semaphore(f"{name}_p{phase[0]}"))
            used.append(s)
            return s

        slot_gathered = [top.enter_context(nc.semaphore(f"slot_gathered{c}")) for c in range(8)]
        slot_scattered = [top.enter_context(nc.semaphore(f"slot_scattered{k}")) for k in range(4)]
        gathered_so_far = [0]

        def steps_from_first(eng, count, body):
            body(0, True)
            if count > 1:
                with eng.Fori(1, count) as s:
                    body(s, False)

        def clear_used():
            numbers = list(used)
            used.clear()
            phase[0] += 1

            with nc.Block() as block:
                @block.sync
                def _(sp):
                    for s in numbers:
                        sp.sem_clear(s)

        x_nodes = sb(top, "x_nodes", [P, NB, F])
        h_nodes = sb(top, "h_nodes", [P, NB, F])
        w_nodes = sb(top, "w_nodes", [P, NB, TW])
        src_type = sb(top, "src_type", [P, T])
        src_cols = sb(top, "src_cols", [P, T], i32)
        window_part = sb(top, "window_part", [P, NCH])
        logit_all = sb(top, "logit_all", [P, T])
        base_int = sb(top, "base_int", [1, NCH], i32)
        spare = sb(top, "spare", [P, 1])
        iota = sb(top, "iota", [P, P])
        part = sb(top, "part", [P, 1])
        ident = sb(top, "ident", [P, P])
        earlier = sb(top, "earlier", [P, P])
        eps_col = sb(top, "eps_col", [P, 1])
        zero_col = sb(top, "zero_col", [P, 1])
        stat = sb(top, "stat", [P, NB])
        stat2 = sb(top, "stat2", [P, NB])
        edge_scale = sb(top, "edge_scale", [P, T])

        agg = ExitStack()
        top.enter_context(agg)
        accT = sb(agg, "accT", [F, NP + WIN])
        rel_col = sb(agg, "rel_col", [P, T])
        other_end = sb(agg, "other_end", [P, T])
        span_max = sb(agg, "span_max", [1, 1], i32)
        degree = sb(agg, "degree", [P, NB])
        inv_root = sb(agg, "inv_root", [P, NB])
        minus = sb(agg, "minus_inv_root", [P, NB])
        minus_sq = sb(agg, "minus_sq", [P, NB])
        one_eps = sb(agg, "one_eps", [P, 1])
        bias2 = sb(agg, "bias2", [P, F])
        cheb_bias = sb(agg, "cheb_bias", [P, F])
        cheb_own = sb(agg, "cheb_own", [F, F])
        cheb = sb(agg, "cheb", [F, 3, 2 * F])
        only_l0 = ExitStack()
        agg.enter_context(only_l0)
        src_hi = sb(only_l0, "src_hi", [P, T])
        src_lo = sb(only_l0, "src_lo", [P, T])

        with ExitStack() as ctx:
            dst_cols = sb(ctx, "dst_cols", [P, T], i32)
            type_int = sb(ctx, "type_int", [P, NB], i32)
            rel_type = sb(ctx, "rel_type", [P, T], i32)
            src_part = sb(ctx, "src_part", [P, T], i32)
            rows = sb(ctx, "rows", [CG, 4, 512], i32)
            base_b = sb(ctx, "base_b", [P, NCH])
            lowest = sb(ctx, "lowest", [CG, 4])
            lowest_int = sb(ctx, "lowest_int", [CG, 4], i32)
            highest = sb(ctx, "highest", [CG, 4])
            span = sb(ctx, "span", [1, NCH])
            loaded = {k: sem(ctx, "ld_" + k) for k in ("x", "src", "dst", "rows", "norm", "rel", "type", "base", "idx")}
            made = sem(ctx, "made")
            step = sem(ctx, "prep_step")
            stored = sem(ctx, "prep_stored")
            rows_loaded = sem(ctx, "rows_loaded")
            norm_step = sem(ctx, "norm_step")
            squared = sem(ctx, "squared")
            halves = [slice(0, NB // 2), slice(NB // 2, NB)]
            with nc.Block() as block:
                @block.gpsimd
                def _(pool):
                    pool.iota(iota[:, :], pattern=[[1, P]], base=0, channel_multiplier=0,
                              allow_small_or_imprecise_dtypes=True).then_inc(made, 1)
                    pool.iota(part[:, :], pattern=[[0, 1]], base=0, channel_multiplier=1,
                              allow_small_or_imprecise_dtypes=True).then_inc(made, 1)
                    pool.memset(eps_col[:, :], EPS).then_inc(made, 1)
                    pool.memset(zero_col[:, :], 0.0)
                    pool.memset(w_nodes[:, :, :], 0.0).then_inc(made, 1)
                    pool.memset(accT[:, :], 0.0).then_inc(made, 1)
                    pool.iota(spare[:, :], pattern=[[0, 1]], base=NP, channel_multiplier=1,
                              allow_small_or_imprecise_dtypes=True)

                @block.sync
                def _(sp):
                    sp.dma_start(rows[:, :, :], A["dst_rows"]).then_inc(loaded["rows"], 16)
                    sp.dma_start(x_nodes[:, :, :], A["x"]).then_inc(loaded["x"], 16)
                    sp.dma_start(dst_cols[:, :], A["dst"]).then_inc(loaded["dst"], 16)
                    sp.wait_ge(step, 3)
                    sp.dma_start(base_row.rearrange("a (p q) -> (a p) q", q=4), lowest[:, :]).then_inc(stored, 16)
                    sp.dma_start(base_row_int.rearrange("a (p q) -> (a p) q", q=4), lowest_int[:, :]).then_inc(stored, 16)
                    sp.dma_start(span_row.rearrange("a (p q) -> (a p) q", q=4), highest[:, :]).then_inc(stored, 16)
                    sp.wait_ge(stored, 48)
                    sp.dma_start(base_b[:, :], base_row.broadcast_to([P, NCH])).then_inc(loaded["base"], 16)
                    sp.dma_start(span[:, :], span_row).then_inc(loaded["base"], 16)
                    sp.dma_start(base_int[:, :], base_row_int).then_inc(loaded["base"], 16)
                    sp.wait_ge(step, 8)
                    sp.dma_start(src_rel, rel_type[:, :]).then_inc(loaded["idx"], 16)
                    sp.wait_ge(loaded["idx"], 16)

                @block.scalar
                def _(act):
                    act.dma_start(src_cols[:, :], A["src"]).then_inc(loaded["src"], 16)
                    act.dma_start(rel_type[:, :], A["edge_type"]).then_inc(loaded["rel"], 16)
                    act.dma_start(edge_scale[:, :], A["norm"]).then_inc(loaded["norm"], 16)
                    act.dma_start(type_int[:, :], A["node_type"]).then_inc(loaded["type"], 16)
                    act.dma_start(one_eps[:, :], A["eps"].broadcast_to([P, 1])).then_inc(rows_loaded, 16)
                    act.dma_start(bias2[:, :], A["bias2"].broadcast_to([P, F])).then_inc(rows_loaded, 16)
                    act.dma_start(cheb_bias[:, :], A["cheb_bias"].broadcast_to([P, F])).then_inc(rows_loaded, 16)
                    act.wait_ge(made, 4)
                    for k, at in enumerate(halves):
                        act.wait_ge(norm_step, 3 + k)
                        act.activation(w_nodes[:, at, 0:F], h_nodes[:, at, :], ACT.Square).then_inc(squared, 1)
                    act.wait_ge(loaded["norm"], 16)

                @block.vector
                def _(dve):
                    dve.wait_ge(loaded["rows"], 16)
                    dve.tensor_reduce(lowest[:, :], rows[:, :, :], AX.X, ALU.min).then_inc(step, 1)
                    dve.tensor_reduce(highest[:, :], rows[:, :, :], AX.X, ALU.max)
                    dve.wait_ge(step, 1)
                    dve.tensor_copy(lowest_int[:, :], lowest[:, :]).then_inc(step, 1)
                    dve.drain()
                    dve.tensor_tensor(highest[:, :], highest[:, :], lowest[:, :], ALU.subtract).then_inc(step, 1)
                    dve.wait_ge(loaded["x"], 16)
                    dve.tensor_reduce(stat[:, :], x_nodes[:, :, :], AX.X, ALU.add).then_inc(norm_step, 1)
                    dve.wait_ge(norm_step, 1)
                    dve.tensor_scalar(stat[:, :], stat[:, :], -1.0 / F, None, ALU.mult).then_inc(norm_step, 1)
                    dve.wait_ge(norm_step, 2)
                    for at in halves:
                        dve.tensor_tensor(h_nodes[:, at, :], x_nodes[:, at, :],
                                          stat[:, at].unsqueeze(2).broadcast_to([P, NB // 2, F]),
                                          ALU.add).then_inc(norm_step, 1)
                    dve.wait_ge(loaded["src"], 16)
                    dve.wait_ge(loaded["dst"], 16)
                    dve.tensor_tensor(other_end[:, :], src_cols[:, :], dst_cols[:, :], ALU.not_equal).then_inc(step, 1)
                    dve.tensor_single_scalar(src_part[:, :], src_cols[:, :], 7,
                                             op=ALU.logical_shift_right).then_inc(step, 1)
                    dve.wait_ge(step, 5)
                    dve.tensor_copy(src_hi[:, :], src_part[:, :]).then_inc(step, 1)
                    dve.wait_ge(step, 6)
                    dve.tensor_single_scalar(src_part[:, :], src_cols[:, :], P - 1, op=ALU.bitwise_and).then_inc(step, 1)
                    dve.wait_ge(loaded["rel"], 16)
                    dve.scalar_tensor_tensor(out=rel_type[:, :], in0=src_cols[:, :], scalar=float(NR),
                                             in1=rel_type[:, :], op0=ALU.mult, op1=ALU.add).then_inc(step, 1)
                    dve.wait_ge(step, 7)
                    dve.tensor_copy(src_lo[:, :], src_part[:, :]).then_inc(step, 1)
                    dve.wait_ge(loaded["base"], 48)
                    dve.tensor_tensor(rel_col[:, :].rearrange("p (g j) -> p g j", j=4),
                                      dst_cols[:, :].rearrange("p (g j) -> p g j", j=4),
                                      base_b[:, :].unsqueeze(2).broadcast_to([P, NCH, 4]), ALU.subtract).then_inc(step, 1)
                    dve.tensor_reduce(span_max[:, :], span[:, :], AX.X, ALU.max).then_inc(step, 1)
                    dve.wait_ge(made, 5)
                    dve.tensor_scalar(ident[:, :], iota[:, :], part[:, 0:1], None, ALU.is_equal).then_inc(step, 1)
                    dve.tensor_scalar(earlier[:, :], iota[:, :], part[:, 0:1], None, ALU.is_lt).then_inc(step, 1)
                    dve.tensor_scalar(window_part[:, :], base_b[:, :], part[:, 0:1], None, ALU.add).then_inc(step, 1)
                    dve.wait_ge(loaded["type"], 16)
                    dve.tensor_copy(w_nodes[:, :, F], type_int[:, :]).then_inc(step, 1)
                    for k, at in enumerate(halves):
                        dve.wait_ge(squared, k + 1)
                        dve.tensor_reduce(stat2[:, at], w_nodes[:, at, 0:F], AX.X, ALU.add).then_inc(norm_step, 1)
                    dve.wait_ge(rows_loaded, 48)
                    dve.tensor_scalar(one_eps[:, :], one_eps[:, :], 1.0, None, ALU.add).then_inc(step, 1)
            clear_used()

        ET = mybir.EngineType
        residual = nc.values_load(span_max[0:1, 0:1], engines=[ET.Pool, ET.Activation, ET.PE, ET.DVE, ET.SP],
                                  min_val=0, max_val=NP)

        def edge_pass(layer, table, width, index_dram, scale_col, rows_too=False, logits_too=False, last_too=False,
                      own_too=False):
            LS = 4
            l0 = layer == 0
            OH, PB = 4, 4
            old = gathered_so_far[0]
            with ExitStack() as ctx:
                index = [sb(ctx, f"index{h}", [P, HC * 4], i32) for h in range(2)]
                gathered = [sb(ctx, f"gathered{c}", [P, 4, width]) for c in range(CPS)]
                onehot = [sb(ctx, f"onehot{k}", [P, 4, WIN]) for k in range(OH)]
                chunk_sum = [ps(ctx, f"chunk_sum{k}") for k in range(PB)]
                index_loaded = [sem(ctx, f"index_loaded{h}") for h in range(2)]
                rows_gathered = slot_gathered
                onehot_ready = sem(ctx, "onehot_ready")
                chunk_started = sem(ctx, "chunk_started")
                sum_ready = sem(ctx, "sum_ready")
                sum_added = sem(ctx, "sum_added")
                if rows_too or logits_too:
                    line = [sb(ctx, f"line{k}", [P, 512], i32) for k in range(LS)]
                    line_loaded = [sem(ctx, f"line_loaded{k}") for k in range(LS)]
                    line_used = sem(ctx, "line_used")
                    beside_step = sem(ctx, "beside_step")
                    junk = sb(ctx, "junk", [P, 4, P])
                if rows_too:
                    has_edge = sb(ctx, "has_edge", [P, NB])
                    raw = sb(ctx, "cheb_raw", [F, 4, F])
                    weights_loaded = sem(ctx, "weights_loaded")
                    cheb_step = sem(ctx, "cheb_step")
                    cheb_root = sem(ctx, "cheb_root")
                    emb_t = sb(ctx, "emb_t", [ZD, NZ])
                    adapt = sb(ctx, "adapt", [ZD, ZD])
                    ab = sb(ctx, "ab", [ZD, NZ])
                    logits = sb(ctx, "logits", [NZ, NZ])
                    types = sb(ctx, "types", [NZ, BPS * P], i32)
                    type_hot = sb(ctx, "type_hot", [NZ, BPS * P])
                    made_rows = sb(ctx, "made_rows", [P, BPS, NZ])
                    zero_rows = sb(ctx, "zero_rows", [WIN, NZ])
                    pair_ps = [ps(ctx, f"pair_ps{k}") for k in range(2)]
                    zero_made = sem(ctx, "zero_made")
                    emb_loaded = sem(ctx, "emb_loaded")
                    types_loaded = sem(ctx, "types_loaded")
                    emb_product = sem(ctx, "emb_product")
                    emb_copied = sem(ctx, "emb_copied")
                    hot = sem(ctx, "type_hot_ready")
                    found = sem(ctx, "pair_found")
                    copied = sem(ctx, "pair_copied")
                    pair_stored = sem(ctx, "pair_stored")
                    tail_stored = sem(ctx, "tail_stored")
                if last_too:
                    ZB = max(z for z in range(1, 34) if (NB + 1) % z == 0)
                    zeros = sb(ctx, "zeros", [P, ZB, MW])
                    dist = sb(ctx, "dist", [P, T])
                    near = sb(ctx, "near", [P, T])
                    half_pi = sb(ctx, "half_pi", [P, 1])
                    zeros_made = sem(ctx, "zeros_made")
                    dist_loaded = sem(ctx, "dist_loaded")
                    wave = sem(ctx, "wave")
                    cut_step = sem(ctx, "cut_step")
                    zeros_stored = sem(ctx, "zeros_stored")
                if own_too:
                    own_stage = sb(ctx, "own_stage", [P, BPS, F])
                    own_hT = sb(ctx, "own_hT", [F, BPS * P])
                    own_tmp = sb(ctx, "own_tmp", [P, BPS, F])
                    own_turned_ps = ps(ctx, "own_turned_ps")
                    own_ps = ps(ctx, "own_ps", [P, BPS, F])
                    own_staged = sem(ctx, "own_staged")
                    own_turned = sem(ctx, "own_turned")
                    own_copied = sem(ctx, "own_copied")
                    own_made = sem(ctx, "own_made")
                    own_added = sem(ctx, "own_added")
                if rows_too:
                    before = sb(ctx, "before", [P, 4])
                    to_row = sb(ctx, "to_row", [P, T], i32)
                    rows_stored = sem(ctx, "rows_stored")
                if logits_too:
                    window = [sb(ctx, f"window{k}", [WIN, NZ]) for k in range(LS)]
                    window_loaded = [sem(ctx, f"window_loaded{k}") for k in range(LS)]
                    turned_hot = [sb(ctx, f"turned_hot{k}", [WIN, 512]) for k in range(2)]
                    turned_ready = sem(ctx, "turned_ready")
                    pairs = [ps(ctx, f"pairs{k}") for k in range(2)]
                    pairs_ready = sem(ctx, "pairs_ready")
                if l0:
                    attr = [sb(ctx, f"attr{h}", [P, HC, 4 * F]) for h in range(2)]
                    attr_loaded = [sem(ctx, f"attr_loaded{h}") for h in range(2)]
                    attr_added = sem(ctx, "attr_added")
                    type_kept = sem(ctx, "type_kept")
                    relu_done = sem(ctx, "relu_done")
                    cell_hi = [sb(ctx, f"cell_hi{k}", [P, 4, P], bf16) for k in range(2)]
                    cell_lo = [sb(ctx, f"cell_lo{k}", [P, 4, P], bf16) for k in range(2)]
                    cells_ready = sem(ctx, "cells_ready")
                    cells_counted = sem(ctx, "cells_counted")
                    histogram = ps(ctx, "histogram")
                    counts = sb(ctx, "counts", [P, P])
                    zero_cells = sb(ctx, "zero_cells", [P, P], bf16)
                    zeroed = sem(ctx, "zeroed")
                    count_copied = sem(ctx, "count_copied")
                    degree_dram = dram("degree_dram", [NP])
                    degree_moved = sem(ctx, "degree_moved")
                with nc.Block() as block:
                    @block.sync
                    def _(sp):
                        with sp.Fori(0, STEPS) as s:
                            for h in range(2):
                                sp.wait_ge(sum_ready, s * CPS + HC * (h + 1))
                                sp.dma_start(index[h][:, :], index_dram[:, bass.ds((s * 2 + h) * (HC * 4), HC * 4)]
                                             ).then_inc(index_loaded[h], 16)
                                if l0:
                                    sp.wait_ge(attr_added, s * CPS + HC * (h + 1))
                                    sp.dma_start(attr[h][:, :, :],
                                                 A["attr48"][bass.ds((s * 2 + h) * HC, HC), :, :]
                                                 .rearrange("c p f -> p c f")).then_inc(attr_loaded[h], 16)
                                for c in range(HC * h, HC * (h + 1)):
                                    q = s * CPS + c
                                    if rows_too or logits_too:
                                        sp.wait_ge(line_used, q + 1)
                                        sp.dma_start(line[c % LS][:, :],
                                                     A["src_lines" if rows_too else "dst_lines"][bass.ds(q, 1), :]
                                                     .broadcast_to([P, 512])).then_inc(line_loaded[c % LS], 16)
                                    if logits_too:
                                        base = sp.value_load(base_int[0:1, bass.ds(q, 1)], min_val=0, max_val=NP)
                                        sp.wait_ge(pairs_ready, q + 1)
                                        sp.dma_start(window[c % LS][:, :], pair_rows[bass.ds(base, WIN), :]
                                                     ).then_inc(window_loaded[c % LS], 16)
                        if rows_too:
                            sp.wait_ge(zero_made, 1)
                            sp.dma_start(pair_rows[NP:NP + WIN, :], zero_rows[:, :]).then_inc(tail_stored, 16)
                            sp.wait_ge(tail_stored, 16)
                            sp.wait_ge(beside_step, NCH * 3)
                            sp.dma_start(sum_rows, to_row[:, :]).then_inc(rows_stored, 16)
                            sp.wait_ge(rows_stored, 16)
                        if l0:
                            sp.wait_ge(count_copied, 1)
                            sp.dma_start(degree_dram.rearrange("(a b) -> a b", b=P), counts[0:NB, :]
                                         ).then_inc(degree_moved, 16)
                            sp.wait_ge(degree_moved, 16)
                            sp.dma_start(degree[:, :], degree_dram.rearrange("(p b) -> p b", b=NB)
                                         ).then_inc(degree_moved, 16)
                            sp.wait_ge(degree_moved, 32)

                    @block.gpsimd
                    def _(pool):
                        if l0:
                            pool.memset(zero_cells[:, :], 0.0).then_inc(zeroed, 1)
                        if rows_too:
                            pool.memset(zero_rows[:, :], 0.0).then_inc(zero_made, 1)
                        if last_too:
                            pool.memset(half_pi[:, :], float(np.pi) / 2).then_inc(zeros_made, 1)
                            pool.memset(zeros[:, :, :], 0.0).then_inc(zeros_made, 1)
                        with pool.Fori(0, STEPS) as s:
                            for c in range(CPS):
                                if c % HC == 0:
                                    pool.wait_ge(index_loaded[c // HC], s * 16 + 16)
                                pool.wait_ge(sum_ready, s * CPS + c + 1)
                                if l0:
                                    pool.wait_ge(type_kept, s * CPS + c + 1)
                                pool.sem_inc(chunk_started, 1)
                                for j in range(4):
                                    t = (c % HC) * 4 + j
                                    pool.indirect_dma_start(
                                        gathered[c][:, j, :], None, table,
                                        bass.IndirectOffsetOnAxis(ap=index[c // HC][:, t:t + 1], axis=0),
                                    ).then_inc(rows_gathered[c], 16)

                    @block.tensor
                    def _(pe):
                        pe.sem_inc(sum_ready, CPS)
                        if logits_too:
                            pe.sem_inc(pairs_ready, LS)
                        if rows_too:
                            pe.sem_inc(found, 1)
                            pe.wait_ge(emb_loaded, 32)
                            pe.matmul(pair_ps[0][0:ZD, 0:NZ], adapt[:, :], emb_t[:, :], start=True, stop=True
                                      ).then_inc(emb_product, 1)
                            pe.wait_ge(emb_copied, 1)
                            pe.matmul(pair_ps[1][0:NZ, 0:NZ], emb_t[:, :], ab[:, :], start=True, stop=True
                                      ).then_inc(emb_product, 1)
                            pe.wait_ge(emb_copied, 2)
                        if own_too:
                            pe.sem_inc(own_turned, 1)
                            pe.sem_inc(own_made, 1)
                        if l0:
                            pe.sem_inc(cells_counted, 2)
                            pe.wait_ge(zeroed, 1)
                            pe.matmul(histogram[:, 0:P], zero_cells[:, :], zero_cells[:, :], start=True, stop=False)
                        with pe.Fori(0, STEPS) as s:
                            for c in range(CPS):
                                q = s * CPS + c
                                if l0:
                                    pe.wait_ge(cells_ready, q + 1)
                                    for j in range(4):
                                        mm = pe.matmul(histogram[:, 0:P], cell_hi[c % 2][:, j, :],
                                                       cell_lo[c % 2][:, j, :], start=False, stop=False,
                                                       skip_group_check=True)
                                    mm.then_inc(cells_counted, 1)
                                pe.wait_ge(onehot_ready, q + 1)
                                if l0:
                                    pe.wait_ge(relu_done, q + 1)
                                else:
                                    pe.wait_ge(rows_gathered[c], s * 64 + 64 + old)
                                pe.wait_ge(sum_added, q + 1)
                                for j in range(4):
                                    mm = pe.matmul(chunk_sum[c % PB][0:F, 0:WIN], gathered[c][:, j, 0:F],
                                                   onehot[c % OH][:, j, :], start=(j == 0), stop=(j == 3))
                                mm.then_inc(sum_ready, 1)
                                if rows_too and c == CPS - 2:
                                    pe.wait_ge(hot, s + 2)
                                    for b in range(BPS):
                                        pe.wait_ge(copied, s * BPS + b + 1)
                                        pe.matmul(pair_ps[b % 2][:, 0:NZ], type_hot[:, b * P:(b + 1) * P],
                                                  logits[:, :], start=True, stop=True).then_inc(found, 1)
                                if own_too and c == 2:
                                    pe.wait_ge(own_staged, s + 1)
                                    for b in range(BPS):
                                        mm = pe.matmul(own_turned_ps[0:F, b * P:(b + 1) * P], own_stage[:, b, :],
                                                       ident[:, :], start=True, stop=True)
                                    mm.then_inc(own_turned, 1)
                                if own_too and c == 5:
                                    pe.wait_ge(own_copied, s + 1)
                                    pe.wait_ge(own_added, s * 2 + 2)
                                    for b in range(BPS):
                                        mm = pe.matmul(own_ps[:, b, :], own_hT[:, b * P:(b + 1) * P], cheb_own[:, :],
                                                       start=True, stop=True)
                                    mm.then_inc(own_made, 1)
                                if logits_too:
                                    pe.wait_ge(turned_ready, q + 1)
                                    pe.wait_ge(window_loaded[c % LS], s * 32 + (c // LS) * 16 + 16)
                                    pe.wait_ge(beside_step, q + 1)
                                    for j in range(4):
                                        mm = pe.matmul(pairs[c % 2][:, j * NZ:(j + 1) * NZ],
                                                       turned_hot[c % 2][:, j * P:(j + 1) * P], window[c % LS][:, :],
                                                       start=True, stop=True)
                                    mm.then_inc(pairs_ready, 1)
                        if l0:
                            pe.matmul(histogram[:, 0:P], zero_cells[:, :], zero_cells[:, :], start=False,
                                      stop=True).then_inc(cells_counted, 1)

                    @block.vector
                    def _(dve):
                        dve.sem_inc(sum_added, PB)
                        if l0:
                            dve.sem_inc(attr_added, CPS)

                        def base_of(s, c):
                            return dve.value_load(base_int[0:1, bass.ds(s * CPS + c, 1)], min_val=0, max_val=NP)

                        def add_sum(s, c, base):
                            dve.wait_ge(sum_ready, s * CPS + c + 1 + CPS)
                            dve.wait_ge(sum_added, s * CPS + c + PB)
                            dve.tensor_tensor(accT[:, bass.ds(base, WIN)], accT[:, bass.ds(base, WIN)],
                                              chunk_sum[c % PB][0:F, 0:WIN], ALU.add).then_inc(sum_added, 1)

                        def rows_of(s, c):
                            q = s * CPS + c
                            dve.wait_ge(line_loaded[c % LS], s * 32 + (c // LS) * 16 + 16)
                            for j in range(4):
                                got = dve.scalar_tensor_tensor(out=junk[:, j, :], in0=line[c % LS][:, j * P:(j + 1) * P],
                                                               scalar=src_cols[:, bass.ds(q * 4 + j, 1)],
                                                               in1=earlier[:, :], op0=ALU.is_equal, op1=ALU.mult,
                                                               accum_out=before[:, j:j + 1])
                            got.then_inc(beside_step, 1)
                            dve.wait_ge(beside_step, q * 3 + 1)
                            dve.sem_inc(line_used, 1)
                            dve.tensor_scalar(before[:, :], before[:, :], float(2 * NP), spare[:, 0:1],
                                              ALU.mult, ALU.min).then_inc(beside_step, 1)
                            dve.wait_ge(beside_step, q * 3 + 2)
                            dve.tensor_tensor(to_row[:, bass.ds(q * 4, 4)], before[:, :], src_cols[:, bass.ds(q * 4, 4)],
                                              ALU.max).then_inc(beside_step, 1)
                            dve.wait_ge(beside_step, q * 3 + 3)

                        def turned_onehot(s, c):
                            q = s * CPS + c
                            dve.wait_ge(line_loaded[c % LS], s * 32 + (c // LS) * 16 + 16)
                            dve.wait_ge(pairs_ready, q + 1 + LS - 2)
                            dve.tensor_scalar(turned_hot[c % 2][:, :], line[c % LS][:, :],
                                              window_part[:, bass.ds(q, 1)], None, ALU.is_equal).then_inc(turned_ready, 1)

                        def logits_of(s, c):
                            q = s * CPS + c
                            dve.wait_ge(pairs_ready, q + 1 + LS)
                            dve.wait_ge(beside_step, q + 2)
                            dve.sem_inc(line_used, 1)
                            for j in range(4):
                                got = dve.scalar_tensor_tensor(out=junk[:, j, 0:NZ], in0=iota[:, 0:NZ],
                                                               scalar=src_type[:, bass.ds(q * 4 + j, 1)],
                                                               in1=pairs[c % 2][:, j * NZ:(j + 1) * NZ],
                                                               op0=ALU.is_equal, op1=ALU.mult,
                                                               accum_out=logit_all[:, bass.ds(q * 4 + j, 1)])
                            got.then_inc(beside_step, 1)

                        if rows_too or logits_too:
                            dve.sem_inc(line_used, LS)
                        if rows_too:
                            dve.sem_inc(hot, 1)
                            dve.wait_ge(emb_product, 1)
                            dve.tensor_copy(ab[:, :], pair_ps[0][0:ZD, 0:NZ]).then_inc(emb_copied, 1)
                            dve.wait_ge(emb_product, 2)
                            dve.tensor_copy(logits[:, :], pair_ps[1][0:NZ, 0:NZ]).then_inc(emb_copied, 1)
                            dve.tensor_scalar(has_edge[:, :], degree[:, :], 0.0, None, ALU.is_gt).then_inc(cheb_step, 1)
                            dve.tensor_scalar(inv_root[:, :], degree[:, :], 1.0, None, ALU.max).then_inc(cheb_step, 1)
                            dve.wait_ge(cheb_root, 1)
                            dve.reciprocal(inv_root[:, :], inv_root[:, :]).then_inc(cheb_step, 1)
                            dve.wait_ge(cheb_step, 3)
                            dve.tensor_tensor(inv_root[:, :], inv_root[:, :], has_edge[:, :],
                                              ALU.mult).then_inc(cheb_step, 1)
                            dve.wait_ge(cheb_step, 4)
                            dve.tensor_scalar(minus[:, :], inv_root[:, :], -1.0, None, ALU.mult).then_inc(cheb_step, 1)
                            dve.wait_ge(cheb_step, 5)
                            dve.tensor_tensor(minus_sq[:, :], minus[:, :], inv_root[:, :],
                                              ALU.mult).then_inc(cheb_step, 1)
                            dve.wait_ge(weights_loaded, 16)
                            dve.tensor_tensor(cheb_own[:, :], raw[:, 0, :], raw[:, 2, :], ALU.subtract)
                            dve.tensor_tensor(cheb[:, 0, F:2 * F], raw[:, 1, :], raw[:, 3, :], ALU.subtract)
                            dve.tensor_scalar(cheb[:, 1:3, F:2 * F], raw[:, 2:4, :], 2.0, None, ALU.mult)
                            dve.tensor_copy(cheb[:, :, 0:F], ident[0:F, 0:F].unsqueeze(1).broadcast_to([F, 3, F]))
                        if last_too:
                            dve.wait_ge(dist_loaded, 16)
                            dve.tensor_scalar(near[:, :], dist[:, :], CUTOFF, None, ALU.is_lt).then_inc(cut_step, 1)
                            dve.wait_ge(cut_step, 1)
                            dve.tensor_scalar(dist[:, :], dist[:, :], -CUTOFF, CUTOFF, ALU.max,
                                              ALU.min).then_inc(cut_step, 1)
                            dve.wait_ge(wave, 1)
                            dve.tensor_scalar(dist[:, :], dist[:, :], 1.0, 0.5, ALU.add, ALU.mult).then_inc(cut_step, 1)
                            dve.wait_ge(cut_step, 3)
                            dve.tensor_tensor(edge_scale[:, :], dist[:, :], near[:, :], ALU.mult)
                        if own_too:
                            dve.sem_inc(own_added, 2)
                        if logits_too:
                            dve.sem_inc(beside_step, 2)

                        def step_of(s):
                            for c in range(CPS):
                                q = s * CPS + c
                                dve.wait_ge(sum_ready, q + 1 + CPS - OH)
                                for j in range(4):
                                    t = q * 4 + j
                                    if scale_col is None:
                                        oh = dve.tensor_scalar(onehot[c % OH][:, j, :], iota[:, :],
                                                               rel_col[:, bass.ds(t, 1)], None, ALU.is_equal)
                                    else:
                                        oh = dve.tensor_scalar(onehot[c % OH][:, j, :], iota[:, :],
                                                               rel_col[:, bass.ds(t, 1)],
                                                               scale_col[:, bass.ds(t, 1)], ALU.is_equal, ALU.mult)
                                oh.then_inc(onehot_ready, 1)
                                if c >= 1:
                                    base = base_of(s, c - 1)
                                if c == CPS - 1:
                                    last_base = base_of(s, c)
                                if l0:
                                    dve.wait_ge(cells_counted, q + 1)
                                    for j in range(4):
                                        t = q * 4 + j
                                        dve.tensor_scalar(cell_hi[c % 2][:, j, :], iota[:, :],
                                                          src_hi[:, bass.ds(t, 1)], None, ALU.is_equal)
                                        oh = dve.tensor_scalar(cell_lo[c % 2][:, j, :], iota[:, :],
                                                               src_lo[:, bass.ds(t, 1)],
                                                               other_end[:, bass.ds(t, 1)], ALU.is_equal, ALU.mult)
                                    oh.then_inc(cells_ready, 1)
                                    dve.wait_ge(attr_loaded[c // HC], s * 16 + 16)
                                    dve.wait_ge(rows_gathered[c], s * 64 + 64 + old)
                                    dve.wait_ge(type_kept, q + 1)
                                    dve.tensor_tensor(gathered[c][:, :, 0:F], gathered[c][:, :, 0:F],
                                                      attr[c // HC][:, c % HC, :].rearrange("p (j f) -> p j f", f=F),
                                                      ALU.add).then_inc(attr_added, 1)
                                if rows_too:
                                    rows_of(s, c)
                                if rows_too and c == 2:
                                    dve.wait_ge(types_loaded, s * 16 + 16)
                                    dve.wait_ge(found, s * BPS + 1)
                                    dve.tensor_scalar(type_hot[:, :], types[:, :], part[0:NZ, 0:1], None,
                                                      ALU.is_equal).then_inc(hot, 1)
                                if own_too and c == 7:
                                    dve.wait_ge(own_made, s + 2)
                                    dve.tensor_tensor(own_tmp[:, :, :], own_ps[:, :, :],
                                                      cheb_bias[:, :].unsqueeze(1).broadcast_to([P, BPS, F]),
                                                      ALU.add).then_inc(own_added, 1)
                                    dve.wait_ge(own_added, s * 2 + 3)
                                    own = x_nodes[:, bass.ds(s * BPS, BPS), :]
                                    dve.tensor_tensor(own, own, own_tmp[:, :, :], ALU.add).then_inc(own_added, 1)
                                if logits_too:
                                    turned_onehot(s, c)
                                if c >= 1:
                                    add_sum(s, c - 1, base)
                                    if logits_too:
                                        logits_of(s, c - 1)
                            add_sum(s, CPS - 1, last_base)
                            if logits_too:
                                logits_of(s, CPS - 1)

                        with dve.Fori(0, STEPS) as s:
                            step_of(s)
                        if l0:
                            dve.wait_ge(cells_counted, NCH + 3)
                            dve.tensor_copy(counts[:, :], histogram[:, 0:P]).then_inc(count_copied, 1)

                    if rows_too:
                        @block.scalar
                        def _(act):
                            act.dma_start(emb_t[:, :], A["emb_t"]).then_inc(emb_loaded, 16)
                            act.dma_start(adapt[:, :], A["adapt"]).then_inc(emb_loaded, 16)
                            act.dma_start(raw[:, :, :], A["cheb"].rearrange("i (k o) -> i k o", k=4)
                                          ).then_inc(weights_loaded, 16)
                            act.wait_ge(cheb_step, 2)
                            act.activation(inv_root[:, :], inv_root[:, :], ACT.Sqrt).then_inc(cheb_root, 1)
                            act.sem_inc(copied, 2)

                            def step_of(s, first):
                                if not first:
                                    act.wait_ge(hot, s + 1)
                                act.dma_start(types[:, :], A["type_line"][:, bass.ds(s * (BPS * P), BPS * P)]
                                              .broadcast_to([NZ, BPS * P])).then_inc(types_loaded, 16)
                                for b in range(BPS):
                                    act.wait_ge(found, s * BPS + b + 2)
                                    if not first and b == 0:
                                        act.wait_ge(pair_stored, s * 16)
                                    act.activation(made_rows[:, b, :], pair_ps[b % 2][:, 0:NZ],
                                                   ACT.Copy).then_inc(copied, 1)
                                act.wait_ge(copied, s * BPS + BPS + 2)
                                act.dma_start(pair_rows[bass.ds(s * (BPS * P), BPS * P), :]
                                              .rearrange("(b p) z -> p b z", p=P), made_rows[:, :, :]
                                              ).then_inc(pair_stored, 16)

                            steps_from_first(act, STEPS, step_of)
                            act.wait_ge(pair_stored, STEPS * 16)

                    if last_too:
                        @block.scalar
                        def _(act):
                            act.dma_start(dist[:, :], A["dist"]).then_inc(dist_loaded, 16)
                            act.wait_ge(zeros_made, 2)
                            act.wait_ge(cut_step, 2)
                            act.activation(dist[:, :], dist[:, :], ACT.Sin, bias=half_pi[:, 0:1],
                                           scale=-float(np.pi) / CUTOFF).then_inc(wave, 1)
                            for k in range(NT):
                                for i, b in enumerate(range(0, NB + 1, ZB)):
                                    done = (k * ((NB + 1) // ZB) + i) * NCH // (NT * ((NB + 1) // ZB))
                                    act.wait_ge(sum_ready, CPS + done)
                                    act.dma_start(sums[k].rearrange("(p b) f -> p b f", b=NB + 1)[:, b:b + ZB, :],
                                                  zeros[:, :, :]).then_inc(zeros_stored, 16)
                            act.dma_start(table_l3[NP:NP + WIN, :],
                                          zeros[:, 0:3, :].rearrange("p k f -> p (k f)").bitcast(bf16)[:, 0:3 * MW]
                                          ).then_inc(zeros_stored, 16)
                            act.wait_ge(zeros_stored, (NT * ((NB + 1) // ZB) + 1) * 16)

                    if own_too:
                        @block.scalar
                        def _(act):
                            with act.Fori(0, STEPS) as s:
                                act.wait_ge(own_turned, s + 1)
                                act.activation(own_stage[:, :, :], h_nodes[:, bass.ds(s * BPS, BPS), :],
                                               ACT.Copy).then_inc(own_staged, 1)
                                act.wait_ge(own_turned, s + 2)
                                act.wait_ge(own_made, s + 1)
                                act.activation(own_hT[:, :], own_turned_ps[0:F, 0:BPS * P],
                                               ACT.Copy).then_inc(own_copied, 1)

                    if l0:
                        @block.scalar
                        def _(act):
                            act.sem_inc(type_kept, CPS)
                            with act.Fori(0, STEPS) as s:
                                for c in range(CPS):
                                    q = s * CPS + c
                                    act.wait_ge(rows_gathered[c], s * 64 + 64 + old)
                                    act.activation(src_type[:, bass.ds(q * 4, 4)], gathered[c][:, :, F],
                                                   ACT.Copy).then_inc(type_kept, 1)
                                    act.wait_ge(attr_added, q + 1 + CPS)
                                    act.activation(gathered[c][:, :, 0:F], gathered[c][:, :, 0:F],
                                                   ACT.Relu).then_inc(relu_done, 1)
            clear_used()
            gathered_so_far[0] += STEPS * 64
            residual_pass(layer, table, width, index_dram, scale_col)

        def residual_pass(layer, table, width, index_dram, scale_col):
            with nc.If(residual > WIN - 1):
                with ExitStack() as ctx:
                    index = sb(ctx, "res_index", [P, 4], i32)
                    rows = sb(ctx, "res_rows", [P, 4, width])
                    attr = sb(ctx, "res_attr", [P, 4 * F])
                    dst_now = sb(ctx, "res_dst", [P, 4], i32)
                    place = sb(ctx, "res_place", [P, 4])
                    beyond = sb(ctx, "res_beyond", [P, 4])
                    onehot = sb(ctx, "res_onehot", [P, 4, WIN])
                    window_sum = ps(ctx, "res_window_sum")
                    loaded = sem(ctx, "res_loaded")
                    idle = sem(ctx, "res_idle")
                    gathered = top.enter_context(nc.semaphore(f"res_gathered_p{phase[0]}"))
                    chunk_started = sem(ctx, "res_chunk_started")
                    step = sem(ctx, "res_step")
                    placed = sem(ctx, "res_placed")
                    summed = sem(ctx, "res_summed")
                    added = sem(ctx, "res_added")
                    HEAD = 5
                    with nc.Block() as block:
                        @block.sync
                        def _(sp):
                            with sp.Fori(0, NCH) as g:
                                sp.wait_ge(added, g * NB + 1)
                                sp.dma_start(index[:, :], index_dram[:, bass.ds(g * 4, 4)]).then_inc(loaded, 16)
                                sp.dma_start(attr[:, :].unsqueeze(1), A["attr48"][bass.ds(g, 1), :, :]
                                             .rearrange("c p f -> p c f")).then_inc(loaded, 16)
                                sp.dma_start(dst_now[:, :], A["dst"][:, bass.ds(g * 4, 4)]).then_inc(loaded, 16)

                        @block.scalar
                        def _(act):
                            act.sem_inc(idle, 1)

                        @block.gpsimd
                        def _(pool):
                            with pool.Fori(0, NCH) as g:
                                pool.wait_ge(loaded, g * 48 + 48)
                                pool.sem_inc(chunk_started, 1)
                                for j in range(4):
                                    pool.indirect_dma_start(
                                        rows[:, j, :], None, table,
                                        bass.IndirectOffsetOnAxis(ap=index[:, j:j + 1], axis=0)).then_inc(gathered, 16)

                        @block.vector
                        def _(dve):
                            dve.sem_inc(added, 1)
                            with dve.Fori(0, NCH) as g:
                                cols = slice(None), bass.ds(g * 4, 4)
                                dve.tensor_scalar(beyond[:, :], rel_col[cols], float(WIN), None,
                                                  ALU.is_ge).then_inc(step, 1)
                                dve.wait_ge(step, g * HEAD + 1)
                                dve.wait_ge(loaded, g * 48 + 48)
                                dve.scalar_tensor_tensor(out=place[:, :], in0=dst_now[:, :], scalar=1.0,
                                                         in1=beyond[:, :], op0=ALU.add, op1=ALU.mult).then_inc(step, 1)
                                dve.wait_ge(step, g * HEAD + 2)
                                dve.tensor_scalar(place[:, :], place[:, :], -1.0, None, ALU.add).then_inc(step, 1)
                                dve.wait_ge(gathered, g * 64 + 64)
                                if layer == 0:
                                    dve.tensor_tensor(rows[:, :, 0:F], rows[:, :, 0:F],
                                                      attr[:, :].rearrange("p (j f) -> p j f", f=F),
                                                      ALU.add).then_inc(step, 1)
                                    dve.wait_ge(step, g * HEAD + 4)
                                    dve.tensor_scalar(rows[:, :, 0:F], rows[:, :, 0:F], 0.0, None,
                                                      ALU.max).then_inc(step, 1)
                                else:
                                    dve.tensor_copy(beyond[:, :], beyond[:, :]).then_inc(step, 2)
                                with dve.Fori(0, NB) as k:
                                    dve.wait_ge(step, g * HEAD + HEAD)
                                    for j in range(4):
                                        scale = None if scale_col is None else scale_col[:, bass.ds(g * 4 + j, 1)]
                                        if scale is None:
                                            oh = dve.tensor_scalar(onehot[:, j, :], iota[:, :], place[:, j:j + 1],
                                                                   None, ALU.is_equal)
                                        else:
                                            oh = dve.tensor_scalar(onehot[:, j, :], iota[:, :], place[:, j:j + 1],
                                                                   scale, ALU.is_equal, ALU.mult)
                                    oh.then_inc(placed, 1)
                                    dve.wait_ge(placed, (g * NB + k) * 2 + 1)
                                    dve.tensor_scalar(place[:, :], place[:, :], -float(WIN), None,
                                                      ALU.add).then_inc(placed, 1)
                                    dve.wait_ge(placed, (g * NB + k) * 2 + 2)
                                    dve.wait_ge(summed, g * NB + k + 1)
                                    dve.tensor_tensor(accT[:, bass.ds(k * WIN, WIN)], accT[:, bass.ds(k * WIN, WIN)],
                                                      window_sum[0:F, 0:WIN], ALU.add).then_inc(added, 1)

                        @block.tensor
                        def _(pe):
                            with pe.Fori(0, NCH) as g:
                                with pe.Fori(0, NB) as k:
                                    pe.wait_ge(step, g * HEAD + HEAD)
                                    pe.wait_ge(placed, (g * NB + k) * 2 + 1)
                                    pe.wait_ge(added, g * NB + k + 1)
                                    for j in range(4):
                                        mm = pe.matmul(window_sum[0:F, 0:WIN], rows[:, j, 0:F], onehot[:, j, :],
                                                       start=(j == 0), stop=(j == 3))
                                    mm.then_inc(summed, 1)
                clear_used()

        def node_update(per_group, n_dve, weight=None, table=None, clear=True, norm=False):
            n_dve += CENTRE if norm else 0
            by_block = accT[:, 0:NP].rearrange("f (p b) -> f b p", b=NB)
            right = ident[0:F, 0:F] if weight is None else weight
            W = F if weight is None else 2 * F
            with ExitStack() as ctx:
                staged = [sb(ctx, f"staged{k}", [F, GB, P]) for k in range(2)]
                tmp = [sb(ctx, f"update_tmp{k}", [P, GB, F]) for k in range(2)]
                turned = [ps(ctx, f"turned{k}", [P, GB + 1, P]) for k in range(2)]
                staged_ready = sem(ctx, "staged_ready")
                turned_ready = sem(ctx, "turned_ready")
                step = sem(ctx, "update_step")
                cleared = sem(ctx, "group_cleared")
                clear_turn = sem(ctx, "clear_turn")
                stored = sem(ctx, "group_stored")
                centred = sem(ctx, "group_centred")
                squared = sem(ctx, "group_squared")
                squares_turn = sem(ctx, "squares_turn")
                with nc.Block() as block:
                    if norm:
                        @block.gpsimd
                        def _(pool):
                            with pool.Fori(0, NG) as g:
                                pool.wait_ge(step, (g + 3) * n_dve)
                                pool.sem_inc(centred, 1)
                                pool.tensor_tensor(group(w_nodes, g * GB), group(h_nodes, g * GB),
                                                   group(h_nodes, g * GB), ALU.mult).then_inc(squared, 1)

                    @block.scalar
                    def _(act):
                        with act.Fori(0, NG // 2) as s:
                            for k in range(2):
                                act.wait_ge(turned_ready, s * 2 + k + 1)
                                sums_of = by_block[:, bass.ds((s * 2 + k) * GB, GB), :]
                                act.activation(staged[k][:, :, :], sums_of, ACT.Copy).then_inc(staged_ready, 1)
                                if clear:
                                    act.wait_ge(staged_ready, s * 2 + k + 1)
                                    act.sem_inc(clear_turn, 1)
                                    act.activation(sums_of, zero_col[0:F, :].unsqueeze(2).broadcast_to([F, GB, P]),
                                                   ACT.Copy).then_inc(cleared, 1)
                        if clear:
                            act.wait_ge(cleared, NG)

                    if table is not None:
                        @block.sync
                        def _(sp):
                            rows_of = table.rearrange("(p b) f -> p b f", b=NB)
                            with sp.Fori(0, NG) as g:
                                sp.wait_ge(step, (g + 3) * n_dve)
                                sp.dma_start(rows_of[:, bass.ds(g * GB, GB), :], group(w_nodes, g * GB)
                                             ).then_inc(stored, 16)
                            sp.wait_ge(stored, NG * 16)

                    @block.tensor
                    def _(pe):
                        pe.sem_inc(turned_ready, 2)
                        with pe.Fori(0, NG // 2) as s:
                            for k in range(2):
                                pe.wait_ge(staged_ready, s * 2 + k + 1)
                                pe.wait_ge(step, (s * 2 + k + 1) * n_dve)
                                for j in range(GB):
                                    mm = pe.matmul(turned[k][:, j, 0:W], staged[k][:, j, :], right,
                                                   start=True, stop=True)
                                mm.then_inc(turned_ready, 1)

                    @block.vector
                    def _(dve):
                        dve.sem_inc(step, 2 * n_dve)

                        def reduce_squares(g):
                            dve.wait_ge(squared, g + 1)
                            dve.sem_inc(squares_turn, 1)
                            dve.tensor_reduce(stat2[:, bass.ds(g * GB, GB)], group(w_nodes, g * GB), AX.X, ALU.add)

                        def two_groups(s, first):
                            for k in range(2):
                                g = s * 2 + k
                                dve.wait_ge(turned_ready, g + 1 + 2)
                                per_group(dve, g * GB, turned[k], tmp[k], step, (g + 2) * n_dve)
                                if norm:
                                    centre(dve, g * GB, step, (g + 3) * n_dve - CENTRE)
                                    if not (first and k == 0):
                                        reduce_squares(g - 1)

                        steps_from_first(dve, NG // 2, two_groups)
                        if norm:
                            reduce_squares(NG - 1)
            clear_used()

        CENTRE = 3

        def centre(dve, b0, step, n):
            dve.wait_ge(step, n)
            dve.tensor_reduce(stat[:, bass.ds(b0, GB)], group(x_nodes, b0), AX.X, ALU.add).then_inc(step, 1)
            dve.wait_ge(step, n + 1)
            dve.tensor_scalar(stat[:, bass.ds(b0, GB)], stat[:, bass.ds(b0, GB)], -1.0 / F, None,
                              ALU.mult).then_inc(step, 1)
            dve.wait_ge(step, n + 2)
            dve.tensor_tensor(group(h_nodes, b0), group(x_nodes, b0), per_node(stat, b0), ALU.add).then_inc(step, 1)

        def scale_relu(table=None, width=F, scale=None):
            with ExitStack() as ctx:
                step = sem(ctx, "ln_step")
                root = sem(ctx, "ln_root")
                stored = sem(ctx, "ln_stored")
                halves = [slice(0, NB // 2), slice(NB // 2, NB)]
                with nc.Block() as block:
                    @block.scalar
                    def _(act):
                        act.activation(stat2[:, :], stat2[:, :], ACT.Sqrt, bias=eps_col[:, 0:1],
                                       scale=1.0 / F).then_inc(root, 1)

                    @block.vector
                    def _(dve):
                        dve.wait_ge(root, 1)
                        dve.reciprocal(stat2[:, :], stat2[:, :]).then_inc(step, 1)
                        dve.wait_ge(step, 1)
                        if table is not None:
                            if scale is None:
                                dve.tensor_copy(stat[:, :], stat2[:, :]).then_inc(step, 1)
                            else:
                                dve.tensor_tensor(stat[:, :], stat2[:, :], scale[:, :], ALU.mult).then_inc(step, 1)
                            dve.wait_ge(step, 2)
                            for at in halves:
                                dve.scalar_tensor_tensor(
                                    out=w_nodes[:, at, 0:F], in0=h_nodes[:, at, :], scalar=0.0,
                                    in1=stat[:, at].unsqueeze(2).broadcast_to([P, NB // 2, F]),
                                    op0=ALU.max, op1=ALU.mult).then_inc(step, 1)
                        for at in halves:
                            dve.scalar_tensor_tensor(
                                out=h_nodes[:, at, :], in0=h_nodes[:, at, :], scalar=0.0,
                                in1=stat2[:, at].unsqueeze(2).broadcast_to([P, NB // 2, F]),
                                op0=ALU.max, op1=ALU.mult).then_inc(step, 1)

                    if table is not None:
                        @block.sync
                        def _(sp):
                            rows_of = table.rearrange("(p b) f -> p b f", b=NB)
                            for k, at in enumerate(halves):
                                sp.wait_ge(step, 3 + k)
                                sp.dma_start(rows_of[:, at, :], w_nodes[:, at, 0:width]).then_inc(stored, 16)
                            sp.wait_ge(stored, 32)
            clear_used()

        def group(tile, b0):
            return tile[:, bass.ds(b0, GB), 0:F]

        def per_node(col, b0):
            return col[:, bass.ds(b0, GB)].unsqueeze(2).broadcast_to([P, GB, F])

        scale_relu(table_l0, TW)
        edge_pass(0, table_l0, TW, A["src"], None)
        only_l0.close()

        def update_l0(dve, b0, turned, tmp, step, n):
            dve.scalar_tensor_tensor(out=tmp[:, :, :], in0=group(h_nodes, b0), scalar=one_eps[:, 0:1],
                                     in1=turned[:, 0:GB, 0:F], op0=ALU.mult, op1=ALU.add).then_inc(step, 1)
            dve.wait_ge(step, n + 1)
            dve.tensor_tensor(group(x_nodes, b0), group(x_nodes, b0), tmp[:, :, :], ALU.add).then_inc(step, 1)

        node_update(update_l0, 2, norm=True)
        scale_relu()

        with ExitStack() as ctx:
            HI = 64
            PARTS = 3
            HB = (4, 3)
            raw = sb(ctx, "w1_raw", [P, RP, 2 * F])
            w1_parts = sb(ctx, "w1_parts", [P, PARTS, RP, 2 * F], bf16)
            w1_third = sb(ctx, "w1_third", [P, RP, 2 * F], bf16)
            w2 = sb(ctx, "w2", [2 * F, RP, 2 * F])
            bias1 = sb(ctx, "bias1", [2 * F, 1])
            ident_half = sb(ctx, "ident_half", [P, P], bf16)
            stage = [sb(ctx, f"stage{k}", [P, GB, 2, P], bf16) for k in range(2)]
            hT = [sb(ctx, f"hT{k}", [P, 2, GB * P], bf16) for k in range(2)]
            h1T = [sb(ctx, f"h1T{x}", [2 * F, RP, HB[x] * P]) for x in range(2)]
            rows = [sb(ctx, f"rel_rows{x}", [P, HB[x], NR * F]) for x in range(2)]
            hT_ps = ps(ctx, "hT_ps", [P, 2, 1024])
            h1_ps = [ps(ctx, f"h1_ps{k}") for k in range(2)]
            h2_ps = [ps(ctx, f"h2_ps{k}") for k in range(2)]
            weights = sem(ctx, "weights")
            zeroed = sem(ctx, "zeroed")
            prepared = sem(ctx, "weights_prepared")
            split = sem(ctx, "h_split")
            turned = sem(ctx, "h_turned")
            first_copied = sem(ctx, "hT0_copied")
            second_copied = sem(ctx, "hT1_copied")
            h1_ready = sem(ctx, "h1_ready")
            h1_taken = sem(ctx, "h1_taken")
            h2_ready = sem(ctx, "h2_ready")
            h2_taken = sem(ctx, "h2_taken")
            stored = [sem(ctx, f"rel_stored{x}") for x in range(2)]
            split_turn = sem(ctx, "split_turn")
            SPLIT = 5

            def pairs_of_groups(eng, body):
                for k in range(2):
                    body(k, k, k == 0, NG == 2)
                if NG > 4:
                    with eng.Fori(1, NG // 2 - 1) as s:
                        for k in range(2):
                            body(s * 2 + k, k, False, False)
                if NG > 2:
                    for k in range(2):
                        body(NG - 2 + k, k, False, True)

            with nc.Block() as block:
                @block.gpsimd
                def _(pool):
                    pool.memset(raw[:, :, :], 0.0).then_inc(zeroed, 1)
                    pool.memset(w2[:, :, :], 0.0).then_inc(zeroed, 1)
                    for k in range(2):
                        pool.memset(stage[k][:, :, :, :], 0.0).then_inc(zeroed, 1)

                @block.sync
                def _(sp):
                    sp.wait_ge(zeroed, 4)
                    for k in range(2):
                        sp.dma_start(raw[k * HI:k * HI + F, :, :], A["w1"].rearrange("i (c n) -> i c n", c=RP)
                                     ).then_inc(weights, 16)
                        sp.dma_start(w2[k * F:(k + 1) * F, :, k * F:(k + 1) * F],
                                     A["w2"].rearrange("i (c k o) -> i c k o", k=2, o=F)[:, :, k, :]
                                     ).then_inc(weights, 16)
                        sp.dma_start(bias1[k * F:(k + 1) * F, :], A["bias1"].rearrange("(f a) -> f a", a=1)
                                     ).then_inc(weights, 16)
                    table = table_l1.rearrange("(p b r) f -> p b (r f)", b=NB, r=NR)
                    with sp.Fori(0, NG) as g:
                        for x in range(2):
                            sp.wait_ge(h2_taken, g * GB + (HB[0], GB)[x] + 2)
                            sp.dma_start(table[:, bass.ds(g * GB + x * HB[0], HB[x]), :], rows[x][:, :, :]
                                         ).then_inc(stored[x], 16)
                    for x in range(2):
                        sp.wait_ge(stored[x], NG * 16)

                @block.tensor
                def _(pe):
                    def turn(g, k, first):
                        pe.wait_ge(split, g * SPLIT + SPLIT)
                        if not first:
                            pe.wait_ge(first_copied, g)
                            pe.wait_ge(second_copied, g)
                        for t in range(2):
                            for j in range(GB):
                                mm = pe.matmul(hT_ps[:, t, j * P:(j + 1) * P], stage[k][:, j, t, :], ident_half[:, :],
                                               start=True, stop=True)
                        mm.then_inc(turned, 1)

                    def h1(g, k, x):
                        pe.wait_ge(first_copied, g + 1)
                        pe.wait_ge(second_copied, g + 1)
                        cols = slice(x * HB[0] * P, (x * HB[0] + HB[x]) * P)
                        for c in range(RP):
                            pe.wait_ge(h1_taken, g * (2 * RP) + x * RP + c + 1)
                            for i in range(PARTS):
                                mm = pe.matmul(h1_ps[c % 2][0:2 * F, 0:HB[x] * P], w1_parts[:, i, c, :],
                                               hT[k][:, i // 2, cols], start=(i == 0), stop=(i == PARTS - 1))
                            mm.then_inc(h1_ready, 1)

                    def h2(g, k, x):
                        pe.wait_ge(h1_taken, g * (2 * RP) + x * RP + RP + 2)
                        for j in range(HB[x]):
                            block_no = x * HB[0] + j
                            slot = (k * GB + block_no) % 2
                            pe.wait_ge(h2_taken, g * GB + block_no + 1)
                            for c in range(RP):
                                mm = pe.matmul(h2_ps[slot][:, c * 2 * F:(c + 1) * 2 * F],
                                               h1T[x][:, c, j * P:(j + 1) * P], w2[:, c, :], start=True, stop=True)
                            mm.then_inc(h2_ready, 1)

                    pe.wait_ge(weights, 96)
                    pe.wait_ge(prepared, 8)
                    turn(0, 0, True)
                    h1(0, 0, 0)

                    def group_of(g, k, first, last):
                        more = not (last and k == 1)
                        if more:
                            turn(g + 1, 1 - k, False)
                        h1(g, k, 1)
                        h2(g, k, 0)
                        if more:
                            h1(g + 1, 1 - k, 0)
                        h2(g, k, 1)

                    pairs_of_groups(pe, group_of)

                @block.scalar
                def _(act):
                    def copy_first(g, k, first):
                        act.wait_ge(turned, g + 1)
                        if not first:
                            act.wait_ge(h1_ready, (g - 1) * (2 * RP))
                        act.activation(hT[k][:, 0, :], hT_ps[:, 0, 0:GB * P], ACT.Copy).then_inc(first_copied, 1)

                    def relu(g, x, first):
                        if not first:
                            act.wait_ge(h2_ready, (g - 1) * GB + (HB[0], GB)[x])
                        for c in range(RP):
                            act.wait_ge(h1_ready, g * (2 * RP) + x * RP + c + 1)
                            act.activation(h1T[x][:, c, :], h1_ps[c % 2][0:2 * F, 0:HB[x] * P], ACT.Relu,
                                           bias=bias1[:, 0:1]).then_inc(h1_taken, 1)

                    act.sem_inc(h1_taken, 2)
                    act.wait_ge(weights, 96)
                    copy_first(0, 0, True)
                    relu(0, 0, True)

                    def group_of(g, k, first, last):
                        more = not (last and k == 1)
                        if more:
                            copy_first(g + 1, 1 - k, first)
                        relu(g, 1, first)
                        if more:
                            relu(g + 1, 0, False)

                    pairs_of_groups(act, group_of)

                @block.vector
                def _(dve):
                    def split_h(g, k, first):
                        n = g * SPLIT
                        if not first:
                            dve.wait_ge(turned, g - 1)
                            dve.sem_inc(split_turn, 1)
                        parts = stage[k]
                        dve.tensor_copy(parts[:, :, 0, 0:F], group(h_nodes, g * GB)).then_inc(split, 1)
                        dve.tensor_copy(parts[:, :, 1, HI:HI + F], group(h_nodes, g * GB)).then_inc(split, 1)
                        dve.wait_ge(split, n + 1)
                        dve.tensor_tensor(group(w_nodes, g * GB), group(h_nodes, g * GB), parts[:, :, 0, 0:F],
                                          ALU.subtract).then_inc(split, 1)
                        dve.wait_ge(split, n + 3)
                        dve.sem_inc(split_turn, 1)
                        dve.tensor_copy(parts[:, :, 0, HI:HI + F], group(w_nodes, g * GB)).then_inc(split, 1)
                        dve.wait_ge(split, n + 4)
                        dve.tensor_tensor(parts[:, :, 1, 0:F], group(w_nodes, g * GB), parts[:, :, 0, HI:HI + F],
                                          ALU.subtract).then_inc(split, 1)

                    def copy_second(g, k, first):
                        dve.wait_ge(turned, g + 1)
                        if not first:
                            dve.wait_ge(h1_ready, (g - 1) * (2 * RP))
                        dve.tensor_copy(hT[k][:, 1, :], hT_ps[:, 1, 0:GB * P]).then_inc(second_copied, 1)

                    def rows_of(g, k, x, first):
                        if not first:
                            dve.wait_ge(stored[x], g * 16)
                        for j in range(HB[x]):
                            block_no = x * HB[0] + j
                            dve.wait_ge(h2_ready, g * GB + block_no + 1)
                            dve.tensor_copy(rows[x][:, j, :], h2_ps[(k * GB + block_no) % 2][:, 0:NR * F]
                                            ).then_inc(h2_taken, 1)

                    dve.sem_inc(h2_taken, 2)
                    dve.tensor_copy(ident_half[:, :], ident[:, :]).then_inc(prepared, 1)
                    dve.wait_ge(zeroed, 4)
                    split_h(0, 0, True)
                    split_h(1, 1, True)
                    dve.wait_ge(weights, 96)
                    dve.tensor_copy(w1_parts[:, 0, :, :], raw[:, :, :]).then_inc(prepared, 1)
                    dve.wait_ge(prepared, 2)
                    dve.tensor_tensor(raw[:, :, :], raw[:, :, :], w1_parts[:, 0, :, :], ALU.subtract).then_inc(prepared, 1)
                    dve.wait_ge(prepared, 3)
                    dve.tensor_copy(w1_parts[:, 1, :, :], raw[:, :, :]).then_inc(prepared, 1)
                    dve.wait_ge(prepared, 4)
                    dve.tensor_tensor(w1_third[:, :, :], raw[:, :, :], w1_parts[:, 1, :, :],
                                      ALU.subtract).then_inc(prepared, 1)
                    dve.wait_ge(prepared, 5)
                    dve.tensor_copy(w1_parts[0:HI, 2, :, :], w1_parts[0:HI, 0, :, :]).then_inc(prepared, 1)
                    dve.tensor_copy(w1_parts[HI:P, 2, :, :], w1_third[HI:P, :, :]).then_inc(prepared, 2)
                    copy_second(0, 0, True)

                    def group_of(g, k, first, last):
                        if not last:
                            split_h(g + 2, k, False)
                        if not (last and k == 1):
                            copy_second(g + 1, 1 - k, first)
                        for x in range(2):
                            rows_of(g, k, x, first)

                    pairs_of_groups(dve, group_of)
        clear_used()
        edge_pass(1, table_l1, F, src_rel, edge_scale, rows_too=True)

        def update_l1(dve, b0, turned, tmp, step, n):
            dve.tensor_tensor(tmp[:, :, :], turned[:, 0:GB, 0:F], bias2[:, :].unsqueeze(1).broadcast_to([P, GB, F]),
                              ALU.add).then_inc(step, 1)
            dve.wait_ge(step, n + 1)
            dve.scalar_tensor_tensor(out=group(x_nodes, b0), in0=tmp[:, :, :], scalar=0.0,
                                     in1=group(x_nodes, b0), op0=ALU.max, op1=ALU.add).then_inc(step, 1)

        node_update(update_l1, 2, norm=True)

        scale_relu(table_l2, F, inv_root)
        for k in (1, 2, 3):
            edge_pass(2, table_l2, F, A["src"], other_end, logits_too=(k == 1), last_too=(k == 2), own_too=(k == 3))

            def update_l2(dve, b0, turned, tmp, step, n):
                if k == 1:
                    dve.tensor_tensor(group(w_nodes, b0), turned[:, 0:GB, 0:F], per_node(minus_sq, b0),
                                      ALU.mult).then_inc(step, 1)
                    n = n + 1
                elif k == 2:
                    dve.tensor_tensor(tmp[:, :, :], turned[:, 0:GB, 0:F], per_node(minus, b0), ALU.mult).then_inc(step, 1)
                    dve.wait_ge(step, n + 1)
                    dve.scalar_tensor_tensor(out=tmp[:, :, :], in0=tmp[:, :, :], scalar=2.0,
                                             in1=group(h_nodes, b0), op0=ALU.mult,
                                             op1=ALU.subtract).then_inc(step, 1)
                    dve.wait_ge(step, n + 2)
                    dve.tensor_tensor(group(w_nodes, b0), tmp[:, :, :], per_node(inv_root, b0),
                                      ALU.mult).then_inc(step, 1)
                    dve.wait_ge(step, n + 3)
                    n = n + 3
                dve.tensor_tensor(tmp[:, :, :], turned[:, 0:GB, F:2 * F], per_node(minus, b0), ALU.mult).then_inc(step, 1)
                dve.wait_ge(step, n + 1)
                dve.tensor_tensor(group(x_nodes, b0), group(x_nodes, b0), tmp[:, :, :], ALU.add).then_inc(step, 1)

            node_update(update_l2, (3, 5, 2)[k - 1], weight=cheb[:, k - 1, :],
                        table=table_l2 if k < 3 else None, clear=k < 3, norm=k == 3)
        agg.close()

        layer3 = ExitStack()
        top.enter_context(layer3)
        w1 = sb(layer3, "filter_w1", [2 * R, 2 * F])
        b1 = sb(layer3, "filter_b1", [2 * F, 1])
        w2 = sb(layer3, "filter_w2", [2 * F + 1, 2 * F])
        gamma = sb(layer3, "gamma", [P, F])
        beta = sb(layer3, "beta", [P, F])
        hidden = [sb(layer3, f"hidden{k}", [2 * F + 1, 256]) for k in range(2)]
        with ExitStack() as ctx:
            PIECES = NB // (2 * GB)

            def piece(i):
                return slice(i * 2 * GB, (i + 1) * 2 * GB)

            mult = sb(ctx, "mult", [P, NB])
            parts = sb(ctx, "parts", [P, NB, 3, MW], bf16)
            small = sem(ctx, "small_loaded")
            mult_loaded = sem(ctx, "mult_loaded")
            consts = sem(ctx, "l3_consts")
            rows_made = sem(ctx, "l3_rows_made")
            first_made = sem(ctx, "first_part_made")
            rest_made = sem(ctx, "rest_made")
            second_made = sem(ctx, "second_part_made")
            third_made = sem(ctx, "third_part_made")
            recip = sem(ctx, "l3_reciprocal")
            root = sem(ctx, "l3_root")
            stored = sem(ctx, "l3_stored")
            with nc.Block() as block:
                @block.sync
                def _(sp):
                    sp.dma_start(mult[:, :], A["node_vec"]).then_inc(mult_loaded, 16)
                    for tile, what in ((gamma[:, :], A["gamma"].broadcast_to([P, F])),
                                       (beta[:, :], A["beta"].broadcast_to([P, F]))):
                        sp.dma_start(tile, what).then_inc(small, 16)
                    sp.wait_ge(consts, 4)
                    for k in range(2):
                        out_cols = slice(k * F, (k + 1) * F)
                        for tile, what in ((w1[k * R:(k + 1) * R, out_cols], A["fw1_t"]),
                                           (w2[k * F:(k + 1) * F, out_cols], A["fw2_t"]),
                                           (w2[2 * F:2 * F + 1, out_cols], A["fb2"]),
                                           (b1[k * F:(k + 1) * F, :], A["fb1"])):
                            sp.dma_start(tile, what).then_inc(small, 16)
                    rows_of = table_l3[0:NP, :].rearrange("(p b) f -> p b f", b=NB)
                    for i in range(PIECES):
                        at = piece(i)
                        sp.wait_ge(third_made, i + 1)
                        sp.dma_start(rows_of[:, at, :], parts[:, at, :, :].rearrange("p b k f -> p b (k f)")
                                     ).then_inc(stored, 16)
                    sp.wait_ge(stored, PIECES * 16)
                    sp.wait_ge(small, 160)

                @block.gpsimd
                def _(pool):
                    pool.memset(w1[:, :], 0.0).then_inc(consts, 1)
                    pool.memset(w2[:, :], 0.0).then_inc(consts, 1)
                    for k in range(2):
                        pool.memset(hidden[k][:, :], 1.0).then_inc(consts, 1)

                @block.scalar
                def _(act):
                    act.activation(stat2[:, :], stat2[:, :], ACT.Sqrt, bias=eps_col[:, 0:1],
                                   scale=1.0 / F).then_inc(root, 1)
                    for i in range(PIECES + 1):
                        if i < PIECES:
                            act.wait_ge(rows_made, i + 1)
                            act.activation(parts[:, piece(i), 0, :], w_nodes[:, piece(i), 0:MW],
                                           ACT.Copy).then_inc(first_made, 1)
                        if i >= 1:
                            act.wait_ge(rest_made, i)
                            act.activation(parts[:, piece(i - 1), 1, :], w_nodes[:, piece(i - 1), 0:MW],
                                           ACT.Copy).then_inc(second_made, 1)

                @block.vector
                def _(dve):
                    def normalised(out, i):
                        return dve.scalar_tensor_tensor(
                            out=out[:, piece(i), 0:F], in0=h_nodes[:, piece(i), :], scalar=0.0,
                            in1=stat2[:, piece(i)].unsqueeze(2).broadcast_to([P, 2 * GB, F]), op0=ALU.max, op1=ALU.mult)

                    dve.wait_ge(mult_loaded, 16)
                    dve.tensor_copy(w_nodes[:, :, F], mult[:, :]).then_inc(recip, 1)
                    dve.wait_ge(root, 1)
                    dve.reciprocal(stat2[:, :], stat2[:, :]).then_inc(recip, 1)
                    dve.wait_ge(recip, 2)
                    for i in range(PIECES + 2):
                        if i < PIECES:
                            normalised(w_nodes, i).then_inc(rows_made, 1)
                        if 1 <= i <= PIECES:
                            rest = w_nodes[:, piece(i - 1), 0:MW]
                            dve.wait_ge(first_made, i)
                            dve.tensor_tensor(rest, rest, parts[:, piece(i - 1), 0, :],
                                              ALU.subtract).then_inc(rest_made, 1)
                        if i >= 2:
                            at = piece(i - 2)
                            dve.wait_ge(second_made, i - 1)
                            dve.tensor_tensor(parts[:, at, 2, :], w_nodes[:, at, 0:MW], parts[:, at, 1, :],
                                              ALU.subtract).then_inc(third_made, 1)
                    for i in range(PIECES):
                        normalised(h_nodes, i)
        clear_used()

        def by_tile(col):
            return col.unsqueeze(2).broadcast_to([P, 4, P])

        with ExitStack() as ctx:
            index = [sb(ctx, f"row_index{h}", [P, HC * 4], i32) for h in range(2)]
            attr_t = [sb(ctx, f"attr_t{h}", [2 * R, HC, 256]) for h in range(2)]
            src_b = [sb(ctx, f"src_b{h}", [P, HC, 512], i32) for h in range(2)]
            dst_b = [sb(ctx, f"dst_b{h}", [P, HC, 512], i32) for h in range(2)]
            window = [sb(ctx, f"window{k}", [WIN, 3 * MW], bf16) for k in range(4)]
            turned_hot = [sb(ctx, f"turned_hot{k}", [WIN, 512], bf16) for k in range(2)]
            same = [sb(ctx, f"same{k}", [P, 4, P], bf16) for k in range(2)]
            rows = [sb(ctx, f"dst_rows{k}", [P, 4, MW]) for k in range(2)]
            weight = [sb(ctx, f"weight{k}", [P, 4]) for k in range(2)]
            msg = [sb(ctx, f"msg{k}", [P, 4, MW]) for k in range(2)]
            part = [[sb(ctx, f"msg{k}_part{i}", [P, 4, MW], bf16) for i in range(3)] for k in range(2)]
            summed = [sb(ctx, f"summed{k}", [P, 4, MW]) for k in range(4)]
            hid_ps = [ps(ctx, f"hid_ps{k}") for k in range(2)]
            gate_ps = [ps(ctx, f"gate_ps{k}") for k in range(2)]
            rows_ps = [ps(ctx, f"rows_ps{k}") for k in range(2)]
            sum_ps = [ps(ctx, f"sum_ps{k}") for k in range(2)]
            index_loaded = [sem(ctx, f"index_loaded{h}") for h in range(2)]
            attr_loaded = [sem(ctx, f"attr_loaded{h}") for h in range(2)]
            src_loaded = [sem(ctx, f"src_loaded{h}") for h in range(2)]
            dst_loaded = [sem(ctx, f"dst_loaded{h}") for h in range(2)]
            window_loaded = [sem(ctx, f"window_loaded{k}") for k in range(4)]
            hid_made = sem(ctx, "hid_made")
            silu_done = sem(ctx, "silu_done")
            gate_made = sem(ctx, "gate_made")
            turned_ready = sem(ctx, "turned_ready")
            rows_found = sem(ctx, "rows_found")
            rows_ready = sem(ctx, "rows_ready")
            same_made = sem(ctx, "same_made")
            step = sem(ctx, "msg_step")
            msg_made = sem(ctx, "msg_made")
            high_made = sem(ctx, "high_made")
            rest_made = sem(ctx, "rest_made")
            mid_made = sem(ctx, "mid_made")
            low_made = sem(ctx, "low_made")
            sums_made = sem(ctx, "sums_made")
            summed_ready = sem(ctx, "summed_ready")
            scattered = [slot_scattered[0:2], slot_scattered[2:4]]
            dma_turn = sem(ctx, "dma_turn")
            D = 3

            def pipelined_steps(eng, body):
                body(0, True, False)
                with eng.Fori(1, STEPS - 1) as s:
                    body(s, False, False)
                body(STEPS - 1, False, True)

            def ahead(stage, s, c, n, last):
                if not (last and c + n >= CPS):
                    stage(s + (c + n) // CPS, (c + n) % CPS)

            def behind(stage, s, c, first):
                if c > 0:
                    stage(s, c - 1, first)
                elif not first:
                    stage(s - 1, CPS - 1, False)

            with nc.Block() as block:
                @block.sync
                def _(sp):
                    def step_of(s, first):
                        for h in range(2):
                            sp.wait_ge(hid_made, s * CPS + HC * (h + 1))
                            sp.dma_start(attr_t[h][:, :, :],
                                         A["ea_t"][bass.ds((s * 2 + h) * HC, HC), :, :]
                                         .rearrange("c r e -> r c e")).then_inc(attr_loaded[h], 16)
                            sp.wait_ge(turned_ready, s * CPS + HC * (h + 1))
                            sp.dma_start(dst_b[h][:, :, :], A["dst_lines"][bass.ds((s * 2 + h) * HC, HC), :]
                                         .unsqueeze(0).broadcast_to([P, HC, 512])).then_inc(dst_loaded[h], 16)
                            sp.wait_ge(same_made, s * CPS + HC * (h + 1))
                            sp.dma_start(src_b[h][:, :, :], A["src_lines"][bass.ds((s * 2 + h) * HC, HC), :]
                                         .unsqueeze(0).broadcast_to([P, HC, 512])).then_inc(src_loaded[h], 16)
                            for c in range(HC * h, HC * (h + 1)):
                                q = s * CPS + c
                                base = sp.value_load(base_int[0:1, bass.ds(q, 1)], min_val=0, max_val=NP)
                                sp.wait_ge(rows_found, q + 1)
                                sp.dma_start(window[c % 4][:, :], table_l3[bass.ds(base, WIN), :]
                                             ).then_inc(window_loaded[c % 4], 16)
                            if not first:
                                for k in range(4):
                                    sp.wait_ge(slot_scattered[k], s * 128 - 64 + h * 64)
                            sp.dma_start(index[h][:, :], sum_rows[:, bass.ds((s * 2 + h) * (HC * 4), HC * 4)]
                                         ).then_inc(index_loaded[h], 16)

                    steps_from_first(sp, STEPS, step_of)

                @block.gpsimd
                def _(pool):
                    def step_of(s, first):
                        for c in range(CPS):
                            if c % HC == 0:
                                pool.wait_ge(index_loaded[c // HC], s * 16 + 16)
                            pool.wait_ge(summed_ready, s * CPS + c + 1 + 2)
                            for j in range(4):
                                if j % 2 == 0:
                                    if not (first and c < 2):
                                        pool.wait_ge(scattered[c % 2][j // 2], s * 128 + (c // 2) * 32)
                                    pool.sem_inc(dma_turn, 1)
                                t = (c % HC) * 4 + j
                                pool.indirect_dma_start(
                                    sums[(c % 2) * 4 + j],
                                    bass.IndirectOffsetOnAxis(ap=index[c // HC][:, t:t + 1], axis=0),
                                    summed[c % 4][:, j, :], None, compute_op=ALU.add,
                                ).then_inc(scattered[c % 2][j // 2], 16)

                    steps_from_first(pool, STEPS, step_of)
                    for k in range(4):
                        pool.wait_ge(slot_scattered[k], STEPS * 128)

                @block.tensor
                def _(pe):
                    pe.sem_inc(hid_made, CPS)
                    pe.sem_inc(gate_made, 2)
                    pe.sem_inc(sums_made, 2)
                    pe.sem_inc(rows_found, 4)

                    def hid(s, c):
                        q = s * CPS + c
                        pe.wait_ge(attr_loaded[c // HC], s * 16 + 16)
                        pe.wait_ge(silu_done, q + 1)
                        pe.matmul(hid_ps[c % 2][0:2 * F, 0:256], w1[:, :], attr_t[c // HC][:, c % HC, :],
                                  start=True, stop=True).then_inc(hid_made, 1)

                    def rows_of(s, c):
                        q = s * CPS + c
                        pe.wait_ge(turned_ready, q + 1 + CPS)
                        pe.wait_ge(window_loaded[c % 4], s * 32 + (c // 4) * 16 + 16)
                        pe.wait_ge(rows_ready, q + 1)
                        for j in range(4):
                            for i in range(3):
                                mm = pe.matmul(rows_ps[c % 2][:, j * MW:(j + 1) * MW],
                                               turned_hot[c % 2][:, j * P:(j + 1) * P],
                                               window[c % 4][:, i * MW:(i + 1) * MW], start=(i == 0), stop=(i == 2))
                        mm.then_inc(rows_found, 1)

                    def gate(s, c):
                        q = s * CPS + c
                        pe.wait_ge(silu_done, q + 1 + 2)
                        pe.wait_ge(msg_made, q + 1)
                        for e in range(2):
                            mm = pe.matmul(gate_ps[c % 2][:, e * 2 * F:(e + 1) * 2 * F], hidden[c % 2][:, e * P:(e + 1) * P],
                                           w2[:, :], start=True, stop=True)
                        mm.then_inc(gate_made, 1)

                    def totals(s, c, first):
                        q = s * CPS + c
                        pe.wait_ge(same_made, q + 1 + CPS)
                        pe.wait_ge(low_made, q + 1)
                        pe.wait_ge(summed_ready, q + 1)
                        for j in range(4):
                            for i in range(3):
                                mm = pe.matmul(sum_ps[c % 2][:, j * MW:(j + 1) * MW], same[c % 2][:, j, :],
                                               part[c % 2][i][:, j, :], start=(i == 0), stop=(i == 2))
                        mm.then_inc(sums_made, 1)

                    hid(0, 0)
                    hid(0, 1)
                    rows_of(0, 0)
                    gate(0, 0)

                    def step_of(s, first, last):
                        for c in range(CPS):
                            ahead(hid, s, c, 2, last)
                            ahead(rows_of, s, c, 1, last)
                            ahead(gate, s, c, 1, last)
                            behind(totals, s, c, first)

                    pipelined_steps(pe, step_of)
                    totals(STEPS - 1, CPS - 1, False)

                @block.scalar
                def _(act):
                    act.sem_inc(silu_done, 2)
                    act.sem_inc(summed_ready, 2)
                    act.sem_inc(rows_ready, 2)

                    def silu(s, c):
                        q = s * CPS + c
                        act.wait_ge(hid_made, q + 1 + CPS)
                        act.wait_ge(gate_made, q + 1)
                        act.activation(hidden[c % 2][0:2 * F, :], hid_ps[c % 2][0:2 * F, 0:256], ACT.Silu,
                                       bias=b1[:, 0:1]).then_inc(silu_done, 1)

                    def rows_of(s, c):
                        q = s * CPS + c
                        act.wait_ge(rows_found, q + 1 + 4)
                        act.wait_ge(msg_made, q + 1)
                        act.activation(rows[c % 2][:, :, :].rearrange("p j f -> p (j f)"),
                                       rows_ps[c % 2][:, 0:4 * MW], ACT.Copy).then_inc(rows_ready, 1)

                    def take_sums(s, c, first):
                        q = s * CPS + c
                        act.wait_ge(sums_made, q + 1 + 2)
                        if not (first and c < 4):
                            for i in range(2):
                                act.wait_ge(scattered[c % 2][i], s * 128 + (c // 2) * 32 - 32)
                        act.activation(summed[c % 4][:, :, :].rearrange("p j f -> p (j f)"),
                                       sum_ps[c % 2][:, 0:4 * MW], ACT.Copy).then_inc(summed_ready, 1)

                    silu(0, 0)
                    silu(0, 1)
                    rows_of(0, 0)

                    def step_of(s, first, last):
                        for c in range(CPS):
                            q = s * CPS + c
                            k = c % 2
                            ahead(rows_of, s, c, 1, last)
                            act.wait_ge(msg_made, q + 1 + 2)
                            act.wait_ge(sums_made, q + 1)
                            act.activation(part[k][0][:, :, :], msg[k][:, :, :], ACT.Copy).then_inc(high_made, 1)
                            ahead(silu, s, c, 2, last)
                            act.wait_ge(rest_made, q + 1)
                            act.activation(part[k][1][:, :, :], msg[k][:, :, :], ACT.Copy).then_inc(mid_made, 1)
                            behind(take_sums, s, c, first)

                    pipelined_steps(act, step_of)
                    take_sums(STEPS - 1, CPS - 1, False)

                @block.vector
                def _(dve):
                    dve.sem_inc(same_made, CPS)
                    dve.sem_inc(turned_ready, CPS)
                    dve.sem_inc(msg_made, 2)

                    def turned_onehot(s, c):
                        q = s * CPS + c
                        dve.wait_ge(dst_loaded[c // HC], s * 16 + 16)
                        dve.wait_ge(rows_found, q + 1 + 4 - 2)
                        dve.tensor_scalar(turned_hot[c % 2][:, :], dst_b[c // HC][:, c % HC, :],
                                          window_part[:, bass.ds(q, 1)], None, ALU.is_equal).then_inc(turned_ready, 1)

                    def same_source(s, c):
                        q = s * CPS + c
                        dve.wait_ge(src_loaded[c // HC], s * 16 + 16)
                        dve.wait_ge(sums_made, q + 1)
                        dve.tensor_tensor(same[c % 2][:, :, :],
                                          src_b[c // HC][:, c % HC, :].rearrange("p (j e) -> p j e", e=P),
                                          by_tile(src_cols[:, bass.ds(q * 4, 4)]), ALU.is_equal).then_inc(same_made, 1)

                    turned_onehot(0, 0)
                    turned_onehot(0, 1)
                    same_source(0, 0)

                    def step_of(s, first, last):
                        for c in range(CPS):
                            q = s * CPS + c
                            k = c % 2
                            n = q * D
                            dve.wait_ge(rows_ready, q + 1 + 2)
                            dve.wait_ge(sums_made, q + 1)
                            dve.tensor_tensor(weight[k][:, :], edge_scale[:, bass.ds(q * 4, 4)], rows[k][:, :, F],
                                              ALU.mult).then_inc(step, 1)
                            dve.tensor_copy(msg[k][:, :, F], rows[k][:, :, F]).then_inc(step, 1)
                            dve.wait_ge(gate_made, q + 1 + 2)
                            for j in range(4):
                                at = ((j % 2) * 2 + j // 2) * F
                                got = dve.scalar_tensor_tensor(out=msg[k][:, j, 0:F], in0=gate_ps[k][:, at:at + F],
                                                               scalar=logit_all[:, bass.ds(q * 4 + j, 1)],
                                                               in1=rows[k][:, j, 0:F], op0=ALU.add, op1=ALU.mult)
                            got.then_inc(step, 1)
                            dve.wait_ge(step, n + D)
                            dve.tensor_tensor(msg[k][:, :, 0:F], msg[k][:, :, 0:F],
                                              weight[k][:, :].unsqueeze(2).broadcast_to([P, 4, F]),
                                              ALU.mult).then_inc(msg_made, 1)
                            ahead(turned_onehot, s, c, 2, last)
                            dve.wait_ge(high_made, q + 1)
                            dve.tensor_tensor(msg[k][:, :, :], msg[k][:, :, :], part[k][0][:, :, :],
                                              ALU.subtract).then_inc(rest_made, 1)
                            ahead(same_source, s, c, 1, last)
                            dve.wait_ge(mid_made, q + 1)
                            dve.tensor_tensor(part[k][2][:, :, :], msg[k][:, :, :], part[k][1][:, :, :],
                                              ALU.subtract).then_inc(low_made, 1)

                    pipelined_steps(dve, step_of)
        clear_used()

        with nc.If(residual > WIN - 1):
            with ExitStack() as ctx:
                row_index = sb(ctx, "res_row_index", [P, 4], i32)
                dst_now = sb(ctx, "res_dst", [P, 4], i32)
                attr_t = sb(ctx, "res_attr_t", [2 * R, 256])
                src_b = sb(ctx, "res_src_b", [P, 4, P], i32)
                base_b = sb(ctx, "res_base_b", [P, NCH])
                row_parts = sb(ctx, "res_row_parts", [P, 4, 3 * MW], bf16)
                rows = sb(ctx, "res_rows", [P, 4, MW])
                pair = sb(ctx, "res_pair", [P, 4, NZ])
                beyond = sb(ctx, "res_beyond", [P, 4])
                far = sb(ctx, "res_far", [P, 4])
                logit = sb(ctx, "res_logit", [P, 4])
                junk = sb(ctx, "res_junk", [P, 4, P])
                same = sb(ctx, "res_same", [P, 4, P])
                msg = sb(ctx, "res_msg", [P, 4, MW])
                summed = sb(ctx, "res_summed", [P, 4, MW])
                hid_ps = ps(ctx, "res_hid_ps")
                gate_ps = ps(ctx, "res_gate_ps")
                sum_ps = ps(ctx, "res_sum_ps")
                loaded = sem(ctx, "res_loaded")
                base_loaded = sem(ctx, "res_base_loaded")
                gathered = top.enter_context(nc.semaphore("res_l3_gathered"))
                scattered = top.enter_context(nc.semaphore("res_l3_scattered"))
                chunk_started = sem(ctx, "res_chunk_started")
                silu_done = sem(ctx, "res_silu_done")
                products = sem(ctx, "res_products")
                step = sem(ctx, "res_step")
                summed_ready = sem(ctx, "res_summed_ready")
                chunk_over = sem(ctx, "res_chunk_over")
                D = 10
                with nc.Block() as block:
                    @block.sync
                    def _(sp):
                        sp.dma_start(base_b[:, :], base_row.broadcast_to([P, NCH])).then_inc(base_loaded, 16)
                        with sp.Fori(0, NCH) as g:
                            sp.wait_ge(chunk_over, g + 1)
                            sp.dma_start(row_index[:, :], sum_rows[:, bass.ds(g * 4, 4)]).then_inc(loaded, 16)
                            sp.dma_start(dst_now[:, :], A["dst"][:, bass.ds(g * 4, 4)]).then_inc(loaded, 16)
                            sp.dma_start(attr_t[:, :], A["ea_t"][bass.ds(g, 1), :, :]
                                         .rearrange("a r e -> (a r) e")).then_inc(loaded, 16)
                            sp.dma_start(src_b[:, :, :].rearrange("p j e -> p (j e)"),
                                         A["src_lines"][bass.ds(g, 1), :].broadcast_to([P, 512])).then_inc(loaded, 16)

                    @block.gpsimd
                    def _(pool):
                        pool.sem_inc(chunk_over, 1)
                        with pool.Fori(0, NCH) as g:
                            pool.wait_ge(loaded, g * 64 + 64)
                            pool.sem_inc(chunk_started, 1)
                            for j in range(4):
                                pool.indirect_dma_start(
                                    row_parts[:, j, :], None, table_l3,
                                    bass.IndirectOffsetOnAxis(ap=dst_now[:, j:j + 1], axis=0)).then_inc(gathered, 16)
                                pool.indirect_dma_start(
                                    pair[:, j, :], None, pair_rows,
                                    bass.IndirectOffsetOnAxis(ap=dst_now[:, j:j + 1], axis=0)).then_inc(gathered, 16)
                            pool.wait_ge(summed_ready, g + 1)
                            pool.sem_inc(chunk_started, 1)
                            for j in range(4):
                                pool.indirect_dma_start(
                                    sums[j], bass.IndirectOffsetOnAxis(ap=row_index[:, j:j + 1], axis=0),
                                    summed[:, j, :], None, compute_op=ALU.add).then_inc(scattered, 16)
                            pool.wait_ge(scattered, g * 64 + 64)
                            pool.sem_inc(chunk_over, 1)

                    @block.tensor
                    def _(pe):
                        with pe.Fori(0, NCH) as g:
                            pe.wait_ge(loaded, g * 64 + 64)
                            pe.sem_inc(chunk_started, 1)
                            pe.matmul(hid_ps[0:2 * F, 0:256], w1[:, :], attr_t[:, :], start=True, stop=True
                                      ).then_inc(products, 1)
                            pe.wait_ge(silu_done, g + 1)
                            for e in range(2):
                                mm = pe.matmul(gate_ps[:, e * 2 * F:(e + 1) * 2 * F], hidden[0][:, e * P:(e + 1) * P],
                                               w2[:, :], start=True, stop=True)
                            mm.then_inc(products, 1)
                            pe.wait_ge(step, g * D + D)
                            for j in range(4):
                                mm = pe.matmul(sum_ps[:, j * MW:(j + 1) * MW], same[:, j, :], msg[:, j, :],
                                               start=True, stop=True)
                            mm.then_inc(products, 1)

                    @block.scalar
                    def _(act):
                        with act.Fori(0, NCH) as g:
                            act.wait_ge(products, g * 3 + 1)
                            act.activation(hidden[0][0:2 * F, :], hid_ps[0:2 * F, 0:256], ACT.Silu,
                                           bias=b1[:, 0:1]).then_inc(silu_done, 1)
                            act.wait_ge(products, g * 3 + 3)
                            act.activation(summed[:, :, :].rearrange("p j f -> p (j f)"), sum_ps[:, 0:4 * MW],
                                           ACT.Copy).then_inc(summed_ready, 1)

                    @block.vector
                    def _(dve):
                        dve.wait_ge(base_loaded, 16)
                        with dve.Fori(0, NCH) as g:
                            n = g * D
                            cols = slice(None), bass.ds(g * 4, 4)
                            dve.wait_ge(loaded, g * 64 + 64)
                            dve.tensor_scalar(far[:, :], dst_now[:, :], base_b[:, bass.ds(g, 1)], float(WIN),
                                              ALU.subtract, ALU.is_ge).then_inc(step, 1)
                            dve.tensor_tensor(same[:, :, :], src_b[:, :, :], by_tile(src_cols[cols]),
                                              ALU.is_equal).then_inc(step, 1)
                            dve.wait_ge(gathered, g * 128 + 128)
                            for j in range(4):
                                got = dve.scalar_tensor_tensor(out=junk[:, j, 0:NZ], in0=iota[:, 0:NZ],
                                                               scalar=src_type[:, bass.ds(g * 4 + j, 1)],
                                                               in1=pair[:, j, :], op0=ALU.is_equal, op1=ALU.mult,
                                                               accum_out=logit[:, j:j + 1])
                            got.then_inc(step, 1)
                            dve.tensor_tensor(rows[:, :, :], row_parts[:, :, 0:MW], row_parts[:, :, MW:2 * MW],
                                              ALU.add).then_inc(step, 1)
                            dve.wait_ge(step, n + 4)
                            dve.tensor_tensor(rows[:, :, :], rows[:, :, :], row_parts[:, :, 2 * MW:3 * MW],
                                              ALU.add).then_inc(step, 1)
                            dve.wait_ge(step, n + 5)
                            dve.tensor_tensor(msg[:, :, F], rows[:, :, F], far[:, :], ALU.mult).then_inc(step, 1)
                            dve.wait_ge(step, n + 6)
                            dve.tensor_tensor(beyond[:, :], edge_scale[cols], msg[:, :, F], ALU.mult).then_inc(step, 1)
                            dve.wait_ge(products, g * 3 + 2)
                            for j in range(4):
                                at = ((j % 2) * 2 + j // 2) * F
                                got = dve.scalar_tensor_tensor(out=msg[:, j, 0:F], in0=gate_ps[:, at:at + F],
                                                               scalar=logit[:, j:j + 1], in1=rows[:, j, 0:F],
                                                               op0=ALU.add, op1=ALU.mult)
                            got.then_inc(step, 1)
                            dve.wait_ge(step, n + 8)
                            dve.tensor_tensor(msg[:, :, 0:F], msg[:, :, 0:F],
                                              beyond[:, :].unsqueeze(2).broadcast_to([P, 4, F]),
                                              ALU.mult).then_inc(step, 2)
            clear_used()

        with ExitStack() as ctx:
            part_sum = [sb(ctx, f"part_sum{k}", [P, NT, GB, MW]) for k in range(2)]
            total = [sb(ctx, f"total{k}", [P, GB, MW]) for k in range(2)]
            x3 = [sb(ctx, f"x3_{k}", [P, GB, F]) for k in range(2)]
            square = [sb(ctx, f"square{k}", [P, GB, F]) for k in range(2)]
            mean = [sb(ctx, f"mean{k}", [P, GB]) for k in range(2)]
            dev = [sb(ctx, f"dev{k}", [P, GB]) for k in range(2)]
            loaded = [sem(ctx, f"part_loaded{k}") for k in range(2)]
            half_added = sem(ctx, "half_added")
            step = sem(ctx, "centre_step")
            squared = sem(ctx, "squared")
            reduced = sem(ctx, "reduced")
            root = sem(ctx, "root")
            normed = sem(ctx, "normed")
            final = sem(ctx, "final")
            turn = sem(ctx, "final_turn")
            stored = sem(ctx, "out_stored")
            CS = 10

            def two_per_step(eng, body):
                steps = NG // 2
                for k in range(2):
                    body(0, k, True, steps == 1)
                if steps > 2:
                    with eng.Fori(1, steps - 1) as s:
                        for k in range(2):
                            body(s, k, False, False)
                if steps > 1:
                    for k in range(2):
                        body(steps - 1, k, False, True)

            row = lambda t: t[:, :].unsqueeze(1).broadcast_to([P, GB, F])
            each = lambda col: col[:, :].unsqueeze(2).broadcast_to([P, GB, F])
            with nc.Block() as block:
                @block.sync
                def _(sp):
                    def load(s, k, first, last):
                        g = s * 2 + k
                        if not first:
                            sp.wait_ge(step, (g - 2) * CS + 3)
                        for i in range(NT):
                            sp.dma_start(part_sum[k][:, i, :, :],
                                         sums[i][0:NP, :].rearrange("(p b) f -> p b f", b=NB)[:, bass.ds(g * GB, GB), :]
                                         ).then_inc(loaded[k], 16)

                    two_per_step(sp, load)

                @block.gpsimd
                def _(pool):
                    def scale_shift_add(g, k):
                        h, x = x3[k][:, :, :], group(x_nodes, g * GB)
                        pool.wait_ge(normed, g * 2 + 2)
                        pool.tensor_tensor(h, h, row(gamma), ALU.mult).then_inc(final, 1)
                        pool.wait_ge(final, g * 3 + 1)
                        pool.tensor_tensor(h, h, row(beta), ALU.add).then_inc(final, 1)
                        pool.wait_ge(final, g * 3 + 2)
                        pool.sem_inc(turn, 1)
                        pool.tensor_tensor(x, x, h, ALU.add).then_inc(final, 1)

                    def add_half(s, k):
                        quarters = part_sum[k][:, :, :, :].rearrange("p (q i) b f -> p q (i b f)", q=4)
                        pool.wait_ge(loaded[k], s * (NT * 16) + NT * 16)
                        pool.tensor_tensor(quarters[:, 1, :], quarters[:, 1, :], quarters[:, 3, :],
                                           ALU.add).then_inc(half_added, 1)

                    add_half(0, 0)

                    def group_of(s, k, first, last):
                        if not (last and k == 1):
                            add_half(s + k, 1 - k)
                        if not (first and k == 0):
                            scale_shift_add(s * 2 + k - 1, 1 - k)

                    two_per_step(pool, group_of)
                    scale_shift_add(NG - 1, 1)

                @block.scalar
                def _(act):
                    def deviation(g, k):
                        act.wait_ge(reduced, g + 1)
                        act.activation(dev[k][:, :], dev[k][:, :], ACT.Sqrt, bias=eps_col[:, 0:1], scale=1.0 / F).then_inc(root, 1)

                    def store(g):
                        act.wait_ge(final, g * 3 + 3)
                        act.dma_start(out[:, bass.ds(g * GB, GB), :], group(x_nodes, g * GB)).then_inc(stored, 16)

                    def group_of(s, k, first, last):
                        g = s * 2 + k
                        if not (first and k == 0):
                            deviation(g - 1, 1 - k)
                        act.wait_ge(step, g * CS + CS)
                        act.activation(square[k][:, :, :], x3[k][:, :, :], ACT.Square).then_inc(squared, 1)
                        if not first:
                            store(g - 2)

                    two_per_step(act, group_of)
                    deviation(NG - 1, 1)
                    store(NG - 2)
                    store(NG - 1)
                    act.wait_ge(stored, NG * 16)

                @block.vector
                def _(dve):
                    def reduce_squares(g, k):
                        dve.wait_ge(squared, g + 1)
                        dve.tensor_reduce(dev[k][:, :], square[k][:, :, :], AX.X, ALU.add).then_inc(reduced, 1)

                    def normalise(g, k):
                        dve.wait_ge(root, g + 1)
                        dve.reciprocal(dev[k][:, :], dev[k][:, :]).then_inc(normed, 1)
                        dve.wait_ge(normed, g * 2 + 1)
                        dve.tensor_tensor(x3[k][:, :, :], x3[k][:, :, :], each(dev[k]), ALU.mult).then_inc(normed, 1)

                    def group_of(s, k, first, last):
                        g = s * 2 + k
                        n = g * CS
                        quarters = part_sum[k][:, :, :, :].rearrange("p (q i) b f -> p q (i b f)", q=4)
                        of_edges = total[k][:, :, 0:F]
                        dve.wait_ge(loaded[k], s * (NT * 16) + NT * 16)
                        dve.tensor_tensor(quarters[:, 0, :], quarters[:, 0, :], quarters[:, 2, :],
                                          ALU.add).then_inc(step, 1)
                        dve.wait_ge(step, n + 1)
                        dve.wait_ge(half_added, g + 1)
                        dve.tensor_tensor(quarters[:, 0, :], quarters[:, 0, :], quarters[:, 1, :],
                                          ALU.add).then_inc(step, 1)
                        dve.wait_ge(step, n + 2)
                        dve.tensor_tensor(total[k][:, :, :], part_sum[k][:, 0, :, :], part_sum[k][:, 1, :, :],
                                          ALU.add).then_inc(step, 1)
                        if not (first and k == 0):
                            reduce_squares(g - 1, 1 - k)
                        dve.wait_ge(step, n + 3)
                        dve.tensor_scalar(mean[k][:, :], total[k][:, :, F], 1e-8, None, ALU.max).then_inc(step, 1)
                        dve.wait_ge(step, n + 4)
                        dve.reciprocal(mean[k][:, :], mean[k][:, :]).then_inc(step, 1)
                        dve.wait_ge(step, n + 5)
                        dve.tensor_tensor(of_edges, of_edges, each(mean[k]), ALU.mult).then_inc(step, 1)
                        dve.wait_ge(step, n + 6)
                        if not first:
                            dve.wait_ge(final, (g - 2) * 3 + 3)
                        dve.tensor_tensor(x3[k][:, :, :], group(h_nodes, g * GB), of_edges, ALU.add).then_inc(step, 1)
                        dve.wait_ge(step, n + 7)
                        dve.tensor_reduce(mean[k][:, :], x3[k][:, :, :], AX.X, ALU.add).then_inc(step, 1)
                        dve.wait_ge(step, n + 8)
                        dve.tensor_scalar(mean[k][:, :], mean[k][:, :], -1.0 / F, None, ALU.mult).then_inc(step, 1)
                        dve.wait_ge(step, n + 9)
                        dve.tensor_tensor(x3[k][:, :, :], x3[k][:, :, :], each(mean[k]), ALU.add).then_inc(step, 1)
                        if not (first and k == 0):
                            normalise(g - 1, 1 - k)

                    two_per_step(dve, group_of)
                    reduce_squares(NG - 1, 1)
                    normalise(NG - 1, 1)


def kernel(x, src, dst, edge_attr_40, edge_attr_48, edge_type_8, edge_weight, edge_weight1, node_type_119, node_vec,
           L0_gnn_eps, L1_gnn_weight1, L1_gnn_weight2, L1_gnn_bias1, L1_gnn_bias2, L2_gnn_weight, L2_gnn_bias,
           L3_gnn_W1, L3_gnn_b1, L3_gnn_W2, L3_gnn_b2, L3_gnn_emb, L3_gnn_adaptW, L3_gnn_gamma, L3_gnn_beta):
    import numpy as _np
    import concourse.bacc as _bacc
    from concourse import mybir as _mybir
    from concourse.bass_utils import run_bass_kernel_spmd as _run

    P = 128
    N, F = x.shape
    E = src.shape[0]
    NB = -(-N // (14 * P)) * 14
    NCH = -(-E // (8 * 512)) * 8
    more_n, more_e = NB * P - N, NCH * 512 - E

    def nodes(a, fill=0):
        a = _np.asarray(a)
        return _np.pad(a, [(0, more_n)] + [(0, 0)] * (a.ndim - 1), constant_values=fill)

    def edges(a, fill=0):
        a = _np.asarray(a)
        return _np.pad(a, [(0, more_e)] + [(0, 0)] * (a.ndim - 1), constant_values=fill)

    def cols(a, fill=0):
        return edges(a, fill).reshape(NCH, P, 4).transpose(1, 0, 2).reshape(P, NCH * 4)

    src_e, dst_e = edges(src, N), edges(dst, N)
    R = edge_attr_40.shape[1]
    arrays = {
        "x": nodes(x).reshape(P, NB, F),
        "src": cols(src, N),
        "dst": cols(dst, N),
        "dst_rows": dst_e.reshape(NCH // 4, 4, 512),
        "src_lines": src_e.reshape(NCH, P, 4).transpose(0, 2, 1).reshape(NCH, 512),
        "dst_lines": dst_e.reshape(NCH, P, 4).transpose(0, 2, 1).reshape(NCH, 512),
        "attr48": edges(edge_attr_48).reshape(NCH, P, 4 * F),
        "ea_t": edges(edge_attr_40).reshape(NCH, P, 2, 2, R).transpose(0, 2, 4, 3, 1).reshape(NCH, 2 * R, 256),
        "edge_type": cols(edge_type_8),
        "dist": cols(edge_weight),
        "norm": cols(_np.asarray(edge_weight1).reshape(E)),
        "node_type": nodes(node_type_119).reshape(P, NB),
        "node_vec": nodes(node_vec).reshape(P, NB),
        "eps": _np.asarray(L0_gnn_eps).reshape(1, 1),
        "w1": _np.asarray(L1_gnn_weight1).transpose(1, 0, 2).reshape(F, -1),
        "w2": _np.asarray(L1_gnn_weight2).transpose(1, 0, 2).reshape(F, -1),
        "bias1": _np.asarray(L1_gnn_bias1),
        "bias2": _np.asarray(L1_gnn_bias2).reshape(1, F),
        "cheb": _np.asarray(L2_gnn_weight).transpose(1, 0, 2).reshape(F, -1),
        "cheb_bias": _np.asarray(L2_gnn_bias).reshape(1, F),
        "fw1_t": _np.asarray(L3_gnn_W1).T,
        "fb1": _np.asarray(L3_gnn_b1).reshape(F, 1),
        "fw2_t": _np.asarray(L3_gnn_W2).T,
        "fb2": _np.asarray(L3_gnn_b2).reshape(1, F),
        "emb_t": _np.asarray(L3_gnn_emb).T,
        "adapt": _np.asarray(L3_gnn_adaptW),
        "type_line": nodes(node_type_119).reshape(1, -1),
        "gamma": _np.asarray(L3_gnn_gamma).reshape(1, F),
        "beta": _np.asarray(L3_gnn_beta).reshape(1, F),
    }
    nc = _bacc.Bacc("TRN2", target_bir_lowering=False, num_devices=1)
    ins, given = {}, {}
    for name, a in arrays.items():
        a = _np.ascontiguousarray(a)
        given[f"in_{name}"] = a
        ins[name] = nc.dram_tensor(f"in_{name}", a.shape, _mybir.dt.from_np(a.dtype), kind="ExternalInput").ap()
    out = nc.dram_tensor("out_0", [P, NB, F], _mybir.dt.float32, kind="ExternalOutput").ap()
    gnn_program(nc, ins, out)
    r = _run(nc, [given], core_ids=[0])
    return r.results[0]["out_0"].reshape(NB * P, F)[:N]
```
